# Optimizing a Trainium2 kernel written in Bass

```python
import numpy as np
import jax
import jax.numpy as jnp

def _softmax(x, axis=-1):
    return jax.nn.softmax(x, axis=axis)

def _gelu(x):
    return jax.nn.gelu(x, approximate=True)

def _silu(x):
    return jax.nn.silu(x)

def _sigmoid(x):
    return jax.nn.sigmoid(x)

def _layernorm(x, axis=-1, eps=1e-05):
    m = jnp.mean(x, axis=axis, keepdims=True)
    v = jnp.var(x, axis=axis, keepdims=True)
    return (x - m) / jnp.sqrt(v + eps)

def _scatter_add(tgt, idx, src, axis=0):
    return tgt.at[idx].add(src)

def _segment_sum(src, seg, n):
    return jax.ops.segment_sum(src, seg, n)
kernel_name = 'mk_seq_preln_d2_jaxref_r8_f15361'

def setup_inputs(seed: int=0):
    np.random.seed(seed)
    _w = jnp.asarray

    def _L0_attn_setup():
        import jax, jax.numpy as jnp
        import numpy as np
        B, S, H = (2, 256, 128)
        NQ, NKV, HD, RANK = (16, 4, 64, 8)
        THETA = 10000.0
        LORA_SCALE = 16 / RANK
        ATTN_SCALE = 1.0 / np.sqrt(HD)

        def _lora_proj(x, W, A, Bm):
            return x @ W.T + x @ A.T @ Bm.T * LORA_SCALE

        def _rope(x, cos_h, sin_h):
            x1, x2 = (x[..., ::2], x[..., 1::2])
            return jnp.concatenate([x1 * cos_h - x2 * sin_h, x1 * sin_h + x2 * cos_h], axis=-1)

        def _forward(x, Wq, Wk, Wv, Wo, qA, qB, kA, kB, vA, vB, oA, oB):
            b, s, _ = x.shape
            q = _lora_proj(x, Wq, qA, qB).reshape(b, s, NQ, HD).transpose(0, 2, 1, 3)
            k = _lora_proj(x, Wk, kA, kB).reshape(b, s, NKV, HD).transpose(0, 2, 1, 3)
            v = _lora_proj(x, Wv, vA, vB).reshape(b, s, NKV, HD).transpose(0, 2, 1, 3)
            inv_freq = 1.0 / THETA ** (jnp.arange(0, HD, 2, dtype=jnp.float32) / HD)
            freqs = jnp.arange(s, dtype=jnp.float32)[:, None] * inv_freq[None, :]
            cos_h = jnp.cos(freqs)[None, None]
            sin_h = jnp.sin(freqs)[None, None]
            q = _rope(q, cos_h, sin_h)
            k = _rope(k, cos_h, sin_h)
            rep = NQ // NKV
            k = jnp.repeat(k, rep, axis=1)
            v = jnp.repeat(v, rep, axis=1)
            attn = jax.nn.softmax(jnp.einsum('bhqd,bhkd->bhqk', q, k) * ATTN_SCALE, axis=-1)
            out = jnp.einsum('bhqk,bhkd->bhqd', attn, v)
            out = out.transpose(0, 2, 1, 3).reshape(b, s, NQ * HD)
            return _lora_proj(out, Wo, oA, oB)
        key = jax.random.key(seed)
        ks = jax.random.split(key, 14)
        n = lambda k, shape, s: jax.random.normal(k, shape, jnp.float32) * s
        return {'x': n(ks[0], (B, S, H), 1.0), 'Wq': n(ks[1], (NQ * HD, H), 0.02), 'Wk': n(ks[2], (NKV * HD, H), 0.02), 'Wv': n(ks[3], (NKV * HD, H), 0.02), 'Wo': n(ks[4], (H, NQ * HD), 0.02), 'qA': n(ks[5], (RANK, H), 0.05), 'qB': n(ks[6], (NQ * HD, RANK), 0.05), 'kA': n(ks[7], (RANK, H), 0.05), 'kB': n(ks[8], (NKV * HD, RANK), 0.05), 'vA': n(ks[9], (RANK, H), 0.05), 'vB': n(ks[10], (NKV * HD, RANK), 0.05), 'oA': n(ks[11], (RANK, NQ * HD), 0.05), 'oB': n(ks[12], (H, RANK), 0.05)}
    _L0_attn_in = _L0_attn_setup()

    def _L0_ffn_setup():
        import jax, jax.numpy as jnp
        import numpy as np
        NUM_EXPERTS = 8
        NUM_LANGS = 4
        TOP_K = 2
        D_MODEL = 128
        EXPERT_SIZE = 512
        B, S = (2, 256)
        key = jax.random.key(seed)
        ks = jax.random.split(key, 6)

        def xavier(k, shape, fan_in, fan_out):
            a = float(np.sqrt(6.0 / (fan_in + fan_out)))
            return jax.random.uniform(k, shape, jnp.float32, -a, a)
        return {'x': jax.random.normal(ks[0], (B, S, D_MODEL), jnp.float32), 'router_w': xavier(ks[1], (NUM_EXPERTS, D_MODEL), D_MODEL, NUM_EXPERTS), 'router_b': jnp.zeros((NUM_EXPERTS,), jnp.float32), 'lang_w': xavier(ks[2], (NUM_LANGS, D_MODEL), D_MODEL, NUM_LANGS), 'lang_b': jnp.zeros((NUM_LANGS,), jnp.float32), 'w1': xavier(ks[3], (NUM_EXPERTS, D_MODEL, EXPERT_SIZE), D_MODEL, EXPERT_SIZE), 'b1': jnp.zeros((NUM_EXPERTS, EXPERT_SIZE), jnp.float32), 'w2': xavier(ks[4], (NUM_EXPERTS, EXPERT_SIZE, D_MODEL), EXPERT_SIZE, D_MODEL), 'b2': jnp.zeros((NUM_EXPERTS, D_MODEL), jnp.float32)}
    _L0_ffn_in = _L0_ffn_setup()

    def _L1_attn_setup():
        import jax, jax.numpy as jnp
        import numpy as np
        from math import sqrt
        EMBED = 128
        HEADS = 16
        key = jax.random.key(seed)
        k1, k2, k3, k4, k5 = jax.random.split(key, 5)
        x = jax.random.normal(k1, (2, 256, EMBED), dtype=jnp.float32)
        s = 1.0 / sqrt(EMBED)
        W_qkv = jax.random.normal(k2, (EMBED, 3 * EMBED), dtype=jnp.float32) * s
        b_qkv = jax.random.normal(k3, (3 * EMBED,), dtype=jnp.float32) * 0.01
        W_out = jax.random.normal(k4, (EMBED, EMBED), dtype=jnp.float32) * s
        b_out = jax.random.normal(k5, (EMBED,), dtype=jnp.float32) * 0.01
        return {'x': x, 'W_qkv': W_qkv, 'b_qkv': b_qkv, 'W_out': W_out, 'b_out': b_out}
    _L1_attn_in = _L1_attn_setup()

    def _L1_ffn_setup():
        import jax, jax.numpy as jnp
        import numpy as np
        DIM = 128
        INTER = 64
        E = 32
        TOPK = 4
        GROUPS = 8
        TOPK_GROUPS = 4
        SHARED_INTER = 2 * INTER
        ROUTE_SCALE = 1.0
        B, S = (8, 512)

        def _gate(xf, gw, gb):
            T = xf.shape[0]
            scores = jax.nn.softmax((xf @ gw + gb).astype(jnp.float32), axis=-1)
            original_scores = scores
            scores_g = scores.reshape(T, GROUPS, E // GROUPS)
            group_scores = jnp.sum(jax.lax.top_k(scores_g, 2)[0], axis=-1)
            gidx = jax.lax.top_k(group_scores, TOPK_GROUPS)[1]
            keep = jnp.zeros((T, GROUPS), bool).at[jnp.arange(T)[:, None], gidx].set(True)
            masked = jnp.where(keep[:, :, None], scores_g, -jnp.inf).reshape(T, E)
            indices = jax.lax.top_k(masked, TOPK)[1]
            weights = jnp.take_along_axis(original_scores, indices, axis=1) * ROUTE_SCALE
            return (weights.astype(xf.dtype), indices)
        key = jax.random.key(seed)
        ks = jax.random.split(key, 16)

        def xav(k, shape):
            fan_in, fan_out = (shape[-2], shape[-1])
            lim = np.sqrt(6.0 / (fan_in + fan_out))
            return jax.random.uniform(k, shape, jnp.float32, -lim, lim)
        return {'x': jax.random.normal(ks[0], (B, S, DIM), jnp.float32), 'gw': xav(ks[1], (DIM, E)), 'gb': jnp.zeros((E,), jnp.float32), 'w1': xav(ks[2], (E, DIM, INTER)), 'b1': jnp.zeros((E, INTER), jnp.float32), 'w3': xav(ks[3], (E, DIM, INTER)), 'b3': jnp.zeros((E, INTER), jnp.float32), 'w2': xav(ks[4], (E, INTER, DIM)), 'b2': jnp.zeros((E, DIM), jnp.float32), 'sw1': xav(ks[5], (DIM, SHARED_INTER)), 'sb1': jnp.zeros((SHARED_INTER,), jnp.float32), 'sw3': xav(ks[6], (DIM, SHARED_INTER)), 'sb3': jnp.zeros((SHARED_INTER,), jnp.float32), 'sw2': xav(ks[7], (SHARED_INTER, DIM)), 'sb2': jnp.zeros((DIM,), jnp.float32)}
    _L1_ffn_in = _L1_ffn_setup()
    _d = {'L0_attn_x': _L0_attn_in['x'], 'L0_attn_Wq': _L0_attn_in['Wq'], 'L0_attn_Wk': _L0_attn_in['Wk'], 'L0_attn_Wv': _L0_attn_in['Wv'], 'L0_attn_Wo': _L0_attn_in['Wo'], 'L0_attn_qA': _L0_attn_in['qA'], 'L0_attn_qB': _L0_attn_in['qB'], 'L0_attn_kA': _L0_attn_in['kA'], 'L0_attn_kB': _L0_attn_in['kB'], 'L0_attn_vA': _L0_attn_in['vA'], 'L0_attn_vB': _L0_attn_in['vB'], 'L0_attn_oA': _L0_attn_in['oA'], 'L0_attn_oB': _L0_attn_in['oB'], 'L0_ffn_router_w': _L0_ffn_in['router_w'], 'L0_ffn_router_b': _L0_ffn_in['router_b'], 'L0_ffn_lang_w': _L0_ffn_in['lang_w'], 'L0_ffn_lang_b': _L0_ffn_in['lang_b'], 'L0_ffn_w1': _L0_ffn_in['w1'], 'L0_ffn_b1': _L0_ffn_in['b1'], 'L0_ffn_w2': _L0_ffn_in['w2'], 'L0_ffn_b2': _L0_ffn_in['b2'], 'L1_attn_W_qkv': _L1_attn_in['W_qkv'], 'L1_attn_b_qkv': _L1_attn_in['b_qkv'], 'L1_attn_W_out': _L1_attn_in['W_out'], 'L1_attn_b_out': _L1_attn_in['b_out'], 'L1_ffn_gw': _L1_ffn_in['gw'], 'L1_ffn_gb': _L1_ffn_in['gb'], 'L1_ffn_w1': _L1_ffn_in['w1'], 'L1_ffn_b1': _L1_ffn_in['b1'], 'L1_ffn_w3': _L1_ffn_in['w3'], 'L1_ffn_b3': _L1_ffn_in['b3'], 'L1_ffn_w2': _L1_ffn_in['w2'], 'L1_ffn_b2': _L1_ffn_in['b2'], 'L1_ffn_sw1': _L1_ffn_in['sw1'], 'L1_ffn_sb1': _L1_ffn_in['sb1'], 'L1_ffn_sw3': _L1_ffn_in['sw3'], 'L1_ffn_sb3': _L1_ffn_in['sb3'], 'L1_ffn_sw2': _L1_ffn_in['sw2'], 'L1_ffn_sb2': _L1_ffn_in['sb2']}
    _x0 = _d['L0_attn_x']
    _d['L0_attn_x'] = jax.random.normal(jax.random.fold_in(jax.random.key(seed), 1), (16, 256, 128), dtype=_x0.dtype)
    del _x0
    return _d

def reference(L0_attn_x, L0_attn_Wq, L0_attn_Wk, L0_attn_Wv, L0_attn_Wo, L0_attn_qA, L0_attn_qB, L0_attn_kA, L0_attn_kB, L0_attn_vA, L0_attn_vB, L0_attn_oA, L0_attn_oB, L0_ffn_router_w, L0_ffn_router_b, L0_ffn_lang_w, L0_ffn_lang_b, L0_ffn_w1, L0_ffn_b1, L0_ffn_w2, L0_ffn_b2, L1_attn_W_qkv, L1_attn_b_qkv, L1_attn_W_out, L1_attn_b_out, L1_ffn_gw, L1_ffn_gb, L1_ffn_w1, L1_ffn_b1, L1_ffn_w3, L1_ffn_b3, L1_ffn_w2, L1_ffn_b2, L1_ffn_sw1, L1_ffn_sb1, L1_ffn_sw3, L1_ffn_sb3, L1_ffn_sw2, L1_ffn_sb2):

    def _L0_attn_ref(x, Wq, Wk, Wv, Wo, qA, qB, kA, kB, vA, vB, oA, oB):
        import jax, jax.numpy as jnp
        import numpy as np
        B, S, H = (2, 256, 128)
        NQ, NKV, HD, RANK = (16, 4, 64, 8)
        THETA = 10000.0
        LORA_SCALE = 16 / RANK
        ATTN_SCALE = 1.0 / np.sqrt(HD)

        def _lora_proj(x, W, A, Bm):
            return x @ W.T + x @ A.T @ Bm.T * LORA_SCALE

        def _rope(x, cos_h, sin_h):
            x1, x2 = (x[..., ::2], x[..., 1::2])
            return jnp.concatenate([x1 * cos_h - x2 * sin_h, x1 * sin_h + x2 * cos_h], axis=-1)

        def _forward(x, Wq, Wk, Wv, Wo, qA, qB, kA, kB, vA, vB, oA, oB):
            b, s, _ = x.shape
            q = _lora_proj(x, Wq, qA, qB).reshape(b, s, NQ, HD).transpose(0, 2, 1, 3)
            k = _lora_proj(x, Wk, kA, kB).reshape(b, s, NKV, HD).transpose(0, 2, 1, 3)
            v = _lora_proj(x, Wv, vA, vB).reshape(b, s, NKV, HD).transpose(0, 2, 1, 3)
            inv_freq = 1.0 / THETA ** (jnp.arange(0, HD, 2, dtype=jnp.float32) / HD)
            freqs = jnp.arange(s, dtype=jnp.float32)[:, None] * inv_freq[None, :]
            cos_h = jnp.cos(freqs)[None, None]
            sin_h = jnp.sin(freqs)[None, None]
            q = _rope(q, cos_h, sin_h)
            k = _rope(k, cos_h, sin_h)
            rep = NQ // NKV
            k = jnp.repeat(k, rep, axis=1)
            v = jnp.repeat(v, rep, axis=1)
            attn = jax.nn.softmax(jnp.einsum('bhqd,bhkd->bhqk', q, k) * ATTN_SCALE, axis=-1)
            out = jnp.einsum('bhqk,bhkd->bhqd', attn, v)
            out = out.transpose(0, 2, 1, 3).reshape(b, s, NQ * HD)
            return _lora_proj(out, Wo, oA, oB)
        return _forward(x, Wq, Wk, Wv, Wo, qA, qB, kA, kB, vA, vB, oA, oB)

    def _L0_ffn_ref(x, router_w, router_b, lang_w, lang_b, w1, b1, w2, b2):
        import jax, jax.numpy as jnp
        import numpy as np
        NUM_EXPERTS = 8
        NUM_LANGS = 4
        TOP_K = 2
        D_MODEL = 128
        EXPERT_SIZE = 512
        B, S = (2, 256)
        lang_logits = x @ lang_w.T + lang_b
        lang_probs = jax.nn.softmax(lang_logits, axis=-1)
        lp_pad = jnp.pad(lang_probs, ((0, 0), (0, 0), (0, 1)))
        idx = jnp.arange(NUM_EXPERTS) % NUM_LANGS
        expert_weights = lp_pad[..., idx] + lp_pad[..., idx + 1]
        router_logits = x @ router_w.T + router_b + 0.1 * expert_weights
        router_probs = jax.nn.softmax(router_logits, axis=-1)
        top_p, top_i = jax.lax.top_k(router_probs, TOP_K)
        top_p = top_p / top_p.sum(axis=-1, keepdims=True)
        h = jax.nn.gelu(jnp.einsum('bsd,edh->bseh', x, w1) + b1, approximate=False)
        expert_out = jnp.einsum('bseh,ehd->bsed', h, w2) + b2
        sel = jnp.take_along_axis(expert_out, top_i[..., None], axis=2)
        return (top_p[..., None] * sel).sum(axis=2)

    def _L1_attn_ref(x, W_qkv, b_qkv, W_out, b_out):
        import jax, jax.numpy as jnp
        import numpy as np
        from math import sqrt
        EMBED = 128
        HEADS = 16
        B, N, E = x.shape
        H = HEADS
        d = E // H
        qkv = x @ W_qkv + b_qkv
        q, k, v = jnp.split(qkv, 3, axis=2)
        q = q.reshape(B, N, H, d)
        k = k.reshape(B, N, H, d)
        v = v.reshape(B, N, H, d)
        energy = jnp.einsum('bqhe,bkhe->bqhk', q, k)
        attn = jax.nn.softmax(energy, axis=-1) / sqrt(E)
        out = jnp.einsum('bihv,bvhd->bihd', attn, v)
        out = out.reshape(B, N, E)
        return out @ W_out + b_out

    def _L1_ffn_ref(x, gw, gb, w1, b1, w3, b3, w2, b2, sw1, sb1, sw3, sb3, sw2, sb2):
        import jax, jax.numpy as jnp
        import numpy as np
        DIM = 128
        INTER = 64
        E = 32
        TOPK = 4
        GROUPS = 8
        TOPK_GROUPS = 4
        SHARED_INTER = 2 * INTER
        ROUTE_SCALE = 1.0
        B, S = (8, 512)

        def _gate(xf, gw, gb):
            T = xf.shape[0]
            scores = jax.nn.softmax((xf @ gw + gb).astype(jnp.float32), axis=-1)
            original_scores = scores
            scores_g = scores.reshape(T, GROUPS, E // GROUPS)
            group_scores = jnp.sum(jax.lax.top_k(scores_g, 2)[0], axis=-1)
            gidx = jax.lax.top_k(group_scores, TOPK_GROUPS)[1]
            keep = jnp.zeros((T, GROUPS), bool).at[jnp.arange(T)[:, None], gidx].set(True)
            masked = jnp.where(keep[:, :, None], scores_g, -jnp.inf).reshape(T, E)
            indices = jax.lax.top_k(masked, TOPK)[1]
            weights = jnp.take_along_axis(original_scores, indices, axis=1) * ROUTE_SCALE
            return (weights.astype(xf.dtype), indices)
        shape = x.shape
        xf = x.reshape(-1, DIM)
        T = xf.shape[0]
        weights, indices = _gate(xf, gw, gb)
        cw = jnp.zeros((T, E), xf.dtype).at[jnp.arange(T)[:, None], indices].add(weights)

        def body(y, p):
            w1e, b1e, w3e, b3e, w2e, b2e, we = p
            h = jax.nn.silu(xf @ w1e + b1e) * (xf @ w3e + b3e)
            return (y + we[:, None] * (h @ w2e + b2e), None)
        y0 = jnp.zeros_like(xf)
        y, _ = jax.lax.scan(body, y0, (w1, b1, w3, b3, w2, b2, cw.T))
        z = jax.nn.silu(xf @ sw1 + sb1) * (xf @ sw3 + sb3) @ sw2 + sb2
        return (y + z).reshape(shape)
    x = L0_attn_x
    x = x + _L0_attn_ref(_layernorm(x, axis=-1), L0_attn_Wq, L0_attn_Wk, L0_attn_Wv, L0_attn_Wo, L0_attn_qA, L0_attn_qB, L0_attn_kA, L0_attn_kB, L0_attn_vA, L0_attn_vB, L0_attn_oA, L0_attn_oB)
    x = x + _L0_ffn_ref(_layernorm(x, axis=-1), L0_ffn_router_w, L0_ffn_router_b, L0_ffn_lang_w, L0_ffn_lang_b, L0_ffn_w1, L0_ffn_b1, L0_ffn_w2, L0_ffn_b2)
    x = x + _L1_attn_ref(_layernorm(x, axis=-1), L1_attn_W_qkv, L1_attn_b_qkv, L1_attn_W_out, L1_attn_b_out)
    x = x + _L1_ffn_ref(_layernorm(x, axis=-1), L1_ffn_gw, L1_ffn_gb, L1_ffn_w1, L1_ffn_b1, L1_ffn_w3, L1_ffn_b3, L1_ffn_w2, L1_ffn_b2, L1_ffn_sw1, L1_ffn_sb1, L1_ffn_sw3, L1_ffn_sb3, L1_ffn_sw2, L1_ffn_sb2)
    return x

_drawn_inputs = setup_inputs


def setup_inputs(seed=0):
    import zlib

    import numpy as np

    out = dict(_drawn_inputs(seed))
    spreads = {'L0_ffn_router_b': (0.0, 0.1),
     'L0_ffn_lang_b': (0.0, 2.0),
     'L0_ffn_b1': (0.0, 0.1),
     'L0_ffn_b2': (0.0, 0.1),
     'L1_ffn_gb': (0.0, 0.278),
     'L1_ffn_b1': (0.0, 0.543),
     'L1_ffn_b3': (0.0, 0.584),
     'L1_ffn_b2': (0.0, 0.332),
     'L1_ffn_sb1': (0.0, 0.1),
     'L1_ffn_sb3': (0.0, 0.1),
     'L1_ffn_sb2': (0.0, 0.1)}
    factors = {'L0_attn_Wq': 6.396,
     'L0_attn_Wk': 6.642,
     'L0_attn_qA': 6.319,
     'L0_attn_qB': 7.281,
     'L0_attn_kA': 8.0,
     'L0_attn_kB': 6.633,
     'L1_attn_b_qkv': 34.687,
     'L1_attn_b_out': 4.302}
    for name, (base, spread) in spreads.items():
        noise = np.random.default_rng([zlib.crc32(name.encode()), seed]).standard_normal(out[name].shape)
        drawn = base * np.exp(spread * noise) if base else spread * noise
        out[name] = jnp.asarray(drawn.astype(out[name].dtype))
    for name, factor in factors.items():
        out[name] = (out[name] * factor).astype(out[name].dtype)
    return out
```

```python
from contextlib import ExitStack

import numpy as np

import concourse.bass as bass
from concourse import mybir

F32 = mybir.dt.float32
F32R = mybir.dt.float32r
U32 = mybir.dt.uint32
I32 = mybir.dt.int32
ACT = mybir.ActivationFunctionType
ALU = mybir.AluOpType
AX_X = mybir.AxisListType.X

P = 128
NB, S, D = 16, 256, 128
T = S // P
NQ, NKV, HD = 16, 4, 64
HALF = HD // 2
RANK = 8
LORA_SCALE = 16 / RANK
E0, H0, NLANG = 8, 512, 4
C0 = E0 * H0 // P
NH1, HD1, PAD1 = 16, 8, 32
G1 = NH1 * PAD1 // P
E1, H1 = 32, 64
C1 = E1 * H1 // P + 1
GROUPS, TOPG, TOPK1 = 8, 4, 4
NQKV0 = (NQ + 2 * NKV) * HD
LN_EPS = 1e-5
THETA = 10000.0

B_ROUTE0, B_GATE1, B_QKV1, B_OUT1 = 0, 12, 44, 428
B_ALL = B_OUT1 + D


class Chain:

    def __init__(self, eng, sem):
        self.eng, self.sem, self.n = eng, sem, 0

    def link(self, ins):
        self.n += 1
        ins.then_inc(self.sem, 1)
        self.eng.wait_ge(self.sem, self.n)


def transformer_layers(nc, a, out):
    with ExitStack() as ctx:
        def sb(name, shape, dt=F32):
            return ctx.enter_context(nc.sbuf_tensor(name, shape, dt))

        wqkv0_h, wqkv0_l = sb("wqkv0_h", [P, NQKV0], F32R), sb("wqkv0_l", [P, NQKV0], F32R)
        wo0 = sb("wo0", [P, NQ // 2, D])
        w1_0h, w1_0l = sb("w1_0h", [P, C0 * P], F32R), sb("w1_0l", [P, C0 * P], F32R)
        w2_0 = sb("w2_0", [P, C0, D])
        b1_0 = sb("b1_0", [P, C0])
        wroute0 = sb("wroute0", [P, NLANG + E0])
        wqkv1_h, wqkv1_l = sb("wqkv1_h", [P, 3 * D], F32R), sb("wqkv1_l", [P, 3 * D], F32R)
        wo1 = sb("wo1", [P, G1, D])
        w13_h, w13_l = sb("w13_h", [P, 2, C1 * P], F32R), sb("w13_l", [P, 2, C1 * P], F32R)
        w2_1 = sb("w2_1", [P, C1, D])
        b13 = sb("b13", [P, 2, C1])
        wgate1 = sb("wgate1", [P, E1])
        b2_0, b2_1 = sb("b2_0", [P, D]), sb("b2_1", [P, D])
        spread = sb("spread", [P, (C1 - 1) * P], F32R)
        bias = sb("bias", [P, B_ALL])
        rope = sb("rope", [P, T, 4, HALF])
        ident = sb("ident", [P, P])
        iota = sb("iota", [P, E1])

        x_in = sb("x_in", [P, T, D])
        xres = sb("xres", [P, T, D])
        y_out = sb("y_out", [P, T, D])
        stats, mv, rstd = sb("stats", [P, T, 6]), sb("mv", [P, T, 2]), sb("rstd", [P, T])
        var, newton = sb("var", [P, T]), sb("newton", [P, T])
        xn = sb("xn", [P, T, D])
        xT = sb("xT", [P, S])
        xT_h, xT_l = sb("xT_h", [P, S], F32R), sb("xT_l", [P, S], F32R)
        q_stk = sb("q_stk", [P, T, NQ, 2 * HD])
        k_stk = sb("k_stk", [P, T, NKV, 2, 2 * HD])
        v0 = sb("v0", [P, T, NKV, HD])
        qT = sb("qT", [P, NQ, S], F32R)
        kT = sb("kT", [P, NKV, 2, S], F32R)
        nmax = sb("nmax", [P, 4, T])
        psums = sb("psums", [P, 4, T])
        rsums = sb("rsums", [P, 4, T])
        prob = sb("prob", [P, 3, T, S])
        probT = sb("probT", [P, 3, 2, S])
        hT = sb("hT", [P, 8, S])
        aT = hT
        gate_z = sb("gate_z", [P, T, E1])
        gate_s = sb("gate_s", [P, 8, T])
        top8 = sb("top8", [P, 2, T, 8])
        topi = sb("topi", [P, 2, T, 8], U32)
        topf = sb("topf", [P, 2, T, 8])
        cw = sb("cw", [P, T, P])
        cwT = sb("cwT", [P, S], F32R)
        ra, rb, ro = (prob[:, n, :, :].rearrange("p t s -> p (t s)") for n in range(3))
        k_flat = k_stk[:, :, :, :, :].rearrange("p t h a c -> p (t h a c)")
        q_flat = q_stk[:, :, :, :].rearrange("p t h c -> p (t h c)")
        q_stk1 = k_flat[:, 0:T * NH1 * PAD1].rearrange("p (t h c) -> p t h c", t=T, h=NH1)
        k_stk1 = k_flat[:, T * NH1 * PAD1:].rearrange("p (t h c) -> p t h c", t=T, h=NH1)
        qkv1 = q_flat[:, 0:768].rearrange("p (t n) -> p t n", t=T)
        gate_t = q_flat[:, 768:1536].rearrange("p (k t e) -> p k t e", k=12, t=T)
        v1 = q_flat[:, 3072:4096].rearrange("p (t h c) -> p t h c", t=T, h=NH1)
        silu = q_flat[:, 1536:2048].rearrange("p (k s) -> p k s", k=2)
        gated = q_flat[:, 2048:3072].rearrange("p (n j s) -> p n j s", n=2, j=2)

        lora_a = probT[0:RANK].rearrange("p c k s -> p (c k s)")[:, 0:3 * D + NQ * HD]
        lora_b = k_flat[0:RANK, 0:NQKV0 + D]
        stage = q_stk[:, :, :, :].rearrange("p t h d -> p (t h d)")
        stage3 = prob[:, :, :, :].rearrange("p c t s -> p (c t s)")

        bank = [ctx.enter_context(nc.psum_tensor(f"bank{i}", [P, 512], F32)) for i in range(8)]

        w_loaded = ctx.enter_context(nc.semaphore("w_loaded"))
        wqkv0_loaded = ctx.enter_context(nc.semaphore("wqkv0_loaded"))
        stage_loaded = ctx.enter_context(nc.semaphore("stage_loaded"))
        stage_split = ctx.enter_context(nc.semaphore("stage_split"))
        zeroed = ctx.enter_context(nc.semaphore("zeroed"))
        lora_ready = ctx.enter_context(nc.semaphore("lora_ready"))
        lora_used = ctx.enter_context(nc.semaphore("lora_used"))
        setup_dve = ctx.enter_context(nc.semaphore("setup_dve"))
        y_stored = ctx.enter_context(nc.semaphore("y_stored"))

        sems = []

        def signal(name):
            sems.append(ctx.enter_context(nc.semaphore(name)))
            return sems[-1]

        x_loaded = signal("x_loaded")
        x_taken = signal("x_taken")
        y_ready = signal("y_ready")
        dve_own = signal("dve_own")
        act_own = signal("act_own")
        normed = signal("normed")
        xT_psum = signal("xT_psum")
        xT_ready = signal("xT_ready")
        qkv_psum = signal("qkv_psum")
        stacked = signal("stacked")
        turned = signal("turned")
        turned_out = signal("turned_out")
        scores_psum = signal("scores_psum")
        max_ready = signal("max_ready")
        exp_ready = signal("exp_ready")
        rsum_ready = signal("rsum_ready")
        prob_ready = signal("prob_ready")
        probT_psum = signal("probT_psum")
        probT_ready = signal("probT_ready")
        heads_done = signal("heads_done")
        aT_ready = signal("aT_ready")
        attn_psum = signal("attn_psum")
        logits_psum = signal("logits_psum")
        route_in = signal("route_in")
        route_exp = signal("route_exp")
        cw_ready = signal("cw_ready")
        cwT_psum = signal("cwT_psum")
        cwT_ready = signal("cwT_ready")
        hid0_psum = signal("hid0_psum")
        hid0_ready = signal("hid0_ready")
        exp_out = signal("exp_out")
        exp_added = signal("exp_added")
        up1_psum = signal("up1_psum")
        spread_psum = signal("spread_psum")
        silu_ready = signal("silu_ready")
        gated_ready = signal("gated_ready")
        hid1_ready = signal("hid1_ready")
        down1_done = signal("down1_done")

        loads = [(lora_a, a["lora_a"]), (lora_b, a["lora_b"])] + [(dst[:], a[name]) for dst, name in (
            (wroute0, "wroute0"), (wgate1, "wgate1"), (b1_0, "b1_0"), (b13, "b13"), (w2_0, "w2_0"),
            (w2_1, "w2_1"), (wo1, "wo1"), (rope, "rope"), (ident, "ident"), (iota, "iota"))]
        n_loads = len(loads) + 5
        splits = [(w1_0h[:, :], w1_0l[:, :], a["w1_0"], stage),
                  (w13_h[:, 0, :], w13_l[:, 0, :], a["w13"][0], stage),
                  (spread[:, :], None, a["spread"], stage),
                  (w13_h[:, 1, :], w13_l[:, 1, :], a["w13"][1], stage),
                  (wqkv1_h[:, :], wqkv1_l[:, :], a["wqkv1"], stage)]

        with nc.Block(no_gpsimd_drain=True) as block:
            @block.sync
            def _(sp):
                sp.dma_start(stage3[:, 0:NQKV0], a["wqkv0"]).then_inc(wqkv0_loaded, 16)
                for n, (_, _, src, st) in enumerate(splits):
                    if n >= 1:
                        sp.wait_ge(stage_split, n)
                    sp.dma_start(st[:, 0:src.shape[1]], src).then_inc(stage_loaded, 16)

            @block.scalar
            def _(act):
                for dst, src in loads:
                    act.dma_start(dst, src).then_inc(w_loaded, 16)
                act.dma_start(x_in[:, :, :], a["x"][0]).then_inc(w_loaded, 16)
                act.dma_start(bias[:, :], a["bias"].partition_broadcast(P)).then_inc(w_loaded, 16)
                act.dma_start(wo0[:, :, :], a["wo0"]).then_inc(w_loaded, 16)
                act.wait_ge(zeroed, 3)
                act.dma_start(b2_0[0:E0, :], a["b2_0"]).then_inc(w_loaded, 16)
                act.dma_start(b2_1[0:2 * E1 + 1, :], a["b2_1"]).then_inc(w_loaded, 16)
                act.wait_ge(w_loaded, 16 * n_loads)

            @block.gpsimd
            def _(pool):
                pool.memset(b2_0[:, :], 0.0).then_inc(zeroed, 1)
                pool.memset(b2_1[:, :], 0.0).then_inc(zeroed, 1)
                pool.memset(cw[:, :, :], 0.0).then_inc(zeroed, 1)

            @block.tensor
            def _(pe):
                pe.wait_ge(w_loaded, 16 * n_loads)
                for j in range(3):
                    c = 512 * j
                    if j < 2:
                        mm = pe.matmul(bank[j][:, :], lora_a[:, 0:D], lora_b[:, c:c + 512], start=True, stop=True)
                    else:
                        pe.matmul(bank[2][:, 0:256], lora_a[:, D:2 * D], lora_b[:, c:c + 256], start=True, stop=True)
                        mm = pe.matmul(bank[2][:, 256:512], lora_a[:, 2 * D:3 * D], lora_b[:, c + 256:c + 512],
                                       start=True, stop=True)
                    mm.then_inc(lora_ready, 1)
                for j in range(NQ // 2):
                    c = 3 * D + j * P
                    mm = pe.matmul(bank[3 + j // 4][:, (j % 4) * D:(j % 4 + 1) * D], lora_a[:, c:c + P],
                                   lora_b[:, NQKV0:NQKV0 + D], start=True, stop=True)
                mm.then_inc(lora_ready, 1)

            @block.vector
            def _(dve):
                own = Chain(dve, setup_dve)
                dve.wait_ge(wqkv0_loaded, 16)
                wq = stage3[:, 0:NQKV0]
                for j in range(3):
                    dve.wait_ge(lora_ready, j + 1)
                    c = slice(512 * j, 512 * (j + 1))
                    own.link(dve.scalar_tensor_tensor(out=wq[:, c], in0=bank[j][:, :], scalar=LORA_SCALE,
                                                      in1=wq[:, c], op0=ALU.mult, op1=ALU.add))
                own.link(dve.tensor_copy(wqkv0_h[:, :], wq))
                own.link(dve.tensor_tensor(wqkv0_l[:, :], wq, wqkv0_h[:, :].bitcast(F32), ALU.subtract))
                dve.wait_ge(lora_ready, 4)
                dve.wait_ge(w_loaded, 16 * n_loads)
                for j in range(2):
                    w = wo0[:, 4 * j:4 * j + 4, :].rearrange("p c d -> p (c d)")
                    own.link(dve.scalar_tensor_tensor(out=w, in0=bank[3 + j][:, :], scalar=LORA_SCALE,
                                                      in1=w, op0=ALU.mult, op1=ALU.add))
                for n, (high, low, src, st) in enumerate(splits):
                    dve.wait_ge(stage_loaded, 16 * (n + 1))
                    raw = st[:, 0:src.shape[1]]
                    own.link(dve.tensor_copy(high, raw))
                    if low is not None:
                        own.link(dve.tensor_tensor(low, raw, high.bitcast(F32), ALU.subtract))
                    dve.sem_inc(stage_split, 1)
                dve.wait_ge(zeroed, 3)
                own.link(dve.memset(cw[:, :, 2 * E1:2 * E1 + 1], 1.0))
        nc.sync.sem_inc(y_stored, 16)

        with nc.Fori(0, NB) as b:
            with nc.Block(no_gpsimd_drain=True) as block:
                @block.sync
                def _(sp):
                    sp.wait_ge(x_taken, 1)
                    sp.wait_ge(y_stored, (b + 1) * 16)
                    nxt = sp.snap((b + 1) % NB)
                    sp.dma_start(x_in[:, :, :], a["x"][bass.ds(nxt, 1)].rearrange("a p t d -> p (a t) d"))\
                        .then_inc(x_loaded, 16)
                    sp.wait_ge(y_ready, 1)
                    sp.dma_start(out[bass.ds(b, 1)].rearrange("a p t d -> p (a t) d"), y_out[:, :, :])\
                        .then_inc(y_stored, 16)
                    sp.wait_ge(x_loaded, 16)

                @block.tensor
                def _(pe):
                    def turn_xn(s):
                        for t in range(T):
                            pe.wait_ge(normed, 2 * s + t + 1)
                            tr = pe.transpose(bank[7][:, t * P:(t + 1) * P], xn[:, t, :], ident[:, :])
                        tr.then_inc(xT_psum, 1)

                    def three(dst, lh, ll, rh, rl, start=True, **k):
                        pe.matmul(dst, lh, rl, start=start, stop=False, **k)
                        pe.matmul(dst, ll, rh, start=False, stop=False, **k)
                        return pe.matmul(dst, lh, rh, start=False, stop=True, **k)

                    def attention(layer, scores, outputs, extra):
                        h0 = NQ * layer
                        for i in range(NQ + 3):
                            extra(i)
                            if i < NQ:
                                if i >= 2:
                                    pe.wait_ge(exp_ready, 2 * (h0 + i - 1))
                                scores(i, bank[i % 2]).then_inc(scores_psum, 1)
                            if 2 <= i < NQ + 2:
                                h = i - 2
                                pe.wait_ge(prob_ready, 2 * (h0 + h + 1))
                                if h >= 2:
                                    pe.wait_ge(probT_ready, h0 + h - 1)
                                for t in range(T):
                                    for k in range(2):
                                        c = k * S + t * P
                                        tr = pe.transpose(bank[2 + h % 2][:, c:c + P],
                                                          prob[:, (h0 + h) % 3, t, k * P:(k + 1) * P], ident[:, :])
                                tr.then_inc(probT_psum, 1)
                            if i >= 3:
                                h = i - 3
                                pe.wait_ge(probT_ready, h0 + h + 1)
                                outputs(h).then_inc(heads_done, 1)

                    turn_xn(0)
                    pe.wait_ge(xT_ready, 1)
                    for t in range(T):
                        tok = slice(t * P, (t + 1) * P)
                        for j in (2, 0, 1):
                            c = slice(512 * j, 512 * (j + 1))
                            three(bank[3 * t + j][:, :], xT_h[:, tok], xT_l[:, tok], wqkv0_h[:, c],
                                  wqkv0_l[:, c]).then_inc(qkv_psum, 1)

                    fills = [0]

                    def turn(blocks, first):
                        n = first + fills[0]
                        if fills[0] >= 2:
                            pe.wait_ge(turned_out, n - 1)
                        for j, block_in in enumerate(blocks):
                            tr = pe.transpose(bank[6 + n % 2][:, j * P:(j + 1) * P], block_in, ident[:, :])
                        tr.then_inc(turned, 1)
                        fills[0] += 1

                    pe.wait_ge(stacked, 4)
                    for kv in range(NKV):
                        turn([k_stk[:, t, kv, part, :] for part in range(2) for t in range(T)], 0)

                    def extra0(i):
                        if i == 0:
                            pe.wait_ge(stacked, 5)
                            turn([q_stk[:, t, j, :] for j in range(2) for t in range(T)], 0)
                        if i % 2 == 0 and i < NQ - 2:
                            if i == 6:
                                pe.wait_ge(stacked, 6)
                            turn([q_stk[:, t, i + 2 + j, :] for j in range(2) for t in range(T)], 0)

                    def scores0(h, dst):
                        pe.wait_ge(turned_out, 4 + h // 2 + 1)
                        kv = h // (NQ // NKV)
                        for t in range(T):
                            q = qT[:, h, t * P:(t + 1) * P]
                            pe.matmul(dst[:, t * S:(t + 1) * S], q, kT[:, kv, 1, :], start=True, stop=False)
                            mm = pe.matmul(dst[:, t * S:(t + 1) * S], q, kT[:, kv, 0, :], start=False, stop=True)
                        return mm

                    def outputs0(h):
                        dst = bank[4 + h // 2 % 2][HD * (h % 2):HD * (h % 2 + 1), 0:S]
                        if h % 2 == 0 and h >= 4:
                            pe.wait_ge(aT_ready, h // 2 - 1)
                        for k in range(2):
                            mm = pe.matmul(dst, v0[:, k, h // (NQ // NKV), :], probT[:, h % 3, k, :],
                                           start=(k == 0), stop=(k == 1))
                        return mm

                    attention(0, scores0, outputs0, extra0)
                    pe.wait_ge(aT_ready, NQ // 2)
                    for t in range(T):
                        for j in range(NQ // 2):
                            mm = pe.matmul(bank[6][:, t * D:(t + 1) * D], aT[:, j, t * P:(t + 1) * P],
                                           wo0[:, j, :], start=(j == 0), stop=(j == NQ // 2 - 1))
                    mm.then_inc(attn_psum, 1)

                    turn_xn(1)
                    pe.wait_ge(xT_ready, 2)
                    for t in range(T):
                        mm = pe.matmul(bank[7][:, 12 * t:12 * t + 12], xT[:, t * P:(t + 1) * P], wroute0[:, :],
                                       start=True, stop=True)
                    mm.then_inc(logits_psum, 1)

                    def down0(e):
                        pe.wait_ge(hid0_ready, 4 * (e + 1))
                        if e >= 2:
                            pe.wait_ge(exp_added, e - 1)
                        for t in range(T):
                            for c in range(4):
                                mm = pe.matmul(bank[4 + e % 2][:, t * D:(t + 1) * D],
                                               hT[:, (e % 2) * 4 + c, t * P:(t + 1) * P], w2_0[:, 4 * e + c, :],
                                               start=(c == 0), stop=(c == 3))
                        mm.then_inc(exp_out, 1)

                    for e in range(E0):
                        for f in range(2):
                            n = 2 * e + f
                            if n >= 4:
                                pe.wait_ge(hid0_ready, 2 * (n - 3))
                            for c in range(2):
                                w = slice((2 * n + c) * P, (2 * n + c + 1) * P)
                                mm = three(bank[n % 4][:, c * S:(c + 1) * S], w1_0h[:, w], w1_0l[:, w],
                                           xT_h[:, :], xT_l[:, :])
                            mm.then_inc(hid0_psum, 1)
                        if e >= 1:
                            down0(e - 1)
                    down0(E0 - 1)

                    def turn_cw(s):
                        pe.wait_ge(cw_ready, s + 1)
                        for t in range(T):
                            tr = pe.transpose(bank[7][:, t * P:(t + 1) * P], cw[:, t, :], ident[:, :])
                        tr.then_inc(cwT_psum, 1)
                        pe.wait_ge(cwT_ready, s + 1)

                    turn_cw(0)
                    for t in range(T):
                        mm = pe.matmul(bank[6][:, t * D:(t + 1) * D], cwT[:, t * P:(t + 1) * P].bitcast(F32),
                                       b2_0[:, :], start=True, stop=True)
                    mm.then_inc(exp_out, 1)

                    turn_xn(2)
                    pe.wait_ge(xT_ready, 3)
                    for t in range(T):
                        tok = slice(t * P, (t + 1) * P)
                        three(bank[t][:, 0:3 * D], xT_h[:, tok], xT_l[:, tok], wqkv1_h[:, :],
                              wqkv1_l[:, :]).then_inc(qkv_psum, 1)
                    fills[0] = 0
                    pe.wait_ge(stacked, 8)
                    for stk in (k_stk1, q_stk1):
                        for g in range(0, G1, 2):
                            turn([stk[:, t, 4 * (g + j):4 * (g + j) + 4, :].rearrange("p h c -> p (h c)")
                                  for j in range(2) for t in range(T)], 12)

                    def scores1(h, dst):
                        pe.wait_ge(turned_out, 12 + 2 + h // 8 + 1)
                        rows = slice(PAD1 * (h % 4), PAD1 * (h % 4 + 1))
                        for t in range(T):
                            mm = pe.matmul(dst[:, t * S:(t + 1) * S], qT[rows, h // 4, t * P:(t + 1) * P],
                                           kT[rows, h // 8, h // 4 % 2, :], start=True, stop=True)
                        return mm

                    def outputs1(h):
                        g, j = h // 4, h % 4
                        dst = bank[4 + g % 2][PAD1 * j:PAD1 * (j + 1), 0:S]
                        if j == 0:
                            pe.wait_ge(aT_ready, 8 + g - 1 if g >= 2 else 8)
                        for k in range(2):
                            mm = pe.matmul(dst, v1[:, k, h, :], probT[:, (NQ + h) % 3, k, :],
                                           start=(k == 0), stop=(k == 1), tile_position=(0, PAD1 * j))
                        return mm

                    attention(1, scores1, outputs1, lambda i: None)
                    pe.wait_ge(aT_ready, 8 + G1)
                    for t in range(T):
                        for g in range(G1):
                            mm = pe.matmul(bank[6][:, t * D:(t + 1) * D], aT[:, g, t * P:(t + 1) * P],
                                           wo1[:, g, :], start=(g == 0), stop=(g == G1 - 1))
                    mm.then_inc(attn_psum, 1)

                    turn_xn(3)
                    pe.wait_ge(xT_ready, 4)
                    for t in range(T):
                        mm = pe.matmul(bank[7][:, E1 * t:E1 * (t + 1)], xT[:, t * P:(t + 1) * P], wgate1[:, :],
                                       start=True, stop=True)
                    mm.then_inc(logits_psum, 1)

                    def chunks(n):
                        return [C1 - 1] if n == 0 else [2 * n - 2, 2 * n - 1]

                    def up1(n):
                        if n >= 2:
                            pe.wait_ge(gated_ready, 2 * (n - 2) + 1)
                        for which in range(2):
                            for j, c in enumerate(chunks(n)):
                                w = slice(c * P, (c + 1) * P)
                                mm = three(bank[2 * which + n % 2][:, j * S:(j + 1) * S], w13_h[:, which, w],
                                           w13_l[:, which, w], xT_h[:, :], xT_l[:, :])
                        mm.then_inc(up1_psum, 1)

                    def spread1(n):
                        if n >= 3:
                            pe.wait_ge(hid1_ready, n - 1)
                        for j, c in enumerate(chunks(n)):
                            mm = pe.matmul(bank[4 + n % 2][:, j * S:(j + 1) * S], spread[:, c * P:(c + 1) * P],
                                           cwT[:, :], start=True, stop=True)
                        mm.then_inc(spread_psum, 1)

                    def down1(n):
                        pe.wait_ge(hid1_ready, n + 1)
                        for j, c in enumerate(chunks(n)):
                            for t in range(T):
                                mm = pe.matmul(bank[6][:, t * D:(t + 1) * D],
                                               hT[:, 2 * (n % 4) + j, t * P:(t + 1) * P], w2_1[:, c, :],
                                               start=(n == 0 and t == 0), stop=False, skip_group_check=True)
                        mm.then_inc(down1_done, 1)

                    up1(0)
                    up1(1)
                    down1(0)
                    turn_cw(1)
                    spread1(1)
                    for n in range(2, 9):
                        up1(n)
                        spread1(n)
                        down1(n - 1)
                    down1(8)
                    for t in range(T):
                        mm = pe.matmul(bank[6][:, t * D:(t + 1) * D], cwT[:, t * P:(t + 1) * P].bitcast(F32),
                                       b2_1[:, :], start=False, stop=(t == T - 1), skip_group_check=True)
                    mm.then_inc(attn_psum, 1)

                @block.scalar
                def _(act):
                    own = Chain(act, act_own)

                    def exps(layer, i):
                        h = NQ * layer + i
                        act.wait_ge(max_ready, h + 1)
                        if h >= 3:
                            act.wait_ge(probT_psum, h - 2)
                        if h >= 4:
                            act.wait_ge(rsum_ready, h - 3)
                        for t in range(T):
                            act.activation(prob[:, h % 3, t, :], bank[i % 2][:, t * S:(t + 1) * S], ACT.Exp,
                                           bias=nmax[:, h % 4, t:t + 1],
                                           accum_out=psums[:, h % 4, t:t + 1]).then_inc(exp_ready, 1)

                    def copy_probT(layer, i):
                        h = NQ * layer + i
                        act.wait_ge(probT_psum, h + 1)
                        if h >= 3:
                            act.wait_ge(heads_done, h - 2)
                        act.activation(probT[:, h % 3, :, :].rearrange("p k s -> p (k s)"), bank[2 + i % 2][:, :],
                                       ACT.Copy).then_inc(probT_ready, 1)

                    def turned_copy(n, dst):
                        act.wait_ge(turned, n + 1)
                        act.activation(dst, bank[6 + n % 2][:, :], ACT.Copy).then_inc(turned_out, 1)

                    for n in range(4):
                        turned_copy(n, kT[:, n, :, :].rearrange("p a s -> p (a s)"))
                    turned_copy(4, qT[:, 0:2, :].rearrange("p a s -> p (a s)"))
                    for i in range(NQ + 3):
                        if i % 2 == 0 and i < NQ - 2:
                            turned_copy(5 + i // 2, qT[:, i + 2:i + 4, :].rearrange("p a s -> p (a s)"))
                        if i < NQ:
                            exps(0, i)
                        if 2 <= i < NQ + 2:
                            copy_probT(0, i - 2)
                        if i >= 4 and i % 2 == 0:
                            j = i // 2 - 2
                            act.wait_ge(heads_done, 2 * j + 2)
                            act.activation(aT[:, j, :], bank[4 + j % 2][:, 0:S], ACT.Copy).then_inc(aT_ready, 1)

                    for n in range(2):
                        act.wait_ge(route_in, n + 1)
                        act.activation(gate_z[:, :, 0:(NLANG, E0)[n]], gate_z[:, :, 0:(NLANG, E0)[n]],
                                       ACT.Exp).then_inc(route_exp, 1)
                    for c in range(C0):
                        act.wait_ge(hid0_psum, c // 2 + 1)
                        if c >= 8:
                            act.wait_ge(exp_out, c // 4 - 1)
                        act.activation(hT[:, c % 8, :], bank[c // 2 % 4][:, (c % 2) * S:(c % 2 + 1) * S],
                                       ACT.Gelu, bias=b1_0[:, c:c + 1]).then_inc(hid0_ready, 1)

                    for n in range(12, 16):
                        g = n % 4 * 2 % 4
                        dst = kT[:, g // 2, :, :] if n < 14 else qT[:, g:g + 2, :]
                        turned_copy(n, dst.rearrange("p a s -> p (a s)"))
                    for i in range(NQ + 4):
                        if i < NQ:
                            exps(1, i)
                        if 2 <= i < NQ + 2:
                            copy_probT(1, i - 2)
                        if i >= 7 and i % 4 == 3:
                            g = i // 4 - 1
                            act.wait_ge(heads_done, NQ + 4 * g + 4)
                            act.activation(aT[:, g, :], bank[4 + g % 2][:, 0:S], ACT.Copy,
                                           scale=float(1 / np.sqrt(D))).then_inc(aT_ready, 1)
                    act.wait_ge(route_in, 3)
                    act.activation(gate_z[:, :, :], gate_z[:, :, :], ACT.Exp).then_inc(route_exp, 1)
                    for k in range(C1):
                        n, j = (0, 0) if k == 0 else ((k + 1) // 2, (k + 1) % 2)
                        c = C1 - 1 if k == 0 else k - 1
                        act.wait_ge(up1_psum, n + 1)
                        if k >= 2:
                            act.wait_ge(gated_ready, k - 1)
                        act.activation(silu[:, k % 2, :], bank[n % 2][:, j * S:(j + 1) * S], ACT.Silu,
                                       bias=b13[:, 0, c:c + 1]).then_inc(silu_ready, 1)

                @block.vector
                def _(dve):
                    own = Chain(dve, dve_own)
                    link = own.link

                    def layer_norm(src):
                        for t in range(T):
                            link(dve.bn_stats(stats[:, t, :], src[:, t, :]))
                        for t in range(T):
                            link(dve.bn_aggr(mv[:, t, :], stats[:, t, :]))
                        link(dve.tensor_scalar(var[:, :], mv[:, :, 1], LN_EPS, None, ALU.add))
                        bits = rstd[:, :].bitcast(I32)
                        link(dve.tensor_scalar(bits, var[:, :].bitcast(I32), 1, None, ALU.logical_shift_right))
                        link(dve.tensor_scalar(bits, bits, -1.0, float(0x5F3759DF), ALU.mult, ALU.add))
                        for _ in range(3):
                            link(dve.tensor_tensor(newton[:, :], rstd[:, :], rstd[:, :], ALU.mult))
                            link(dve.scalar_tensor_tensor(out=newton[:, :], in0=newton[:, :], scalar=-0.5,
                                                          in1=var[:, :], op0=ALU.mult, op1=ALU.mult))
                            link(dve.scalar_tensor_tensor(out=rstd[:, :], in0=newton[:, :], scalar=1.5,
                                                          in1=rstd[:, :], op0=ALU.add, op1=ALU.mult))
                        for t in range(T):
                            dve.tensor_scalar(xn[:, t, :], src[:, t, :], mv[:, t, 0:1], rstd[:, t:t + 1],
                                              ALU.subtract, ALU.mult).then_inc(normed, 1)

                    def split_xT(s):
                        dve.wait_ge(xT_psum, s + 1)
                        link(dve.tensor_copy(xT[:, :], bank[7][:, 0:S]))
                        link(dve.tensor_copy(xT_h[:, :], xT[:, :]))
                        dve.tensor_tensor(xT_l[:, :], xT[:, :], xT_h[:, :].bitcast(F32), ALU.subtract)\
                            .then_inc(xT_ready, 1)

                    def softmax_steps(layer, i):
                        if i < NQ:
                            h = NQ * layer + i
                            dve.wait_ge(scores_psum, h + 1)
                            if h >= 4:
                                dve.wait_ge(exp_ready, 2 * (h - 3))
                            dve.tensor_reduce(nmax[:, h % 4, :], bank[i % 2][:, :].rearrange("p (t s) -> p t s", t=T),
                                              AX_X, ALU.max, negate=True).then_inc(max_ready, 1)
                        if i >= 1:
                            h = NQ * layer + i - 1
                            dve.wait_ge(exp_ready, 2 * (h + 1))
                            dve.reciprocal(rsums[:, h % 4, :], psums[:, h % 4, :]).then_inc(rsum_ready, 1)
                            dve.wait_ge(rsum_ready, h + 1)
                            for t in range(T):
                                dve.tensor_scalar(prob[:, h % 3, t, :], prob[:, h % 3, t, :],
                                                  rsums[:, h % 4, t:t + 1], None, ALU.mult)\
                                    .then_inc(prob_ready, 1)

                    layer_norm(x_in)
                    split_xT(0)
                    for t, j in ((0, 2), (1, 2), (0, 0), (1, 0), (0, 1), (1, 1)):
                        heads = 8 if j < 2 else NKV
                        n = heads * HD
                        ps = bank[3 * t + j]
                        dve.wait_ge(qkv_psum, 3 * t + (2, 3, 1)[j])
                        for k, dst in ((0, ra), (1, rb)):
                            table = rope[:, t, k + (0 if j < 2 else 2), :].unsqueeze(1).to_broadcast([P, 2 * heads, HALF])
                            link(dve.tensor_tensor(dst[:, 0:n].rearrange("p (h d) -> p h d", d=HALF),
                                                   ps[:, 0:n].rearrange("p (h d) -> p h d", d=HALF), table, ALU.mult))
                        xc = ra[:, 0:n].rearrange("p (h a d) -> p h a d", a=2, d=HALF)
                        xs = rb[:, 0:n].rearrange("p (h a d) -> p h a d", a=2, d=HALF)
                        o = ro[:, 0:n].rearrange("p (h a d) -> p h a d", a=2, d=HALF)
                        link(dve.tensor_tensor(o[:, :, 0, :], xc[:, :, 0, :], xs[:, :, 1, :], ALU.subtract))
                        link(dve.tensor_tensor(o[:, :, 1, :], xs[:, :, 0, :], xc[:, :, 1, :], ALU.add))
                        o = ro[:, 0:n].rearrange("p (h d) -> p h d", d=HD)
                        if j < 2:
                            stk = q_stk[:, t, 8 * j:8 * j + 8, :]
                            link(dve.tensor_copy(stk[:, :, 0:HD].bitcast(F32R), o))
                            dve.tensor_tensor(stk[:, :, HD:2 * HD].bitcast(F32R), o, stk[:, :, 0:HD], ALU.subtract)\
                                .then_inc(stacked, 1)
                            if t == 0:
                                dve.wait_ge(stacked, (3, 5)[j])
                        else:
                            link(dve.tensor_copy(v0[:, t, :, :].rearrange("p h d -> p (h d)"), ps[:, n:2 * n]))
                            for half in range(2):
                                c = slice(half * HD, (half + 1) * HD)
                                link(dve.tensor_copy(k_stk[:, t, :, 0, c].bitcast(F32R), o))
                            link(dve.tensor_tensor(k_stk[:, t, :, 1, 0:HD].bitcast(F32R), o, k_stk[:, t, :, 0, 0:HD],
                                                   ALU.subtract))
                            dve.tensor_tensor(k_stk[:, t, :, 1, HD:2 * HD].bitcast(F32R), o, k_stk[:, t, :, 0, 0:HD],
                                              ALU.subtract).then_inc(stacked, 1)
                    for i in range(NQ + 1):
                        softmax_steps(0, i)
                    dve.wait_ge(attn_psum, 1)
                    link(dve.tensor_tensor(xres[:, :, :], bank[6][:, 0:S].rearrange("p (t d) -> p t d", t=T),
                                           x_in[:, :, :], ALU.add))
                    dve.sem_inc(x_taken, 1)

                    def g(k, n):
                        return gate_t[:, k, :, 0:n]

                    def sc(k):
                        return gate_s[:, k, :]

                    def wide(v, n):
                        return v.unsqueeze(2).to_broadcast([P, T, n])

                    def softmax_in(z, n):
                        link(dve.tensor_reduce(sc(0), z, AX_X, ALU.max))
                        link(dve.tensor_tensor(gate_z[:, :, 0:n], z, wide(sc(0), n), ALU.subtract))
                        dve.sem_inc(route_in, 1)

                    def softmax_out(n, dst):
                        link(dve.tensor_reduce(sc(1), gate_z[:, :, 0:n], AX_X, ALU.add))
                        link(dve.reciprocal(sc(2), sc(1)))
                        link(dve.tensor_tensor(dst, gate_z[:, :, 0:n], wide(sc(2), n), ALU.mult))

                    def top(slot, vals, n):
                        for t in range(T):
                            link(dve.max(out=top8[:, slot, t, :], in_=vals[:, t, :]))
                        for t in range(T):
                            link(dve.max_index(topi[:, slot, t, :], top8[:, slot, t, :], vals[:, t, :]))
                        link(dve.tensor_copy(topf[:, slot, :, :], topi[:, slot, :, :]))

                    def hit(dst, slot, k, n):
                        link(dve.tensor_tensor(dst, iota[:, 0:n].unsqueeze(1).to_broadcast([P, T, n]),
                                               wide(topf[:, slot, :, k], n), ALU.is_equal))

                    layer_norm(xres)
                    split_xT(1)
                    dve.wait_ge(logits_psum, 1)
                    nr = NLANG + E0
                    b_route = bias[:, B_ROUTE0:B_ROUTE0 + nr].unsqueeze(1).to_broadcast([P, T, nr])
                    link(dve.tensor_tensor(g(0, nr), bank[7][:, 0:T * nr].rearrange("p (t n) -> p t n", t=T),
                                           b_route, ALU.add))
                    softmax_in(g(0, NLANG), NLANG)
                    dve.wait_ge(route_exp, 1)
                    softmax_out(NLANG, g(1, NLANG))
                    link(dve.tensor_tensor(g(2, NLANG - 1), g(1, NLANG - 1), gate_t[:, 1, :, 1:NLANG], ALU.add))
                    link(dve.tensor_copy(gate_t[:, 2, :, NLANG - 1:NLANG], gate_t[:, 1, :, NLANG - 1:NLANG]))
                    for r in range(E0 // NLANG):
                        link(dve.scalar_tensor_tensor(out=gate_t[:, 3, :, r * NLANG:(r + 1) * NLANG],
                                                      in0=g(2, NLANG), scalar=0.1,
                                                      in1=gate_t[:, 0, :, (r + 1) * NLANG:(r + 2) * NLANG],
                                                      op0=ALU.mult, op1=ALU.add))
                    softmax_in(g(3, E0), E0)
                    dve.wait_ge(route_exp, 2)
                    softmax_out(E0, g(4, E0))
                    top(0, g(4, E0), E0)
                    link(dve.tensor_tensor(sc(3), top8[:, 0, :, 0], top8[:, 0, :, 1], ALU.add))
                    link(dve.reciprocal(sc(4), sc(3)))
                    for k in range(2):
                        link(dve.tensor_tensor(sc(5 + k), top8[:, 0, :, k], sc(4), ALU.mult))
                        hit(g(5 + k, E0), 0, k, E0)
                        link(dve.tensor_tensor(g(7 + k, E0), g(5 + k, E0), wide(sc(5 + k), E0), ALU.mult))
                    link(dve.tensor_tensor(cw[:, :, 0:E0], g(7, E0), g(8, E0), ALU.add))
                    dve.sem_inc(cw_ready, 1)
                    for e in range(E0):
                        dve.wait_ge(exp_out, e + 1)
                        for t in range(T):
                            dve_add = dve.scalar_tensor_tensor(
                                out=xres[:, t, :], in0=bank[4 + e % 2][:, t * D:(t + 1) * D],
                                scalar=cw[:, t, e:e + 1], in1=xres[:, t, :], op0=ALU.mult, op1=ALU.add)
                            if t < T - 1:
                                link(dve_add)
                        dve_add.then_inc(exp_added, 1)
                        dve.wait_ge(exp_added, e + 1)

                    def copy_cw(s):
                        dve.wait_ge(cwT_psum, s + 1)
                        dve.tensor_copy(cwT[:, :] if s else cwT[:, :], bank[7][:, 0:S]).then_inc(cwT_ready, 1)

                    copy_cw(0)
                    dve.wait_ge(exp_out, E0 + 1)
                    dve.tensor_tensor(xres[:, :, :], bank[6][:, 0:S].rearrange("p (t d) -> p t d", t=T),
                                      xres[:, :, :], ALU.add).then_inc(exp_added, 1)
                    dve.wait_ge(exp_added, E0 + 1)

                    layer_norm(xres)
                    split_xT(2)
                    for t in range(T):
                        dve.wait_ge(qkv_psum, 6 + t + 1)
                        link(dve.tensor_tensor(qkv1[:, t, :], bank[t][:, 0:3 * D], bias[:, B_QKV1:B_QKV1 + 3 * D],
                                               ALU.add))
                    link(dve.memset(v1[:, :, :, :], 0.0))
                    link(dve.tensor_copy(v1[:, :, :, 0:HD1], qkv1[:, :, 2 * D:3 * D].rearrange("p t (h e) -> p t h e", e=HD1)))
                    for t in range(T):
                        q = qkv1[:, t, 0:D].rearrange("p (h e) -> p h e", e=HD1)
                        k = qkv1[:, t, D:2 * D].rearrange("p (h e) -> p h e", e=HD1)
                        part = [slice(HD1 * i, HD1 * (i + 1)) for i in range(4)]
                        qs, ks = q_stk1[:, t, :, :], k_stk1[:, t, :, :]
                        for i in (0, 2):
                            link(dve.tensor_copy(qs[:, :, part[i]].bitcast(F32R), q))
                        for i in (1, 3):
                            link(dve.tensor_tensor(qs[:, :, part[i]].bitcast(F32R), q, qs[:, :, part[0]], ALU.subtract))
                        for i in (0, 1):
                            link(dve.tensor_copy(ks[:, :, part[i]].bitcast(F32R), k))
                        for i in (2, 3):
                            link(dve.tensor_tensor(ks[:, :, part[i]].bitcast(F32R), k, ks[:, :, part[0]], ALU.subtract))
                        dve.sem_inc(stacked, 1)
                    for i in range(NQ + 1):
                        softmax_steps(1, i)
                    dve.wait_ge(attn_psum, 2)
                    link(dve.tensor_tensor(xres[:, :, :], bank[6][:, 0:S].rearrange("p (t d) -> p t d", t=T),
                                           xres[:, :, :], ALU.add))
                    link(dve.tensor_tensor(xres[:, :, :], xres[:, :, :],
                                           bias[:, B_OUT1:B_OUT1 + D].unsqueeze(1).to_broadcast([P, T, D]), ALU.add))

                    layer_norm(xres)
                    split_xT(3)
                    dve.wait_ge(logits_psum, 2)
                    link(dve.tensor_tensor(g(0, E1), bank[7][:, 0:T * E1].rearrange("p (t n) -> p t n", t=T),
                                           bias[:, B_GATE1:B_GATE1 + E1].unsqueeze(1).to_broadcast([P, T, E1]),
                                           ALU.add))
                    softmax_in(g(0, E1), E1)

                    def gate_chunk(k):
                        n, j = (0, 0) if k == 0 else ((k + 1) // 2, (k + 1) % 2)
                        c = C1 - 1 if k == 0 else k - 1
                        dve.wait_ge(silu_ready, k + 1)
                        dst = hT[:, 0, :] if k == 0 else gated[:, n % 2, j, :]
                        ins = dve.scalar_tensor_tensor(out=dst, in0=bank[2 + n % 2][:, j * S:(j + 1) * S],
                                                       scalar=b13[:, 1, c:c + 1], in1=silu[:, k % 2, :],
                                                       op0=ALU.add, op1=ALU.mult)
                        ins.then_inc(gated_ready, 1)
                        if k == 0:
                            dve.wait_ge(gated_ready, 1)
                            dve.sem_inc(hid1_ready, 1)

                    def weigh(n):
                        dve.wait_ge(spread_psum, n)
                        dve.wait_ge(gated_ready, 2 * n + 1)
                        if n >= 4:
                            dve.wait_ge(down1_done, n - 3)
                        dve.tensor_tensor(hT[:, 2 * (n % 4):2 * (n % 4) + 2, :], gated[:, n % 2, :, :],
                                          bank[4 + n % 2][:, :].rearrange("p (c s) -> p c s", c=2), ALU.mult)\
                            .then_inc(hid1_ready, 1)

                    dve.wait_ge(route_exp, 3)
                    softmax_out(E1, g(1, E1))
                    quad = gate_t[:, 1, :, :].rearrange("p t (g a b) -> p t g a b", a=2, b=2)
                    hi, lo = g(2, 16), g(3, 16)
                    link(dve.tensor_tensor(hi, gate_t[:, 1, :, :].rearrange("p t (g b) -> p t g b", b=2)[:, :, :, 0],
                                           gate_t[:, 1, :, :].rearrange("p t (g b) -> p t g b", b=2)[:, :, :, 1], ALU.max))
                    link(dve.tensor_tensor(lo, gate_t[:, 1, :, :].rearrange("p t (g b) -> p t g b", b=2)[:, :, :, 0],
                                           gate_t[:, 1, :, :].rearrange("p t (g b) -> p t g b", b=2)[:, :, :, 1], ALU.min))
                    hi2, lo2 = (v.rearrange("p t (g a) -> p t g a", a=2) for v in (hi, lo))
                    link(dve.tensor_tensor(g(4, GROUPS), hi2[:, :, :, 0], hi2[:, :, :, 1], ALU.max))
                    link(dve.tensor_tensor(g(5, GROUPS), hi2[:, :, :, 0], hi2[:, :, :, 1], ALU.min))
                    link(dve.tensor_tensor(g(6, GROUPS), lo2[:, :, :, 0], lo2[:, :, :, 1], ALU.max))
                    link(dve.tensor_tensor(g(7, GROUPS), g(5, GROUPS), g(6, GROUPS), ALU.max))
                    link(dve.tensor_tensor(g(8, GROUPS), g(4, GROUPS), g(7, GROUPS), ALU.add))
                    top(0, g(8, GROUPS), GROUPS)
                    hit(g(9, GROUPS), 0, 0, GROUPS)
                    for k in range(1, TOPG):
                        hit(g(10, GROUPS), 0, k, GROUPS)
                        link(dve.tensor_tensor(g(9, GROUPS), g(9, GROUPS), g(10, GROUPS), ALU.add))
                    link(dve.tensor_scalar(g(10, GROUPS), g(9, GROUPS), -1.0, None, ALU.add))
                    by_group = gate_t[:, 1, :, :].rearrange("p t (g e) -> p t g e", g=GROUPS)
                    kept = gate_t[:, 11, :, :].rearrange("p t (g e) -> p t g e", g=GROUPS)
                    for t in range(T):
                        link(dve.tensor_tensor(kept[:, t], by_group[:, t],
                                               gate_t[:, 9, t, 0:GROUPS].unsqueeze(2).to_broadcast([P, GROUPS, 4]), ALU.mult))
                        link(dve.tensor_tensor(kept[:, t], kept[:, t],
                                               gate_t[:, 10, t, 0:GROUPS].unsqueeze(2).to_broadcast([P, GROUPS, 4]), ALU.add))
                    top(1, g(11, E1), E1)
                    for k in range(TOPK1):
                        hit(g(2, E1), 1, k, E1)
                        dst = g(3 + k % 2, E1)
                        link(dve.tensor_tensor(g(5, E1) if k else dst, g(2, E1), wide(top8[:, 1, :, k], E1), ALU.mult))
                        if k:
                            link(dve.tensor_tensor(dst, g(5, E1), g(3 + (k - 1) % 2, E1), ALU.add))
                    whole = g(3 + (TOPK1 - 1) % 2, E1)
                    link(dve.tensor_copy(cw[:, :, 0:E1].bitcast(F32R), whole))
                    link(dve.tensor_tensor(cw[:, :, E1:2 * E1].bitcast(F32R), whole, cw[:, :, 0:E1], ALU.subtract))
                    dve.sem_inc(cw_ready, 1)
                    gate_chunk(0)
                    copy_cw(1)
                    for n in range(1, 9):
                        gate_chunk(2 * n - 1)
                        gate_chunk(2 * n)
                        weigh(n)
                    dve.wait_ge(x_loaded, 16)
                    dve.wait_ge(attn_psum, 3)
                    dve.tensor_tensor(y_out[:, :, :], bank[6][:, 0:S].rearrange("p (t d) -> p t d", t=T),
                                      xres[:, :, :], ALU.add).then_inc(y_ready, 1)

            nc.all_engine_barrier(sems_to_clear=range(sems[0].num, sems[-1].num + 1))
        nc.sync.wait_ge(y_stored, 16 * (NB + 1))


def laid_out(i):
    f = np.float32

    def halves(w):
        h = w.shape[0] // HD
        return w.reshape(h, HALF, 2, -1).transpose(0, 2, 1, 3).reshape(w.shape)

    def cat(*xs):
        return np.ascontiguousarray(np.concatenate(xs, axis=-1))

    inv_freq = (f(1.0) / f(THETA) ** (np.arange(0, HD, 2, dtype=f) / f(HD))).astype(f)
    ang = np.arange(S, dtype=f)[:, None] * inv_freq[None, :]
    cos, sin = np.cos(ang).astype(f), np.sin(ang).astype(f)
    scale = f(1 / np.sqrt(HD))
    rope = np.stack([cos * scale, sin * scale, cos, sin], axis=1).reshape(T, P, 4, HALF)
    spread = np.zeros((P, C1 - 1, 2, H1), f)
    for e in range(E1):
        spread[e, e // 2, e % 2] = 1
        spread[E1 + e, e // 2, e % 2] = 1
    wo1 = np.zeros((G1, 4, PAD1, D), f)
    wo1[:, :, 0:HD1] = i["L1_attn_W_out"].reshape(G1, 4, HD1, D)

    def columns(w, sw):
        return cat(w.transpose(1, 0, 2).reshape(D, E1 * H1), sw)

    def chunked(w, sw):
        return np.concatenate([w.reshape(-1, D), sw]).reshape(-1, P, D).transpose(1, 0, 2)

    def per_chunk(b, sb):
        return np.concatenate([b.reshape(-1), sb]).reshape(-1, P).T

    return {
        "x": i["L0_attn_x"].reshape(NB, T, P, D).transpose(0, 2, 1, 3),
        "wqkv0": cat(halves(i["L0_attn_Wq"]).T, halves(i["L0_attn_Wk"]).T, i["L0_attn_Wv"].T),
        "lora_a": cat(i["L0_attn_qA"], i["L0_attn_kA"], i["L0_attn_vA"], i["L0_attn_oA"]),
        "lora_b": cat(halves(i["L0_attn_qB"]).T, halves(i["L0_attn_kB"]).T, i["L0_attn_vB"].T,
                      i["L0_attn_oB"].T),
        "wo0": i["L0_attn_Wo"].T.reshape(NQ // 2, P, D).transpose(1, 0, 2),
        "wroute0": cat(i["L0_ffn_lang_w"].T, i["L0_ffn_router_w"].T),
        "w1_0": i["L0_ffn_w1"].transpose(1, 0, 2).reshape(D, E0 * H0),
        "b1_0": i["L0_ffn_b1"].reshape(C0, P).T,
        "w2_0": i["L0_ffn_w2"].reshape(C0, P, D).transpose(1, 0, 2),
        "b2_0": i["L0_ffn_b2"],
        "wqkv1": i["L1_attn_W_qkv"],
        "wo1": wo1.reshape(G1, P, D).transpose(1, 0, 2),
        "wgate1": i["L1_ffn_gw"],
        "w13": np.stack([columns(i["L1_ffn_w1"], i["L1_ffn_sw1"]), columns(i["L1_ffn_w3"], i["L1_ffn_sw3"])]),
        "b13": np.stack([per_chunk(i["L1_ffn_b1"], i["L1_ffn_sb1"]),
                         per_chunk(i["L1_ffn_b3"], i["L1_ffn_sb3"])], axis=1),
        "w2_1": chunked(i["L1_ffn_w2"], i["L1_ffn_sw2"]),
        "b2_1": np.concatenate([i["L1_ffn_b2"], i["L1_ffn_b2"], i["L1_ffn_sb2"][None]]),
        "bias": cat(i["L0_ffn_lang_b"], i["L0_ffn_router_b"], i["L1_ffn_gb"], i["L1_attn_b_qkv"],
                    i["L1_attn_b_out"]),
        "rope": rope.transpose(1, 0, 2, 3),
        "ident": np.eye(P, dtype=f),
        "iota": np.tile(np.arange(E1, dtype=f), (P, 1)),
        "spread": spread.reshape(P, -1),
    }


def kernel(**inputs):
    import concourse.bacc as bacc
    from concourse.bass_utils import run_bass_kernel_spmd

    nc = bacc.Bacc("TRN2", target_bir_lowering=False, num_devices=1)
    arrays, aps = {}, {}
    for name, v in laid_out({k: np.asarray(v) for k, v in inputs.items()}).items():
        arrays[f"in_{name}"] = np.ascontiguousarray(v)
        aps[name] = nc.dram_tensor(f"in_{name}", v.shape, F32, kind="ExternalInput").ap()
    out = nc.dram_tensor("out", (NB, P, T, D), F32, kind="ExternalOutput").ap()
    transformer_layers(nc, aps, out)
    r = run_bass_kernel_spmd(nc, [arrays], core_ids=[0])
    return r.results[0]["out"].transpose(0, 2, 1, 3).reshape(NB, S, D)
```

```python
from contextlib import ExitStack

import numpy as np

import concourse.bass as bass
from concourse import mybir

F32 = mybir.dt.float32
F32R = mybir.dt.float32r
U32 = mybir.dt.uint32
I32 = mybir.dt.int32
ACT = mybir.ActivationFunctionType
ALU = mybir.AluOpType
AX_X = mybir.AxisListType.X

P = 128
NB, S, D = 16, 256, 128
T = S // P
NQ, NKV, HD = 16, 4, 64
HALF = HD // 2
RANK = 8
LORA_SCALE = 16 / RANK
E0, H0, NLANG = 8, 512, 4
C0 = E0 * H0 // P
NH1, HD1, PAD1 = 16, 8, 32
G1 = NH1 * PAD1 // P
E1, H1 = 32, 64
C1 = E1 * H1 // P + 1
GROUPS, TOPG, TOPK1 = 8, 4, 4
NQKV0 = (NQ + 2 * NKV) * HD
LN_EPS = 1e-5
THETA = 10000.0

QKV_ORDER = [(0, 2), (1, 2), (0, 0), (1, 0), (0, 1), (1, 1)]

B_ROUTE0, B_GATE1, B_QKV1, B_OUT1 = 0, 12, 44, 428
B_ALL = B_OUT1 + D


class Chain:

    def __init__(self, eng, sem):
        self.eng, self.sem, self.n = eng, sem, 0

    def link(self, ins):
        self.n += 1
        ins.then_inc(self.sem, 1)
        self.eng.wait_ge(self.sem, self.n)


def transformer_layers(nc, a, out):
    with ExitStack() as ctx:
        def sb(name, shape, dt=F32):
            return ctx.enter_context(nc.sbuf_tensor(name, shape, dt))

        wqkv0_h, wqkv0_l = sb("wqkv0_h", [P, NQKV0], F32R), sb("wqkv0_l", [P, NQKV0], F32R)
        wo0 = sb("wo0", [P, NQ // 2, D])
        w1_0h, w1_0l = sb("w1_0h", [P, C0 * P], F32R), sb("w1_0l", [P, C0 * P], F32R)
        w2_0 = sb("w2_0", [P, C0, D])
        b1_0 = sb("b1_0", [P, C0])
        wroute0 = sb("wroute0", [P, NLANG + E0])
        wqkv1_h, wqkv1_l = sb("wqkv1_h", [P, 3 * D], F32R), sb("wqkv1_l", [P, 3 * D], F32R)
        wo1 = sb("wo1", [P, G1, D])
        w13_h, w13_l = sb("w13_h", [P, 2, C1 * P], F32R), sb("w13_l", [P, 2, C1 * P], F32R)
        w2_1 = sb("w2_1", [P, C1, D])
        b13 = sb("b13", [P, 2, C1])
        wgate1 = sb("wgate1", [P, E1])
        b2_0, b2_1 = sb("b2_0", [P, D]), sb("b2_1", [P, D])
        bias = sb("bias", [P, B_ALL])
        rope = sb("rope", [P, T, 4, HALF])
        ident = sb("ident", [P, P])
        iota = sb("iota", [P, E1])

        x_in = sb("x_in", [P, T, D])
        xres_x, xres_y = sb("xres_x", [P, T, D]), sb("xres_y", [P, T, D])
        y_out = sb("y_out", [P, T, D])
        stats, mv, rstd = sb("stats", [P, T, 6]), sb("mv", [P, T, 2]), sb("rstd", [P, T])
        var, newton = sb("var", [P, T]), sb("newton", [P, T])
        xn = sb("xn", [P, 2, T, D])
        xT = sb("xT", [P, S])
        xT_h, xT_l = sb("xT_h", [P, 3, S], F32R), sb("xT_l", [P, 3, S], F32R)
        q_stk = sb("q_stk", [P, T, NQ, 2 * HD])
        k_stk = sb("k_stk", [P, T, NKV, 2, 2 * HD])
        v0 = sb("v0", [P, T, NKV, HD])
        qT = sb("qT", [P, NQ, S], F32R)
        kT = sb("kT", [P, NKV, 2, S], F32R)
        nmax = sb("nmax", [P, 4, T])
        psums = sb("psums", [P, 4, T])
        rsums = sb("rsums", [P, 4, T])
        prob = sb("prob", [P, 3, T, S])
        probT = sb("probT", [P, 3, 2, S])
        hT = sb("hT", [P, 8, S])
        aT = hT
        gate_z = sb("gate_z", [P, T, E1])
        gate_s = sb("gate_s", [P, 8, T])
        top8 = sb("top8", [P, 2, T, 8])
        topi = sb("topi", [P, 2, T, 8], U32)
        topf = sb("topf", [P, 2, T, 8])
        cw0, cw1 = sb("cw0", [P, T, P]), sb("cw1", [P, T, P])
        qkv1 = sb("qkv1", [P, T, 3 * D + PAD1 - HD1])
        gate_t = q_stk[:, :, :, :].rearrange("p t h d -> p (t h d)")[:, 0:12 * T * E1]            .rearrange("p (k t n) -> p k t n", k=12, t=T)
        cwT = sb("cwT", [P, S], F32R)
        ra, rb, ro = (prob[:, n, :, :].rearrange("p t s -> p (t s)") for n in range(3))
        spread = qT[:, :, :].rearrange("p h s -> p (h s)")[:, 0:(C1 - 1) * P]
        k_flat = k_stk[:, :, :, :, :].rearrange("p t h a c -> p (t h a c)")
        q_stk1 = k_flat[:, 0:T * NH1 * PAD1].rearrange("p (t h c) -> p t h c", t=T, h=NH1)
        k_stk1 = k_flat[:, T * NH1 * PAD1:].rearrange("p (t h c) -> p t h c", t=T, h=NH1)
        t_flat = probT[:, :, :, :].rearrange("p n k s -> p (n k s)")
        silu = t_flat[:, 0:512].rearrange("p (k s) -> p k s", k=2)
        gated = t_flat[:, 512:1536].rearrange("p (n j s) -> p n j s", n=2, j=2)

        lora_a = probT[0:RANK].rearrange("p c k s -> p (c k s)")[:, 0:3 * D + NQ * HD]
        lora_b = k_flat[0:RANK, 0:NQKV0 + D]
        stage = q_stk[:, :, :, :].rearrange("p t h d -> p (t h d)")
        stage3 = prob[:, :, :, :].rearrange("p c t s -> p (c t s)")

        bank = [ctx.enter_context(nc.psum_tensor(f"bank{i}", [P, 512], F32)) for i in range(8)]

        w_loaded = ctx.enter_context(nc.semaphore("w_loaded"))
        wqkv0_loaded = ctx.enter_context(nc.semaphore("wqkv0_loaded"))
        stage_loaded = ctx.enter_context(nc.semaphore("stage_loaded"))
        stage_split = ctx.enter_context(nc.semaphore("stage_split"))
        zeroed = ctx.enter_context(nc.semaphore("zeroed"))
        lora_ready = ctx.enter_context(nc.semaphore("lora_ready"))
        lora_used = ctx.enter_context(nc.semaphore("lora_used"))
        setup_dve = ctx.enter_context(nc.semaphore("setup_dve"))
        y_stored = ctx.enter_context(nc.semaphore("y_stored"))
        spread_loaded = ctx.enter_context(nc.semaphore("spread_loaded"))

        sems = []

        def signal(name):
            sems.append(ctx.enter_context(nc.semaphore(name)))
            return sems[-1]

        x_loaded = signal("x_loaded")
        x_taken = signal("x_taken")
        y_free = signal("y_free")
        y_ready = signal("y_ready")
        dve_own = signal("dve_own")
        normed = [signal(f"normed{s}") for s in range(4)]
        xT_psum = [signal(f"xT_psum{s}") for s in range(4)]
        xT_ready = [signal(f"xT_ready{s}") for s in range(4)]
        qkv0_psum = signal("qkv0_psum")
        rotating = signal("rotating")
        rotated_half = signal("rotated_half")
        rotated = signal("rotated")
        v0_ready = signal("v0_ready")
        high_ready = signal("high_ready")
        stacked0 = signal("stacked0")
        qkv1_psum = signal("qkv1_psum")
        qkv1_ready = signal("qkv1_ready")
        stacked1 = signal("stacked1")
        turned = signal("turned")
        turned_out = signal("turned_out")
        scores_psum = signal("scores_psum")
        max_ready = signal("max_ready")
        exp_ready = signal("exp_ready")
        rsum_ready = signal("rsum_ready")
        prob_ready = signal("prob_ready")
        probT_psum = signal("probT_psum")
        probT_ready = signal("probT_ready")
        heads_done = signal("heads_done")
        aT0_ready = signal("aT0_ready")
        aT1_ready = signal("aT1_ready")
        attn0_psum = signal("attn0_psum")
        attn1_psum = signal("attn1_psum")
        handed = signal("handed")
        logits0_psum = signal("logits0_psum")
        logits1_psum = signal("logits1_psum")
        route_in0 = signal("route_in0")
        route_exp = signal("route_exp")
        route_in1 = signal("route_in1")
        route_exp1 = signal("route_exp1")
        cw0_ready = signal("cw0_ready")
        cw1_ready = signal("cw1_ready")
        cwT0_psum = signal("cwT0_psum")
        cwT1_psum = signal("cwT1_psum")
        cwT0_ready = signal("cwT0_ready")
        cwT1_ready = signal("cwT1_ready")
        hid0_psum = signal("hid0_psum")
        hid0_ready = signal("hid0_ready")
        exp_out = signal("exp_out")
        exp_added = signal("exp_added")
        up1_psum = signal("up1_psum")
        spread_psum = signal("spread_psum")
        silu_ready = signal("silu_ready")
        gated_ready = signal("gated_ready")
        hid1_ready = signal("hid1_ready")
        down1_done = signal("down1_done")

        loads = [(lora_a, a["lora_a"]), (lora_b, a["lora_b"])] + [(dst[:], a[name]) for dst, name in (
            (wroute0, "wroute0"), (wgate1, "wgate1"), (b1_0, "b1_0"), (b13, "b13"), (w2_0, "w2_0"),
            (w2_1, "w2_1"), (wo1, "wo1"), (rope, "rope"), (ident, "ident"), (iota, "iota"))]
        n_loads = len(loads) + 5
        splits = [(w1_0h[:, :], w1_0l[:, :], a["w1_0"], stage),
                  (w13_h[:, 0, :], w13_l[:, 0, :], a["w13"][0], stage),
                  (w13_h[:, 1, :], w13_l[:, 1, :], a["w13"][1], stage),
                  (wqkv1_h[:, :], wqkv1_l[:, :], a["wqkv1"], stage)]

        with nc.Block(no_gpsimd_drain=True) as block:
            @block.sync
            def _(sp):
                sp.dma_start(stage3[:, 0:NQKV0], a["wqkv0"]).then_inc(wqkv0_loaded, 16)
                for n, (_, _, src, st) in enumerate(splits):
                    if n >= 1:
                        sp.wait_ge(stage_split, n)
                    sp.dma_start(st[:, 0:src.shape[1]], src).then_inc(stage_loaded, 16)

            @block.scalar
            def _(act):
                for dst, src in loads:
                    act.dma_start(dst, src).then_inc(w_loaded, 16)
                act.dma_start(x_in[:, :, :], a["x"][0]).then_inc(w_loaded, 16)
                act.dma_start(bias[:, :], a["bias"].partition_broadcast(P)).then_inc(w_loaded, 16)
                act.dma_start(wo0[:, :, :], a["wo0"]).then_inc(w_loaded, 16)
                act.wait_ge(zeroed, 5)
                act.dma_start(b2_0[0:E0, :], a["b2_0"]).then_inc(w_loaded, 16)
                act.dma_start(b2_1[0:2 * E1 + 1, :], a["b2_1"]).then_inc(w_loaded, 16)
                act.wait_ge(w_loaded, 16 * n_loads)

            @block.gpsimd
            def _(pool):
                pool.memset(b2_0[:, :], 0.0).then_inc(zeroed, 1)
                pool.memset(b2_1[:, :], 0.0).then_inc(zeroed, 1)
                pool.memset(cw0[:, :, :], 0.0).then_inc(zeroed, 1)
                pool.memset(cw1[:, :, :], 0.0).then_inc(zeroed, 1)
                pool.memset(qkv1[:, :, 3 * D:], 0.0).then_inc(zeroed, 1)

            @block.tensor
            def _(pe):
                pe.wait_ge(w_loaded, 16 * n_loads)
                for j in range(3):
                    c = 512 * j
                    if j < 2:
                        mm = pe.matmul(bank[j][:, :], lora_a[:, 0:D], lora_b[:, c:c + 512], start=True, stop=True)
                    else:
                        pe.matmul(bank[2][:, 0:256], lora_a[:, D:2 * D], lora_b[:, c:c + 256], start=True, stop=True)
                        mm = pe.matmul(bank[2][:, 256:512], lora_a[:, 2 * D:3 * D], lora_b[:, c + 256:c + 512],
                                       start=True, stop=True)
                    mm.then_inc(lora_ready, 1)
                for j in range(NQ // 2):
                    c = 3 * D + j * P
                    mm = pe.matmul(bank[3 + j // 4][:, (j % 4) * D:(j % 4 + 1) * D], lora_a[:, c:c + P],
                                   lora_b[:, NQKV0:NQKV0 + D], start=True, stop=True)
                mm.then_inc(lora_ready, 1)

            @block.vector
            def _(dve):
                own = Chain(dve, setup_dve)
                dve.wait_ge(wqkv0_loaded, 16)
                wq = stage3[:, 0:NQKV0]
                for j in range(3):
                    dve.wait_ge(lora_ready, j + 1)
                    c = slice(512 * j, 512 * (j + 1))
                    own.link(dve.scalar_tensor_tensor(out=wq[:, c], in0=bank[j][:, :], scalar=LORA_SCALE,
                                                      in1=wq[:, c], op0=ALU.mult, op1=ALU.add))
                own.link(dve.tensor_copy(wqkv0_h[:, :], wq))
                own.link(dve.tensor_tensor(wqkv0_l[:, :], wq, wqkv0_h[:, :].bitcast(F32), ALU.subtract))
                dve.wait_ge(lora_ready, 4)
                dve.wait_ge(w_loaded, 16 * n_loads)
                for j in range(2):
                    w = wo0[:, 4 * j:4 * j + 4, :].rearrange("p c d -> p (c d)")
                    own.link(dve.scalar_tensor_tensor(out=w, in0=bank[3 + j][:, :], scalar=LORA_SCALE,
                                                      in1=w, op0=ALU.mult, op1=ALU.add))
                for n, (high, low, src, st) in enumerate(splits):
                    dve.wait_ge(stage_loaded, 16 * (n + 1))
                    raw = st[:, 0:src.shape[1]]
                    own.link(dve.tensor_copy(high, raw))
                    if low is not None:
                        own.link(dve.tensor_tensor(low, raw, high.bitcast(F32), ALU.subtract))
                    dve.sem_inc(stage_split, 1)
                dve.wait_ge(zeroed, 5)
                own.link(dve.memset(cw1[:, :, 2 * E1:2 * E1 + 1], 1.0))
        nc.sync.sem_inc(y_stored, 16)

        def one_turn(x_on, y_on, q_on, x_next=None, y_of=None):

            def h_base(layer):
                return NQ if layer == 1 and x_on else 0

            turned_base = 8 + 4 if x_on else 0

            with nc.Block(no_gpsimd_drain=True) as block:
                @block.sync
                def _(sp):
                    if x_on:
                        sp.wait_ge(x_taken, 1)
                        sp.dma_start(x_in[:, :, :], a["x"][bass.ds(sp.snap(x_next), 1)].rearrange("a p t d -> p (a t) d"))\
                            .then_inc(x_loaded, 16)
                    if y_on:
                        sp.wait_ge(y_stored, y_of * 16 + 16)
                        sp.sem_inc(y_free, 1)
                        sp.wait_ge(y_ready, 1)
                        sp.dma_start(out[bass.ds(sp.snap(y_of), 1)].rearrange("a p t d -> p (a t) d"), y_out[:, :, :])\
                            .then_inc(y_stored, 16)
                    if x_on:
                        sp.wait_ge(x_loaded, 16)

                @block.tensor
                def _(pe):
                    def turn_xn(s, dst):
                        for t in range(T):
                            pe.wait_ge(normed[s], t + 1)
                            tr = pe.transpose(dst[:, t * P:(t + 1) * P], xn[:, s % 2, t, :], ident[:, :])
                        tr.then_inc(xT_psum[s], 1)

                    def three(dst, lh, ll, rh, rl):
                        pe.matmul(dst, lh, rl, start=True, stop=False)
                        pe.matmul(dst, ll, rh, start=False, stop=False)
                        return pe.matmul(dst, lh, rh, start=False, stop=True)

                    def heads(layer, scores, outputs, extra):
                        h0 = h_base(layer)
                        for i in range(NQ + 3):
                            extra(i)
                            if i < NQ:
                                if h0 + i >= 2:
                                    pe.wait_ge(exp_ready, 2 * (h0 + i - 1))
                                scores(i, bank[i % 2]).then_inc(scores_psum, 1)
                            if 2 <= i < NQ + 2:
                                h = i - 2
                                pe.wait_ge(prob_ready, 2 * (h0 + h + 1))
                                if h0 + h >= 2:
                                    pe.wait_ge(probT_ready, h0 + h - 1)
                                for t in range(T):
                                    for k in range(2):
                                        c = k * S + t * P
                                        tr = pe.transpose(bank[2 + h % 2][:, c:c + P],
                                                          prob[:, (h0 + h) % 3, t, k * P:(k + 1) * P], ident[:, :])
                                tr.then_inc(probT_psum, 1)
                            if i >= 3:
                                h = i - 3
                                pe.wait_ge(probT_ready, h0 + h + 1)
                                outputs(h, (h0 + h) % 3).then_inc(heads_done, 1)

                    def fill(n, blocks):
                        if n >= 2:
                            pe.wait_ge(turned_out, n - 1)
                        for j, block_in in enumerate(blocks):
                            tr = pe.transpose(bank[6 + n % 2][:, j * P:(j + 1) * P], block_in, ident[:, :])
                        tr.then_inc(turned, 1)

                    def fill_k0(kv):
                        fill(kv, [k_stk[:, t, kv, part, :] for part in range(2) for t in range(T)])

                    def fill_q0(pair):
                        fill(4 + pair, [q_stk[:, t, 2 * pair + j, :] for j in range(2) for t in range(T)])

                    def fill_1(n):
                        stk, g = (k_stk1, q_stk1)[n // 2], n % 2 * 2
                        pe.wait_ge(stacked1, T)
                        fill(turned_base + n, [stk[:, t, 4 * (g + j):4 * (g + j) + 4, :].rearrange("p h c -> p (h c)")
                                               for j in range(2) for t in range(T)])

                    def extra0(i):
                        if i == 0:
                            fill_q0(0)
                        if i % 2 == 0 and i < NQ - 2:
                            fill_q0(i // 2 + 1)
                        if y_on and i >= NQ - 1:
                            fill_1(i - NQ + 1)

                    def scores0(h, dst):
                        pe.wait_ge(turned_out, 4 + h // 2 + 1)
                        kv = h // (NQ // NKV)
                        for t in range(T):
                            q = qT[:, h, t * P:(t + 1) * P]
                            pe.matmul(dst[:, t * S:(t + 1) * S], q, kT[:, kv, 1, :], start=True, stop=False)
                            mm = pe.matmul(dst[:, t * S:(t + 1) * S], q, kT[:, kv, 0, :], start=False, stop=True)
                        return mm

                    def outputs0(h, slot):
                        dst = bank[4 + h // 2 % 2][HD * (h % 2):HD * (h % 2 + 1), 0:S]
                        if h % 2 == 0 and h >= 4:
                            pe.wait_ge(aT0_ready, h // 2 - 1)
                        for k in range(2):
                            mm = pe.matmul(dst, v0[:, k, h // (NQ // NKV), :], probT[:, slot, k, :],
                                           start=(k == 0), stop=(k == 1))
                        return mm

                    if x_on:
                        for kv in range(NKV):
                            fill_k0(kv)
                        heads(0, scores0, outputs0, extra0)
                        pe.wait_ge(turned_out, turned_base + (4 if y_on else 0))
                        pe.wait_ge(aT0_ready, NQ // 2)
                        for t in range(T):
                            for j in range(NQ // 2):
                                mm = pe.matmul(bank[6][:, t * D:(t + 1) * D], aT[:, j, t * P:(t + 1) * P],
                                               wo0[:, j, :], start=(j == 0), stop=(j == NQ // 2 - 1))
                        mm.then_inc(attn0_psum, 1)
                    elif y_on:
                        for n in range(4):
                            fill_1(n)

                    def scores1(h, dst):
                        pe.wait_ge(turned_out, turned_base + 2 + h // 8 + 1)
                        rows = slice(PAD1 * (h % 4), PAD1 * (h % 4 + 1))
                        for t in range(T):
                            mm = pe.matmul(dst[:, t * S:(t + 1) * S], qT[rows, h // 4, t * P:(t + 1) * P],
                                           kT[rows, h // 8, h // 4 % 2, :], start=True, stop=True)
                        return mm

                    def outputs1(h, slot):
                        g, j = h // 4, h % 4
                        dst = bank[4 + g % 2][PAD1 * j:PAD1 * (j + 1), 0:S]
                        if j == 0 and g >= 2:
                            pe.wait_ge(aT1_ready, g - 1)
                        for k in range(2):
                            mm = pe.matmul(dst, qkv1[:, k, 2 * D + HD1 * h:2 * D + HD1 * h + PAD1], probT[:, slot, k, :],
                                           start=(k == 0), stop=(k == 1), tile_position=(0, PAD1 * j))
                        return mm

                    def router0(i):
                        if i == 4:
                            turn_xn(1, bank[6])
                        if i == 8:
                            pe.wait_ge(xT_ready[1], 1)
                            for t in range(T):
                                mm = pe.matmul(bank[7][:, 12 * t:12 * t + 12], xT[:, t * P:(t + 1) * P],
                                               wroute0[:, :], start=True, stop=True)
                            mm.then_inc(logits0_psum, 1)

                    if y_on:
                        heads(1, scores1, outputs1, router0 if x_on else lambda i: None)
                        pe.wait_ge(aT1_ready, G1)
                        for t in range(T):
                            for g in range(G1):
                                mm = pe.matmul(bank[6][:, t * D:(t + 1) * D], aT[:, g, t * P:(t + 1) * P],
                                               wo1[:, g, :], start=(g == 0), stop=(g == G1 - 1))
                        mm.then_inc(attn1_psum, 1)
                    elif x_on:
                        router0(4)
                        router0(8)

                    def router1(e):
                        if e == 2:
                            turn_xn(3, bank[6])
                        if e == 3:
                            pe.wait_ge(xT_ready[3], 1)
                            for t in range(T):
                                mm = pe.matmul(bank[7][:, E1 * t:E1 * (t + 1)], xT[:, t * P:(t + 1) * P],
                                               wgate1[:, :], start=True, stop=True)
                            mm.then_inc(logits1_psum, 1)

                    def down0(e):
                        pe.wait_ge(hid0_ready, 4 * (e + 1))
                        if e >= 2:
                            pe.wait_ge(exp_added, e - 1)
                        for t in range(T):
                            for c in range(4):
                                mm = pe.matmul(bank[4 + e % 2][:, t * D:(t + 1) * D],
                                               hT[:, (e % 2) * 4 + c, t * P:(t + 1) * P], w2_0[:, 4 * e + c, :],
                                               start=(c == 0), stop=(c == 3))
                        mm.then_inc(exp_out, 1)

                    def turn_cw(cw, ready, psum):
                        pe.wait_ge(ready, 1)
                        for t in range(T):
                            tr = pe.transpose(bank[7][:, t * P:(t + 1) * P], cw[:, t, :], ident[:, :])
                        tr.then_inc(psum, 1)

                    if x_on:
                        for e in range(E0):
                            for f in range(2):
                                n = 2 * e + f
                                if n >= 4:
                                    pe.wait_ge(hid0_ready, 2 * (n - 3))
                                for c in range(2):
                                    w = slice((2 * n + c) * P, (2 * n + c + 1) * P)
                                    mm = three(bank[n % 4][:, c * S:(c + 1) * S], w1_0h[:, w], w1_0l[:, w],
                                               xT_h[:, 0, :], xT_l[:, 0, :])
                                mm.then_inc(hid0_psum, 1)
                            if e >= 1:
                                down0(e - 1)
                            if y_on:
                                router1(e)
                        down0(E0 - 1)
                        turn_cw(cw0, cw0_ready, cwT0_psum)
                        pe.wait_ge(cwT0_ready, 1)
                        for t in range(T):
                            mm = pe.matmul(bank[6][:, t * D:(t + 1) * D], cwT[:, t * P:(t + 1) * P].bitcast(F32),
                                           b2_0[:, :], start=True, stop=True)
                        mm.then_inc(exp_out, 1)
                    elif y_on:
                        router1(2)
                        router1(3)

                    def chunks(n):
                        return [C1 - 1] if n == 0 else [2 * n - 2, 2 * n - 1]

                    def up1(n):
                        if n >= 2:
                            pe.wait_ge(gated_ready, 2 * (n - 2) + 1)
                        for which in range(2):
                            for j, c in enumerate(chunks(n)):
                                w = slice(c * P, (c + 1) * P)
                                mm = three(bank[2 * which + n % 2][:, j * S:(j + 1) * S], w13_h[:, which, w],
                                           w13_l[:, which, w], xT_h[:, 1, :], xT_l[:, 1, :])
                        mm.then_inc(up1_psum, 1)

                    def spread1(n):
                        if n >= 2:
                            pe.wait_ge(hid1_ready, n)
                        for j, c in enumerate(chunks(n)):
                            mm = pe.matmul(bank[4][:, j * S:(j + 1) * S], spread[:, c * P:(c + 1) * P], cwT[:, :],
                                           start=True, stop=True)
                        mm.then_inc(spread_psum, 1)

                    def down1(n):
                        pe.wait_ge(hid1_ready, n + 1)
                        for j, c in enumerate(chunks(n)):
                            for t in range(T):
                                mm = pe.matmul(bank[6][:, t * D:(t + 1) * D],
                                               hT[:, 2 * (n % 4) + j, t * P:(t + 1) * P], w2_1[:, c, :],
                                               start=(n == 0 and t == 0), stop=False, skip_group_check=True)
                        mm.then_inc(down1_done, 1)

                    def beside1(n):
                        if q_on and n == 1:
                            turn_xn(0, bank[5])
                        if q_on and 2 <= n < 8:
                            if n == 2:
                                pe.wait_ge(xT_ready[0], 1)
                            else:
                                pe.wait_ge(rotating, n - 2)
                                pe.wait_ge(v0_ready, min(n - 2, T))
                            t, j = QKV_ORDER[n - 2]
                            tok, c = slice(t * P, (t + 1) * P), slice(512 * j, 512 * (j + 1))
                            three(bank[5][:, :], xT_h[:, 2, tok], xT_l[:, 2, tok], wqkv0_h[:, c], wqkv0_l[:, c])\
                                .then_inc(qkv0_psum, 1)
                        if x_on and n == 3:
                            turn_xn(2, bank[7])
                        if x_on and n in (5, 6):
                            t = n - 5
                            if t == 0:
                                pe.wait_ge(xT_ready[2], 1)
                            else:
                                pe.wait_ge(qkv1_ready, 1)
                            tok = slice(t * P, (t + 1) * P)
                            three(bank[7][:, 0:3 * D], xT_h[:, 0, tok], xT_l[:, 0, tok], wqkv1_h[:, :],
                                  wqkv1_l[:, :]).then_inc(qkv1_psum, 1)

                    if y_on:
                        up1(0)
                        up1(1)
                        turn_cw(cw1, cw1_ready, cwT1_psum)
                        down1(0)
                        pe.wait_ge(cwT1_ready, 1)
                        pe.wait_ge(spread_loaded, y_of * 16 + 16)
                        spread1(1)
                        beside1(1)
                        for n in range(2, 9):
                            up1(n)
                            down1(n - 1)
                            spread1(n)
                            beside1(n)
                        down1(8)
                        for t in range(T):
                            mm = pe.matmul(bank[6][:, t * D:(t + 1) * D], cwT[:, t * P:(t + 1) * P].bitcast(F32),
                                           b2_1[:, :], start=False, stop=(t == T - 1), skip_group_check=True)
                        mm.then_inc(down1_done, 1)
                    else:
                        for n in range(1, 9):
                            beside1(n)

                @block.scalar
                def _(act):
                    def exps(layer, i):
                        h = h_base(layer) + i
                        act.wait_ge(max_ready, h + 1)
                        if h >= 3:
                            act.wait_ge(probT_psum, h - 2)
                        if h >= 4:
                            act.wait_ge(rsum_ready, h - 3)
                        for t in range(T):
                            act.activation(prob[:, h % 3, t, :], bank[i % 2][:, t * S:(t + 1) * S], ACT.Exp,
                                           bias=nmax[:, h % 4, t:t + 1],
                                           accum_out=psums[:, h % 4, t:t + 1]).then_inc(exp_ready, 1)

                    def copy_probT(layer, i):
                        h = h_base(layer) + i
                        act.wait_ge(probT_psum, h + 1)
                        if h >= 3:
                            act.wait_ge(heads_done, h - 2)
                        act.activation(probT[:, h % 3, :, :].rearrange("p k s -> p (k s)"), bank[2 + i % 2][:, :],
                                       ACT.Copy).then_inc(probT_ready, 1)

                    def copy_turned(n, dst):
                        act.wait_ge(turned, n + 1)
                        act.activation(dst.rearrange("p a s -> p (a s)"), bank[6 + n % 2][:, :], ACT.Copy)\
                            .then_inc(turned_out, 1)

                    def copy_turned1(n):
                        g = n % 2 * 2
                        if x_on:
                            act.wait_ge(scores_psum, NQ // 2)
                        copy_turned(turned_base + n, kT[:, n, :, :] if n < 2 else qT[:, g:g + 2, :])

                    if x_on:
                        for n in range(4):
                            copy_turned(n, kT[:, n, :, :])
                        copy_turned(4, qT[:, 0:2, :])
                        for i in range(NQ + 3):
                            if i % 2 == 0 and i < NQ - 2:
                                copy_turned(5 + i // 2, qT[:, i + 2:i + 4, :])
                            if i < NQ:
                                exps(0, i)
                            if 2 <= i < NQ + 2:
                                copy_probT(0, i - 2)
                            if i >= 4 and i % 2 == 0:
                                j = i // 2 - 2
                                act.wait_ge(heads_done, 2 * j + 2)
                                act.activation(aT[:, j, :], bank[4 + j % 2][:, 0:S], ACT.Copy).then_inc(aT0_ready, 1)
                            if y_on and i >= NQ - 1:
                                copy_turned1(i - NQ + 1)
                    elif y_on:
                        for n in range(4):
                            copy_turned1(n)

                    def route_exp0(n):
                        act.wait_ge(route_in0, n + 1)
                        z = gate_z[:, :, 0:(NLANG, E0)[n]]
                        act.activation(z, z, ACT.Exp).then_inc(route_exp, 1)

                    if y_on:
                        for i in range(NQ + 4):
                            if i < NQ:
                                exps(1, i)
                            if 2 <= i < NQ + 2:
                                copy_probT(1, i - 2)
                            if i >= 7 and i % 4 == 3:
                                g = i // 4 - 1
                                act.wait_ge(heads_done, h_base(1) + 4 * g + 4)
                                if x_on and g == 0:
                                    act.wait_ge(attn0_psum, 1)
                                act.activation(aT[:, g, :], bank[4 + g % 2][:, 0:S], ACT.Copy,
                                               scale=float(1 / np.sqrt(D))).then_inc(aT1_ready, 1)
                            if x_on and i in (11, 15):
                                route_exp0((i - 11) // 4)
                    elif x_on:
                        route_exp0(0)
                        route_exp0(1)

                    if x_on:
                        for c in range(C0):
                            act.wait_ge(hid0_psum, c // 2 + 1)
                            if c == 0 and y_on:
                                act.wait_ge(attn1_psum, 1)
                            if c >= 8:
                                act.wait_ge(exp_out, c // 4 - 1)
                            act.activation(hT[:, c % 8, :], bank[c // 2 % 4][:, (c % 2) * S:(c % 2 + 1) * S],
                                           ACT.Gelu, bias=b1_0[:, c:c + 1]).then_inc(hid0_ready, 1)
                            if c == 19 and y_on:
                                act.wait_ge(route_in1, 1)
                                act.activation(gate_z[:, :, :], gate_z[:, :, :], ACT.Exp).then_inc(route_exp1, 1)
                    elif y_on:
                        act.wait_ge(route_in1, 1)
                        act.activation(gate_z[:, :, :], gate_z[:, :, :], ACT.Exp).then_inc(route_exp1, 1)

                    def silus(n):
                        for k in ([0] if n == 0 else [2 * n - 1, 2 * n]):
                            j = 0 if k == 0 else (k + 1) % 2
                            c = C1 - 1 if k == 0 else k - 1
                            act.wait_ge(up1_psum, n + 1)
                            if k >= 2:
                                act.wait_ge(gated_ready, k - 1)
                            act.activation(silu[:, k % 2, :], bank[n % 2][:, j * S:(j + 1) * S], ACT.Silu,
                                           bias=b13[:, 0, c:c + 1]).then_inc(silu_ready, 1)

                    def high_parts(m):
                        t, j = QKV_ORDER[m]
                        if j == 2:
                            act.wait_ge(rotating, m + 1)
                            act.activation(v0[:, t, :, :].rearrange("p h d -> p (h d)"), bank[5][:, 256:512],
                                           ACT.Copy).then_inc(v0_ready, 1)
                        act.wait_ge(rotated, m + 1)
                        if j == 2:
                            for half in range(2):
                                hi = act.activation(k_stk[:, t, :, 0, half * HD:(half + 1) * HD].bitcast(F32R),
                                                    ro[:, 0:NKV * HD].rearrange("p (h d) -> p h d", d=HD), ACT.Copy)
                        else:
                            hi = act.activation(q_stk[:, t, 8 * j:8 * j + 8, 0:HD].bitcast(F32R),
                                                ro[:, :].rearrange("p (h d) -> p h d", d=HD), ACT.Copy)
                        hi.then_inc(high_ready, 1)

                    if y_on:
                        silus(0)
                        silus(1)
                        for n in range(2, 9):
                            silus(n)
                            if q_on and n >= 3:
                                high_parts(n - 3)
                    elif q_on:
                        for m in range(6):
                            high_parts(m)

                @block.gpsimd
                def _(pool):
                    if y_on:
                        pool.tensor_copy(xres_y[:, :, :], xres_x[:, :, :]).then_inc(handed, 1)
                        pool.wait_ge(attn1_psum, 1)
                        pool.dma_start(spread, a["spread"]).then_inc(spread_loaded, 16)
                    if q_on:
                        for m, (t, j) in enumerate(QKV_ORDER):
                            heads = 8 if j < 2 else NKV
                            n = heads * HD
                            xc = ra[:, 0:n].rearrange("p (h a d) -> p h a d", a=2, d=HALF)
                            xs = rb[:, 0:n].rearrange("p (h a d) -> p h a d", a=2, d=HALF)
                            o = ro[:, 0:n].rearrange("p (h a d) -> p h a d", a=2, d=HALF)
                            pool.wait_ge(rotating, m + 1)
                            if m >= 1:
                                pool.wait_ge(stacked0, m)
                            pool.tensor_tensor(o[:, :, 0, :], xc[:, :, 0, :], xs[:, :, 1, :], ALU.subtract)\
                                .then_inc(rotated_half, 1)
                            pool.tensor_tensor(o[:, :, 1, :], xs[:, :, 0, :], xc[:, :, 1, :], ALU.add)\
                                .then_inc(rotated, 1)
                            pool.wait_ge(rotated_half, m + 1)
                            pool.wait_ge(rotated, m + 1)
                            pool.wait_ge(high_ready, m + 1)
                            o = ro[:, 0:n].rearrange("p (h d) -> p h d", d=HD)
                            if j < 2:
                                stk = q_stk[:, t, 8 * j:8 * j + 8, :]
                                lo = pool.tensor_tensor(stk[:, :, HD:2 * HD].bitcast(F32R), o, stk[:, :, 0:HD],
                                                        ALU.subtract)
                            else:
                                for half in range(2):
                                    lo = pool.tensor_tensor(k_stk[:, t, :, 1, half * HD:(half + 1) * HD].bitcast(F32R),
                                                            o, k_stk[:, t, :, 0, 0:HD], ALU.subtract)
                            lo.then_inc(stacked0, 1)

                @block.vector
                def _(dve):
                    own = Chain(dve, dve_own)
                    link = own.link

                    def norm_stats(src):
                        for t in range(T):
                            link(dve.bn_stats(stats[:, t, :], src[:, t, :]))
                        for t in range(T):
                            link(dve.bn_aggr(mv[:, t, :], stats[:, t, :]))
                        link(dve.tensor_scalar(var[:, :], mv[:, :, 1], LN_EPS, None, ALU.add))
                        bits = rstd[:, :].bitcast(I32)
                        link(dve.tensor_scalar(bits, var[:, :].bitcast(I32), 1, None, ALU.logical_shift_right))
                        link(dve.tensor_scalar(bits, bits, -1.0, float(0x5F3759DF), ALU.mult, ALU.add))

                    def norm_newton():
                        for _ in range(3):
                            link(dve.tensor_tensor(newton[:, :], rstd[:, :], rstd[:, :], ALU.mult))
                            link(dve.scalar_tensor_tensor(out=newton[:, :], in0=newton[:, :], scalar=-0.5,
                                                          in1=var[:, :], op0=ALU.mult, op1=ALU.mult))
                            link(dve.scalar_tensor_tensor(out=rstd[:, :], in0=newton[:, :], scalar=1.5,
                                                          in1=rstd[:, :], op0=ALU.add, op1=ALU.mult))

                    def norm_apply(s, src):
                        for t in range(T):
                            dve.tensor_scalar(xn[:, s % 2, t, :], src[:, t, :], mv[:, t, 0:1], rstd[:, t:t + 1],
                                              ALU.subtract, ALU.mult).then_inc(normed[s], 1)

                    def split_xT(s, src, slot, whole):
                        dve.wait_ge(xT_psum[s], 1)
                        if whole:
                            link(dve.tensor_copy(xT[:, :], src[:, 0:S]))
                            src = xT
                        link(dve.tensor_copy(xT_h[:, slot, :], src[:, 0:S]))
                        dve.tensor_tensor(xT_l[:, slot, :], src[:, 0:S], xT_h[:, slot, :].bitcast(F32), ALU.subtract)\
                            .then_inc(xT_ready[s], 1)

                    def softmax_steps(layer, i):
                        if i < NQ:
                            h = h_base(layer) + i
                            dve.wait_ge(scores_psum, h + 1)
                            if h >= 4:
                                dve.wait_ge(exp_ready, 2 * (h - 3))
                            dve.tensor_reduce(nmax[:, h % 4, :], bank[i % 2][:, :].rearrange("p (t s) -> p t s", t=T),
                                              AX_X, ALU.max, negate=True).then_inc(max_ready, 1)
                        if i >= 1:
                            h = h_base(layer) + i - 1
                            dve.wait_ge(exp_ready, 2 * (h + 1))
                            dve.reciprocal(rsums[:, h % 4, :], psums[:, h % 4, :]).then_inc(rsum_ready, 1)
                            dve.wait_ge(rsum_ready, h + 1)
                            for t in range(T):
                                dve.tensor_scalar(prob[:, h % 3, t, :], prob[:, h % 3, t, :],
                                                  rsums[:, h % 4, t:t + 1], None, ALU.mult)\
                                    .then_inc(prob_ready, 1)

                    def stack1(i):
                        if x_on and i == 2:
                            dve.wait_ge(turned, 4)
                        if i < 3 or i >= 11:
                            return
                        part = [slice(HD1 * n, HD1 * (n + 1)) for n in range(4)]
                        t, n = (i - 3) // 4, (i - 3) % 4
                        q = qkv1[:, t, 0:D].rearrange("p (h e) -> p h e", e=HD1)
                        k = qkv1[:, t, D:2 * D].rearrange("p (h e) -> p h e", e=HD1)
                        qs, ks = q_stk1[:, t, :, :], k_stk1[:, t, :, :]
                        if n == 0:
                            for p in (0, 2):
                                link(dve.tensor_copy(qs[:, :, part[p]].bitcast(F32R), q))
                        if n == 1:
                            for p in (1, 3):
                                link(dve.tensor_tensor(qs[:, :, part[p]].bitcast(F32R), q, qs[:, :, part[0]],
                                                       ALU.subtract))
                        if n == 2:
                            for p in (0, 1):
                                link(dve.tensor_copy(ks[:, :, part[p]].bitcast(F32R), k))
                        if n == 3:
                            for p in (2, 3):
                                link(dve.tensor_tensor(ks[:, :, part[p]].bitcast(F32R), k, ks[:, :, part[0]],
                                                       ALU.subtract))
                            dve.sem_inc(stacked1, 1)

                    for i in range(NQ + 1):
                        if x_on:
                            softmax_steps(0, i)
                        if y_on:
                            stack1(i)

                    def g(k, n):
                        return gate_t[:, k, :, 0:n]

                    def sc(k):
                        return gate_s[:, k, :]

                    def wide(v, n):
                        return v.unsqueeze(2).to_broadcast([P, T, n])

                    def softmax_in(z, n):
                        link(dve.tensor_reduce(sc(0), z, AX_X, ALU.max))
                        link(dve.tensor_tensor(gate_z[:, :, 0:n], z, wide(sc(0), n), ALU.subtract))

                    def softmax_out(n, dst):
                        link(dve.tensor_reduce(sc(1), gate_z[:, :, 0:n], AX_X, ALU.add))
                        link(dve.reciprocal(sc(2), sc(1)))
                        link(dve.tensor_tensor(dst, gate_z[:, :, 0:n], wide(sc(2), n), ALU.mult))

                    def top(slot, vals, n):
                        for t in range(T):
                            link(dve.max(out=top8[:, slot, t, :], in_=vals[:, t, :]))
                        for t in range(T):
                            link(dve.max_index(topi[:, slot, t, :], top8[:, slot, t, :], vals[:, t, :]))
                        link(dve.tensor_copy(topf[:, slot, :, :], topi[:, slot, :, :]))

                    def hit(dst, slot, k, n):
                        link(dve.tensor_tensor(dst, iota[:, 0:n].unsqueeze(1).to_broadcast([P, T, n]),
                                               wide(topf[:, slot, :, k], n), ALU.is_equal))

                    def route0(i):
                        if i == 0:
                            dve.wait_ge(attn0_psum, 1)
                            if y_on:
                                dve.wait_ge(handed, 1)
                            link(dve.tensor_tensor(xres_x[:, :, :], bank[6][:, 0:S].rearrange("p (t d) -> p t d", t=T),
                                                   x_in[:, :, :], ALU.add))
                            dve.sem_inc(x_taken, 1)
                        if i == 1:
                            norm_stats(xres_x)
                        if i == 2:
                            norm_newton()
                        if i == 3:
                            norm_apply(1, xres_x)
                        if i == 6:
                            split_xT(1, bank[6], 0, True)
                        if i == 9:
                            dve.wait_ge(logits0_psum, 1)
                            nr = NLANG + E0
                            b_route = bias[:, B_ROUTE0:B_ROUTE0 + nr].unsqueeze(1).to_broadcast([P, T, nr])
                            link(dve.tensor_tensor(g(0, nr), bank[7][:, 0:T * nr].rearrange("p (t n) -> p t n", t=T),
                                                   b_route, ALU.add))
                            softmax_in(g(0, NLANG), NLANG)
                            dve.sem_inc(route_in0, 1)
                        if i == 12:
                            dve.wait_ge(route_exp, 1)
                            softmax_out(NLANG, g(1, NLANG))
                            link(dve.tensor_tensor(g(2, NLANG - 1), g(1, NLANG - 1), gate_t[:, 1, :, 1:NLANG], ALU.add))
                            link(dve.tensor_copy(gate_t[:, 2, :, NLANG - 1:NLANG], gate_t[:, 1, :, NLANG - 1:NLANG]))
                        if i == 13:
                            for r in range(E0 // NLANG):
                                link(dve.scalar_tensor_tensor(out=gate_t[:, 3, :, r * NLANG:(r + 1) * NLANG],
                                                              in0=g(2, NLANG), scalar=0.1,
                                                              in1=gate_t[:, 0, :, (r + 1) * NLANG:(r + 2) * NLANG],
                                                              op0=ALU.mult, op1=ALU.add))
                            softmax_in(g(3, E0), E0)
                            dve.sem_inc(route_in0, 1)
                        if i == 16:
                            dve.wait_ge(route_exp, 2)
                            softmax_out(E0, g(4, E0))
                            top(0, g(4, E0), E0)
                            link(dve.tensor_tensor(sc(3), top8[:, 0, :, 0], top8[:, 0, :, 1], ALU.add))
                            link(dve.reciprocal(sc(4), sc(3)))
                            for k in range(2):
                                link(dve.tensor_tensor(sc(5 + k), top8[:, 0, :, k], sc(4), ALU.mult))
                                hit(g(5 + k, E0), 0, k, E0)
                                link(dve.tensor_tensor(g(7 + k, E0), g(5 + k, E0), wide(sc(5 + k), E0), ALU.mult))
                            link(dve.tensor_tensor(cw0[:, :, 0:E0], g(7, E0), g(8, E0), ALU.add))
                            dve.sem_inc(cw0_ready, 1)

                    for i in range(NQ + 1):
                        if y_on:
                            softmax_steps(1, i)
                        if x_on:
                            route0(i)

                    def gate1(e):
                        if e == 0:
                            dve.wait_ge(attn1_psum, 1)
                            dve.wait_ge(handed, 1)
                            link(dve.tensor_tensor(xres_y[:, :, :], bank[6][:, 0:S].rearrange("p (t d) -> p t d", t=T),
                                                   xres_y[:, :, :], ALU.add))
                            link(dve.tensor_tensor(xres_y[:, :, :], xres_y[:, :, :],
                                                   bias[:, B_OUT1:B_OUT1 + D].unsqueeze(1).to_broadcast([P, T, D]),
                                                   ALU.add))
                            norm_stats(xres_y)
                            norm_newton()
                            norm_apply(3, xres_y)
                        if e == 2:
                            split_xT(3, bank[6], 1, True)
                        if e == 3:
                            dve.wait_ge(logits1_psum, 1)
                            link(dve.tensor_tensor(g(0, E1), bank[7][:, 0:T * E1].rearrange("p (t n) -> p t n", t=T),
                                                   bias[:, B_GATE1:B_GATE1 + E1].unsqueeze(1).to_broadcast([P, T, E1]),
                                                   ALU.add))
                            softmax_in(g(0, E1), E1)
                            dve.sem_inc(route_in1, 1)
                        if e == 4:
                            dve.wait_ge(route_exp1, 1)
                            softmax_out(E1, g(1, E1))
                            pairs = gate_t[:, 1, :, :].rearrange("p t (g b) -> p t g b", b=2)
                            hi, lo = g(2, 2 * GROUPS), g(3, 2 * GROUPS)
                            link(dve.tensor_tensor(hi, pairs[:, :, :, 0], pairs[:, :, :, 1], ALU.max))
                            link(dve.tensor_tensor(lo, pairs[:, :, :, 0], pairs[:, :, :, 1], ALU.min))
                            hi2, lo2 = (v.rearrange("p t (g a) -> p t g a", a=2) for v in (hi, lo))
                            link(dve.tensor_tensor(g(4, GROUPS), hi2[:, :, :, 0], hi2[:, :, :, 1], ALU.max))
                            link(dve.tensor_tensor(g(5, GROUPS), hi2[:, :, :, 0], hi2[:, :, :, 1], ALU.min))
                            link(dve.tensor_tensor(g(6, GROUPS), lo2[:, :, :, 0], lo2[:, :, :, 1], ALU.max))
                            link(dve.tensor_tensor(g(7, GROUPS), g(5, GROUPS), g(6, GROUPS), ALU.max))
                            link(dve.tensor_tensor(g(8, GROUPS), g(4, GROUPS), g(7, GROUPS), ALU.add))
                        if e == 5:
                            top(0, g(8, GROUPS), GROUPS)
                            hit(g(9, GROUPS), 0, 0, GROUPS)
                            for k in range(1, TOPG):
                                hit(g(10, GROUPS), 0, k, GROUPS)
                                link(dve.tensor_tensor(g(9, GROUPS), g(9, GROUPS), g(10, GROUPS), ALU.add))
                            link(dve.tensor_scalar(g(10, GROUPS), g(9, GROUPS), -1.0, None, ALU.add))
                        if e == 6:
                            by_group = gate_t[:, 1, :, :].rearrange("p t (g e) -> p t g e", g=GROUPS)
                            kept = gate_t[:, 11, :, :].rearrange("p t (g e) -> p t g e", g=GROUPS)
                            for t in range(T):
                                link(dve.tensor_tensor(kept[:, t], by_group[:, t],
                                                       gate_t[:, 9, t, 0:GROUPS].unsqueeze(2).to_broadcast([P, GROUPS, 4]),
                                                       ALU.mult))
                                link(dve.tensor_tensor(kept[:, t], kept[:, t],
                                                       gate_t[:, 10, t, 0:GROUPS].unsqueeze(2).to_broadcast([P, GROUPS, 4]),
                                                       ALU.add))
                            top(1, g(11, E1), E1)
                        if e == 7:
                            for k in range(TOPK1):
                                hit(g(2, E1), 1, k, E1)
                                dst = g(3 + k % 2, E1)
                                link(dve.tensor_tensor(g(5, E1) if k else dst, g(2, E1), wide(top8[:, 1, :, k], E1),
                                                       ALU.mult))
                                if k:
                                    link(dve.tensor_tensor(dst, g(5, E1), g(3 + (k - 1) % 2, E1), ALU.add))
                            whole = g(3 + (TOPK1 - 1) % 2, E1)
                            link(dve.tensor_copy(cw1[:, :, 0:E1].bitcast(F32R), whole))
                            link(dve.tensor_tensor(cw1[:, :, E1:2 * E1].bitcast(F32R), whole, cw1[:, :, 0:E1],
                                                   ALU.subtract))
                            dve.sem_inc(cw1_ready, 1)

                    def add_expert(e):
                        dve.wait_ge(exp_out, e + 1)
                        for t in range(T):
                            add = dve.scalar_tensor_tensor(
                                out=xres_x[:, t, :], in0=bank[4 + e % 2][:, t * D:(t + 1) * D],
                                scalar=cw0[:, t, e:e + 1], in1=xres_x[:, t, :], op0=ALU.mult, op1=ALU.add)
                            if t < T - 1:
                                link(add)
                        add.then_inc(exp_added, 1)
                        dve.wait_ge(exp_added, e + 1)

                    for e in range(E0):
                        if y_on:
                            gate1(e)
                        if x_on:
                            add_expert(e)
                    if x_on:
                        dve.wait_ge(cwT0_psum, 1)
                        dve.tensor_copy(cwT[:, :], bank[7][:, 0:S]).then_inc(cwT0_ready, 1)
                        dve.wait_ge(exp_out, E0 + 1)
                        dve.tensor_tensor(xres_x[:, :, :], bank[6][:, 0:S].rearrange("p (t d) -> p t d", t=T),
                                          xres_x[:, :, :], ALU.add).then_inc(exp_added, 1)
                        dve.wait_ge(exp_added, E0 + 1)

                    def gate_chunk(k):
                        n, j = (0, 0) if k == 0 else ((k + 1) // 2, (k + 1) % 2)
                        c = C1 - 1 if k == 0 else k - 1
                        dve.wait_ge(silu_ready, k + 1)
                        dst = hT[:, 0, :] if k == 0 else gated[:, n % 2, j, :]
                        dve.scalar_tensor_tensor(out=dst, in0=bank[2 + n % 2][:, j * S:(j + 1) * S],
                                                 scalar=b13[:, 1, c:c + 1], in1=silu[:, k % 2, :],
                                                 op0=ALU.add, op1=ALU.mult).then_inc(gated_ready, 1)
                        if k == 0:
                            dve.wait_ge(gated_ready, 1)
                            dve.sem_inc(hid1_ready, 1)

                    def weigh(n):
                        dve.wait_ge(spread_psum, n)
                        dve.wait_ge(gated_ready, 2 * n + 1)
                        if n >= 4:
                            dve.wait_ge(down1_done, n - 3)
                        dve.tensor_tensor(hT[:, 2 * (n % 4):2 * (n % 4) + 2, :], gated[:, n % 2, :, :],
                                          bank[4][:, :].rearrange("p (c s) -> p c s", c=2), ALU.mult)\
                            .then_inc(hid1_ready, 1)

                    def beside1(n):
                        if q_on and n == 0:
                            if x_on:
                                dve.wait_ge(x_loaded, 16)
                            norm_stats(x_in)
                            norm_newton()
                            norm_apply(0, x_in)
                        if x_on and n == 1:
                            norm_stats(xres_x)
                            norm_newton()
                            norm_apply(2, xres_x) if not q_on else None
                        if q_on and n == 1:
                            split_xT(0, bank[5], 2, False)
                            if x_on:
                                norm_apply(2, xres_x)
                        if q_on and 2 <= n < 8:
                            m = n - 2
                            t, j = QKV_ORDER[m]
                            heads = 8 if j < 2 else NKV
                            w = heads * HD
                            dve.wait_ge(qkv0_psum, m + 1)
                            if m >= 1:
                                dve.wait_ge(rotated, m)
                                dve.wait_ge(rotated_half, m)
                            for k, dst in ((0, ra), (1, rb)):
                                table = rope[:, t, k + (0 if j < 2 else 2), :].unsqueeze(1)\
                                    .to_broadcast([P, 2 * heads, HALF])
                                ins = dve.tensor_tensor(dst[:, 0:w].rearrange("p (h d) -> p h d", d=HALF),
                                                        bank[5][:, 0:w].rearrange("p (h d) -> p h d", d=HALF),
                                                        table, ALU.mult)
                                if k == 0:
                                    link(ins)
                            ins.then_inc(rotating, 1)
                        if x_on and n == 3:
                            split_xT(2, bank[7], 0, False)
                        if x_on and n in (5, 6):
                            t = n - 5
                            dve.wait_ge(qkv1_psum, t + 1)
                            dve.tensor_tensor(qkv1[:, t, 0:3 * D], bank[7][:, 0:3 * D], bias[:, B_QKV1:B_QKV1 + 3 * D],
                                              ALU.add).then_inc(qkv1_ready, 1)

                    if y_on:
                        gate_chunk(0)
                        dve.wait_ge(cwT1_psum, 1)
                        dve.tensor_copy(cwT[:, :], bank[7][:, 0:S]).then_inc(cwT1_ready, 1)
                    beside1(0)
                    for n in range(1, 9):
                        if y_on:
                            gate_chunk(2 * n - 1)
                            gate_chunk(2 * n)
                            weigh(n)
                        beside1(n)
                    if y_on:
                        dve.wait_ge(y_free, 1)
                        dve.wait_ge(down1_done, 10)
                        dve.tensor_tensor(y_out[:, :, :], bank[6][:, 0:S].rearrange("p (t d) -> p t d", t=T),
                                          xres_y[:, :, :], ALU.add).then_inc(y_ready, 1)

            nc.all_engine_barrier(sems_to_clear=range(sems[0].num, sems[-1].num + 1))

        one_turn(x_on=False, y_on=False, q_on=True)
        one_turn(x_on=True, y_on=False, q_on=True, x_next=1)
        with nc.Fori(1, NB) as b:
            one_turn(x_on=True, y_on=True, q_on=True, x_next=(b + 1) % NB, y_of=b - 1)
        one_turn(x_on=False, y_on=True, q_on=False, y_of=NB - 1)
        nc.sync.wait_ge(y_stored, 16 * (NB + 1))


def laid_out(i):
    f = np.float32

    def halves(w):
        h = w.shape[0] // HD
        return w.reshape(h, HALF, 2, -1).transpose(0, 2, 1, 3).reshape(w.shape)

    def cat(*xs):
        return np.ascontiguousarray(np.concatenate(xs, axis=-1))

    inv_freq = (f(1.0) / f(THETA) ** (np.arange(0, HD, 2, dtype=f) / f(HD))).astype(f)
    ang = np.arange(S, dtype=f)[:, None] * inv_freq[None, :]
    cos, sin = np.cos(ang).astype(f), np.sin(ang).astype(f)
    scale = f(1 / np.sqrt(HD))
    rope = np.stack([cos * scale, sin * scale, cos, sin], axis=1).reshape(T, P, 4, HALF)
    spread = np.zeros((P, C1 - 1, 2, H1), f)
    for e in range(E1):
        spread[e, e // 2, e % 2] = 1
        spread[E1 + e, e // 2, e % 2] = 1
    wo1 = np.zeros((G1, 4, PAD1, D), f)
    wo1[:, :, 0:HD1] = i["L1_attn_W_out"].reshape(G1, 4, HD1, D)

    def columns(w, sw):
        return cat(w.transpose(1, 0, 2).reshape(D, E1 * H1), sw)

    def chunked(w, sw):
        return np.concatenate([w.reshape(-1, D), sw]).reshape(-1, P, D).transpose(1, 0, 2)

    def per_chunk(b, sb):
        return np.concatenate([b.reshape(-1), sb]).reshape(-1, P).T

    return {
        "x": i["L0_attn_x"].reshape(NB, T, P, D).transpose(0, 2, 1, 3),
        "wqkv0": cat(halves(i["L0_attn_Wq"]).T, halves(i["L0_attn_Wk"]).T, i["L0_attn_Wv"].T),
        "lora_a": cat(i["L0_attn_qA"], i["L0_attn_kA"], i["L0_attn_vA"], i["L0_attn_oA"]),
        "lora_b": cat(halves(i["L0_attn_qB"]).T, halves(i["L0_attn_kB"]).T, i["L0_attn_vB"].T,
                      i["L0_attn_oB"].T),
        "wo0": i["L0_attn_Wo"].T.reshape(NQ // 2, P, D).transpose(1, 0, 2),
        "wroute0": cat(i["L0_ffn_lang_w"].T, i["L0_ffn_router_w"].T),
        "w1_0": i["L0_ffn_w1"].transpose(1, 0, 2).reshape(D, E0 * H0),
        "b1_0": i["L0_ffn_b1"].reshape(C0, P).T,
        "w2_0": i["L0_ffn_w2"].reshape(C0, P, D).transpose(1, 0, 2),
        "b2_0": i["L0_ffn_b2"],
        "wqkv1": i["L1_attn_W_qkv"],
        "wo1": wo1.reshape(G1, P, D).transpose(1, 0, 2),
        "wgate1": i["L1_ffn_gw"],
        "w13": np.stack([columns(i["L1_ffn_w1"], i["L1_ffn_sw1"]), columns(i["L1_ffn_w3"], i["L1_ffn_sw3"])]),
        "b13": np.stack([per_chunk(i["L1_ffn_b1"], i["L1_ffn_sb1"]),
                         per_chunk(i["L1_ffn_b3"], i["L1_ffn_sb3"])], axis=1),
        "w2_1": chunked(i["L1_ffn_w2"], i["L1_ffn_sw2"]),
        "b2_1": np.concatenate([i["L1_ffn_b2"], i["L1_ffn_b2"], i["L1_ffn_sb2"][None]]),
        "bias": cat(i["L0_ffn_lang_b"], i["L0_ffn_router_b"], i["L1_ffn_gb"], i["L1_attn_b_qkv"],
                    i["L1_attn_b_out"]),
        "rope": rope.transpose(1, 0, 2, 3),
        "ident": np.eye(P, dtype=f),
        "iota": np.tile(np.arange(E1, dtype=f), (P, 1)),
        "spread": spread.reshape(P, -1),
    }


def kernel(**inputs):
    import concourse.bacc as bacc
    from concourse.bass_utils import run_bass_kernel_spmd

    nc = bacc.Bacc("TRN2", target_bir_lowering=False, num_devices=1)
    arrays, aps = {}, {}
    for name, v in laid_out({k: np.asarray(v) for k, v in inputs.items()}).items():
        arrays[f"in_{name}"] = np.ascontiguousarray(v)
        aps[name] = nc.dram_tensor(f"in_{name}", v.shape, F32, kind="ExternalInput").ap()
    out = nc.dram_tensor("out", (NB, P, T, D), F32, kind="ExternalOutput").ap()
    transformer_layers(nc, aps, out)
    r = run_bass_kernel_spmd(nc, [arrays], core_ids=[0])
    return r.results[0]["out"].transpose(0, 2, 1, 3).reshape(NB, S, D)
```

```python
from contextlib import ExitStack

import numpy as np

import concourse.bass as bass
from concourse import mybir

F32 = mybir.dt.float32
F32R = mybir.dt.float32r
U32 = mybir.dt.uint32
I32 = mybir.dt.int32
ACT = mybir.ActivationFunctionType
ALU = mybir.AluOpType
AX_X = mybir.AxisListType.X

P = 128
NB, S, D = 16, 256, 128
T = S // P
NQ, NKV, HD = 16, 4, 64
HALF = HD // 2
RANK = 8
LORA_SCALE = 16 / RANK
E0, H0, NLANG = 8, 512, 4
C0 = E0 * H0 // P
NH1, HD1, PAD1 = 16, 8, 32
G1 = NH1 * PAD1 // P
E1, H1 = 32, 64
C1 = E1 * H1 // P + 1
GROUPS, TOPG, TOPK1 = 8, 4, 4
NQKV0 = (NQ + 2 * NKV) * HD
LN_EPS = 1e-5
THETA = 10000.0

FILLS0, FILLS1 = [0, 1, 3, 4, 6, 7, 9], [11, 13, 15, 17]

QKV_ORDER = [(0, 2), (1, 2), (0, 0), (1, 0), (0, 1), (1, 1)]

B_ROUTE0, B_GATE1, B_QKV1, B_OUT1 = 0, 12, 44, 428
B_ALL = B_OUT1 + D


class Chain:

    def __init__(self, eng, sem):
        self.eng, self.sem, self.n = eng, sem, 0

    def step(self, ins):
        self.n += 1
        ins.then_inc(self.sem, 1)

    def settle(self, n):
        self.eng.wait_ge(self.sem, n)

    def link(self, ins):
        self.n += 1
        ins.then_inc(self.sem, 1)
        self.eng.wait_ge(self.sem, self.n)


def transformer_layers(nc, a, out):
    with ExitStack() as ctx:
        def sb(name, shape, dt=F32):
            return ctx.enter_context(nc.sbuf_tensor(name, shape, dt))

        wqkv0_h, wqkv0_l = sb("wqkv0_h", [P, NQKV0], F32R), sb("wqkv0_l", [P, NQKV0], F32R)
        wo0 = sb("wo0", [P, NQ // 2, D])
        w1_0h, w1_0l = sb("w1_0h", [P, C0 * P], F32R), sb("w1_0l", [P, C0 * P], F32R)
        w2_0 = sb("w2_0", [P, C0, D])
        b1_0 = sb("b1_0", [P, C0])
        wroute0 = sb("wroute0", [P, NLANG + E0])
        wqkv1_h, wqkv1_l = sb("wqkv1_h", [P, 3 * D], F32R), sb("wqkv1_l", [P, 3 * D], F32R)
        wo1 = sb("wo1", [P, G1, D])
        w13_h, w13_l = sb("w13_h", [P, 2, C1 * P], F32R), sb("w13_l", [P, 2, C1 * P], F32R)
        w2_1 = sb("w2_1", [P, C1, D])
        b13 = sb("b13", [P, 2, C1])
        wgate1 = sb("wgate1", [P, E1])
        b2_0, b2_1 = sb("b2_0", [P, D]), sb("b2_1", [P, D])
        bias = sb("bias", [P, B_ALL])
        rope = sb("rope", [P, T, 4, HALF])
        ident = sb("ident", [P, P])
        iota = sb("iota", [P, E1])

        x_in = sb("x_in", [P, T, D])
        xres_x, xres_y = sb("xres_x", [P, T, D]), sb("xres_y", [P, T, D])
        stats, mv, rstd = sb("stats", [P, T, 6]), sb("mv", [P, T, 2]), sb("rstd", [P, T])
        var, newton = sb("var", [P, T]), sb("newton", [P, T])
        xn = sb("xn", [P, T, D])
        xT = sb("xT", [P, S])
        xT_h, xT_l = sb("xT_h", [P, 3, S], F32R), sb("xT_l", [P, 3, S], F32R)
        q_stk = sb("q_stk", [P, T, NQ, 2 * HD])
        k_stk = sb("k_stk", [P, T, NKV, 2, 2 * HD])
        v0 = sb("v0", [P, T, NKV, HD])
        qT = sb("qT", [P, NQ, S], F32R)
        kT = sb("kT", [P, NKV, 2, S], F32R)
        nmax = sb("nmax", [P, 4, T])
        psums = sb("psums", [P, 4, T])
        rsums = sb("rsums", [P, 4, T])
        prob = sb("prob", [P, 4, T, S])
        probT = sb("probT", [P, 3, 2, S])
        hT = sb("hT", [P, 8, S])
        aT = hT
        gate_z = sb("gate_z", [P, T, E1])
        gate_s = sb("gate_s", [P, 8, T])
        top8 = sb("top8", [P, 2, T, 8])
        topi = sb("topi", [P, 2, T, 8], U32)
        topf = sb("topf", [P, 2, T, 8])
        cw0, cw1 = sb("cw0", [P, T, P]), sb("cw1", [P, T, P])
        qkv1 = sb("qkv1", [P, T, 3 * D + PAD1 - HD1])
        gate_t = q_stk[:, :, :, :].rearrange("p t h d -> p (t h d)")[:, 0:12 * T * E1]            .rearrange("p (k t n) -> p k t n", k=12, t=T)
        cwT = sb("cwT", [P, S], F32R)
        ra, rb, *ro = (prob[:, n, :, :].rearrange("p t s -> p (t s)") for n in range(4))
        spread = qT[:, :, :].rearrange("p h s -> p (h s)")[:, NQ * S - (C1 - 1) * P:]
        k_flat = k_stk[:, :, :, :, :].rearrange("p t h a c -> p (t h a c)")
        q_stk1 = k_flat[:, 0:T * NH1 * PAD1].rearrange("p (t h c) -> p t h c", t=T, h=NH1)
        k_stk1 = k_flat[:, T * NH1 * PAD1:].rearrange("p (t h c) -> p t h c", t=T, h=NH1)
        t_flat = probT[:, :, :, :].rearrange("p n k s -> p (n k s)")
        silu = t_flat[:, 0:512].rearrange("p (k s) -> p k s", k=2)
        gated = t_flat[:, 512:1536].rearrange("p (n j s) -> p n j s", n=2, j=2)

        lora_a = probT[0:RANK].rearrange("p c k s -> p (c k s)")[:, 0:3 * D + NQ * HD]
        lora_b = k_flat[0:RANK, 0:NQKV0 + D]
        stage_q = q_stk[:, :, :, :].rearrange("p t h d -> p (t h d)")
        stage_h = hT[:, :, :].rearrange("p c s -> p (c s)")
        stage_v = v0[:, :, :, :].rearrange("p t h d -> p (t h d)")
        stage_p = prob[:, :, :, :].rearrange("p c t s -> p (c t s)")

        bank = [ctx.enter_context(nc.psum_tensor(f"bank{i}", [P, 512], F32)) for i in range(8)]

        w_loaded = ctx.enter_context(nc.semaphore("w_loaded"))
        wqkv0_loaded = ctx.enter_context(nc.semaphore("wqkv0_loaded"))
        stage_loaded = [ctx.enter_context(nc.semaphore(f"stage_loaded{n}")) for n in range(6)]
        high_made = ctx.enter_context(nc.semaphore("high_made"))
        lora_loaded = ctx.enter_context(nc.semaphore("lora_loaded"))
        zeroed = ctx.enter_context(nc.semaphore("zeroed"))
        lora_ready = ctx.enter_context(nc.semaphore("lora_ready"))
        setup_dve = ctx.enter_context(nc.semaphore("setup_dve"))
        y_stored = ctx.enter_context(nc.semaphore("y_stored"))
        spread_loaded = ctx.enter_context(nc.semaphore("spread_loaded"))

        sems = []

        def signal(name):
            sems.append(ctx.enter_context(nc.semaphore(name)))
            return sems[-1]

        x_loaded = signal("x_loaded")
        x_taken = signal("x_taken")
        y_free = signal("y_free")
        y_ready = signal("y_ready")
        dve_own = signal("dve_own")
        pool_own = signal("pool_own")
        normed = [signal(f"normed{s}") for s in range(4)]
        guessed = [signal(f"guessed{s}") for s in range(4)]
        refined = [signal(f"refined{s}") for s in range(4)]
        xT_psum = [signal(f"xT_psum{s}") for s in range(4)]
        xT_ready = [signal(f"xT_ready{s}") for s in range(4)]
        qkv0_psum = signal("qkv0_psum")
        rotating = signal("rotating")
        rotated_half = signal("rotated_half")
        rotated = signal("rotated")
        v0_ready = signal("v0_ready")
        high_ready = signal("high_ready")
        stacked0 = signal("stacked0")
        qkv1_psum = signal("qkv1_psum")
        qkv1_ready = signal("qkv1_ready")
        stacked1 = signal("stacked1")
        turned = signal("turned")
        turned_out = signal("turned_out")
        turned1 = signal("turned1")
        turned1_out = signal("turned1_out")
        head_turned = signal("head_turned")
        head_turned_out = signal("head_turned_out")
        scores_psum = signal("scores_psum")
        max_ready = signal("max_ready")
        exp_ready = signal("exp_ready")
        rsum_ready = signal("rsum_ready")
        prob_ready = signal("prob_ready")
        probT_psum = signal("probT_psum")
        probT_ready = signal("probT_ready")
        heads_done = signal("heads_done")
        aT0_ready = signal("aT0_ready")
        aT1_ready = signal("aT1_ready")
        attn0_psum = signal("attn0_psum")
        attn1_psum = signal("attn1_psum")
        handed = signal("handed")
        logits0_psum = signal("logits0_psum")
        logits1_psum = signal("logits1_psum")
        route_in0 = signal("route_in0")
        route_exp = signal("route_exp")
        route_in1 = signal("route_in1")
        route_exp1 = signal("route_exp1")
        cw0_ready = signal("cw0_ready")
        cw1_ready = signal("cw1_ready")
        cwT0_psum = signal("cwT0_psum")
        cwT1_psum = signal("cwT1_psum")
        cwT0_ready = signal("cwT0_ready")
        cwT1_ready = signal("cwT1_ready")
        hid0_psum = signal("hid0_psum")
        hid0_ready = signal("hid0_ready")
        exp_out = signal("exp_out")
        biases0_psum = signal("biases0_psum")
        exp_added = signal("exp_added")
        up1_psum = signal("up1_psum")
        spread_psum = signal("spread_psum")
        silu_ready = signal("silu_ready")
        gated_ready = signal("gated_ready")
        hid1_ready = signal("hid1_ready")
        down1_done = signal("down1_done")

        loads = [(dst[:], a[name]) for dst, name in (
            (wroute0, "wroute0"), (wgate1, "wgate1"), (b1_0, "b1_0"), (b13, "b13"), (wo1, "wo1"),
            (rope, "rope"), (ident, "ident"), (iota, "iota"), (w2_0, "w2_0"), (w2_1, "w2_1"))]
        n_loads = len(loads) + 5
        n13, fit = C1 * P, 8 * S
        splits = [(w1_0h[:, :], w1_0l[:, :], a["w1_0"], stage_q[:, 0:C0 * P]),
                  (w13_h[:, 0, 0:fit], w13_l[:, 0, 0:fit], a["w13"][0][:, 0:fit], stage_h),
                  (w13_h[:, 0, fit:], w13_l[:, 0, fit:], a["w13"][0][:, fit:], stage_p[:, NQKV0:NQKV0 + n13 - fit]),
                  (wqkv1_h[:, :], wqkv1_l[:, :], a["wqkv1"], stage_p[:, NQKV0 + n13 - fit:NQKV0 + n13 - fit + 3 * D]),
                  (w13_h[:, 1, fit:], w13_l[:, 1, fit:], a["w13"][1][:, fit:], stage_v[:, 0:n13 - fit]),
                  (w13_h[:, 1, 0:fit], w13_l[:, 1, 0:fit], a["w13"][1][:, 0:fit], k_flat)]

        with nc.Block(no_gpsimd_drain=True) as block:
            @block.sync
            def _(sp):
                sp.dma_start(stage_p[:, 0:NQKV0], a["wqkv0"]).then_inc(wqkv0_loaded, 16)
                for n, (_, _, src, raw) in enumerate(splits):
                    if n == len(splits) - 1:
                        sp.wait_ge(lora_ready, 4)
                    sp.dma_start(raw, src).then_inc(stage_loaded[n], 16)

            @block.scalar
            def _(act):
                act.dma_start(lora_a, a["lora_a"]).then_inc(lora_loaded, 16)
                act.dma_start(lora_b, a["lora_b"]).then_inc(lora_loaded, 16)
                for dst, src in loads:
                    act.dma_start(dst, src).then_inc(w_loaded, 16)
                act.dma_start(x_in[:, :, :], a["x"][0]).then_inc(w_loaded, 16)
                act.dma_start(bias[:, :], a["bias"].partition_broadcast(P)).then_inc(w_loaded, 16)
                act.dma_start(wo0[:, :, :], a["wo0"]).then_inc(w_loaded, 16)
                act.wait_ge(zeroed, 5)
                act.dma_start(b2_0[0:E0, :], a["b2_0"]).then_inc(w_loaded, 16)
                act.dma_start(b2_1[0:2 * E1 + 1, :], a["b2_1"]).then_inc(w_loaded, 16)
                for n, (high, _, _, raw) in enumerate(splits):
                    act.wait_ge(stage_loaded[n], 16)
                    act.activation(high, raw, ACT.Copy).then_inc(high_made, 1)
                act.wait_ge(w_loaded, 16 * n_loads)

            @block.gpsimd
            def _(pool):
                pool.memset(b2_0[:, :], 0.0).then_inc(zeroed, 1)
                pool.memset(b2_1[:, :], 0.0).then_inc(zeroed, 1)
                pool.memset(cw0[:, :, :], 0.0).then_inc(zeroed, 1)
                pool.memset(cw1[:, :, :], 0.0).then_inc(zeroed, 1)
                pool.memset(qkv1[:, :, 3 * D:], 0.0).then_inc(zeroed, 1)

            @block.tensor
            def _(pe):
                pe.wait_ge(lora_loaded, 32)
                for j in range(3):
                    c = 512 * j
                    if j < 2:
                        mm = pe.matmul(bank[j][:, :], lora_a[:, 0:D], lora_b[:, c:c + 512], start=True, stop=True)
                    else:
                        pe.matmul(bank[2][:, 0:256], lora_a[:, D:2 * D], lora_b[:, c:c + 256], start=True, stop=True)
                        mm = pe.matmul(bank[2][:, 256:512], lora_a[:, 2 * D:3 * D], lora_b[:, c + 256:c + 512],
                                       start=True, stop=True)
                    mm.then_inc(lora_ready, 1)
                for j in range(NQ // 2):
                    c = 3 * D + j * P
                    mm = pe.matmul(bank[3 + j // 4][:, (j % 4) * D:(j % 4 + 1) * D], lora_a[:, c:c + P],
                                   lora_b[:, NQKV0:NQKV0 + D], start=True, stop=True)
                mm.then_inc(lora_ready, 1)

            @block.vector
            def _(dve):
                own = Chain(dve, setup_dve)
                dve.wait_ge(wqkv0_loaded, 16)
                wq = stage_p[:, 0:NQKV0]
                for j in range(3):
                    dve.wait_ge(lora_ready, j + 1)
                    c = slice(512 * j, 512 * (j + 1))
                    own.link(dve.scalar_tensor_tensor(out=wq[:, c], in0=bank[j][:, :], scalar=LORA_SCALE,
                                                      in1=wq[:, c], op0=ALU.mult, op1=ALU.add))
                own.link(dve.tensor_copy(wqkv0_h[:, :], wq))
                own.link(dve.tensor_tensor(wqkv0_l[:, :], wq, wqkv0_h[:, :].bitcast(F32), ALU.subtract))
                for n, (high, low, _, raw) in enumerate(splits):
                    dve.wait_ge(high_made, n + 1)
                    own.link(dve.tensor_tensor(low, raw, high.bitcast(F32), ALU.subtract))
                dve.wait_ge(lora_ready, 4)
                dve.wait_ge(w_loaded, 16 * n_loads)
                for j in range(2):
                    w = wo0[:, 4 * j:4 * j + 4, :].rearrange("p c d -> p (c d)")
                    own.link(dve.scalar_tensor_tensor(out=w, in0=bank[3 + j][:, :], scalar=LORA_SCALE,
                                                      in1=w, op0=ALU.mult, op1=ALU.add))
                dve.wait_ge(zeroed, 5)
                own.link(dve.memset(cw1[:, :, 2 * E1:2 * E1 + 1], 1.0))
        nc.sync.sem_inc(y_stored, 16)

        def one_turn(x_on, y_on, q_on, x_next=None, y_of=None):

            heads = [(0, h) for h in range(NQ) if x_on] + [(1, h) for h in range(NH1) if y_on]
            first1 = NQ if x_on else 0

            def s_bank(h):
                return bank[(0, 1, 7)[h % 3]]

            with nc.Block(no_gpsimd_drain=True) as block:
                @block.sync
                def _(sp):
                    if y_on:
                        sp.wait_ge(y_stored, y_of * 16 + 16)
                        sp.sem_inc(y_free, 1)
                    if x_on:
                        sp.wait_ge(x_taken, 1)
                        sp.dma_start(x_in[:, :, :], a["x"][bass.ds(sp.snap(x_next), 1)].rearrange("a p t d -> p (a t) d"))\
                            .then_inc(x_loaded, 16)
                    if y_on:
                        sp.wait_ge(y_ready, 1)
                        sp.dma_start(out[bass.ds(sp.snap(y_of), 1)].rearrange("a p t d -> p (a t) d"), xres_y[:, :, :])\
                            .then_inc(y_stored, 16)
                    if x_on:
                        sp.wait_ge(x_loaded, 16)

                @block.tensor
                def _(pe):
                    def turn_xn(s, dst):
                        for t in range(T):
                            pe.wait_ge(normed[s], t + 1)
                            tr = pe.transpose(dst[:, t * P:(t + 1) * P], xn[:, t, :], ident[:, :])
                        tr.then_inc(xT_psum[s], 1)

                    def three(dst, lh, ll, rh, rl):
                        pe.matmul(dst, lh, rl, start=True, stop=False)
                        pe.matmul(dst, ll, rh, start=False, stop=False)
                        return pe.matmul(dst, lh, rh, start=False, stop=True)

                    def fill(blocks):
                        for j, block_in in enumerate(blocks):
                            tr = pe.transpose(bank[6][:, j * P:(j + 1) * P], block_in, ident[:, :])
                        return tr

                    def fill_q0(n):
                        if n >= 1:
                            pe.wait_ge(turned_out, n)
                        fill([q_stk[:, t, 2 * n + 2 + j, :] for j in range(2) for t in range(T)]).then_inc(turned, 1)

                    def fill_1(n):
                        stk, g = (k_stk1, q_stk1)[n % 2], n // 2 * 2
                        if n == 0:
                            pe.wait_ge(stacked1, T)
                            if x_on:
                                pe.wait_ge(turned_out, len(FILLS0))
                        else:
                            pe.wait_ge(turned1_out, n)
                        fill([stk[:, t, 4 * (g + j):4 * (g + j) + 4, :].rearrange("p h c -> p (h c)")
                              for j in range(2) for t in range(T)]).then_inc(turned1, 1)

                    def scores0(h, dst):
                        if h >= 2:
                            pe.wait_ge(turned_out, h // 2)
                        kv = h // (NQ // NKV)
                        for t in range(T):
                            q = qT[:, h, t * P:(t + 1) * P]
                            pe.matmul(dst[:, t * S:(t + 1) * S], q, kT[:, kv, 1, :], start=True, stop=False)
                            mm = pe.matmul(dst[:, t * S:(t + 1) * S], q, kT[:, kv, 0, :], start=False, stop=True)
                        return mm

                    def outputs0(h, slot):
                        dst = bank[4 + h // 2 % 2][HD * (h % 2):HD * (h % 2 + 1), 0:S]
                        if h % 2 == 0 and h >= 4:
                            pe.wait_ge(aT0_ready, h // 2 - 1)
                        for k in range(2):
                            mm = pe.matmul(dst, v0[:, k, h // (NQ // NKV), :], probT[:, slot, k, :],
                                           start=(k == 0), stop=(k == 1))
                        return mm

                    def project0(t, pairs):
                        if t == 0:
                            pe.wait_ge(turned_out, len(FILLS0))
                            if y_on:
                                pe.wait_ge(turned1_out, 4)
                            pe.wait_ge(aT0_ready, pairs[-1] + 1)
                        for j in pairs:
                            mm = pe.matmul(bank[6][:, t * D:(t + 1) * D], aT[:, j, t * P:(t + 1) * P],
                                           wo0[:, j, :], start=(j == 0 and t == 0), stop=(j == NQ // 2 - 1),
                                           skip_group_check=True)
                        if t == T - 1 and pairs[-1] == NQ // 2 - 1:
                            mm.then_inc(attn0_psum, 1)

                    def scores1(h, dst):
                        pe.wait_ge(turned1_out, 2 * (h // 8) + 2)
                        rows = slice(PAD1 * (h % 4), PAD1 * (h % 4 + 1))
                        for t in range(T):
                            mm = pe.matmul(dst[:, t * S:(t + 1) * S], qT[rows, h // 4, t * P:(t + 1) * P],
                                           kT[rows, h // 8, h // 4 % 2, :], start=True, stop=True)
                        return mm

                    def outputs1(h, slot):
                        g, j = h // 4, h % 4
                        dst = bank[4 + g % 2][PAD1 * j:PAD1 * (j + 1), 0:S]
                        if j == 0 and g < 2 and x_on:
                            pe.wait_ge(aT0_ready, NQ // 2 - 1 + g)
                        if j == 0 and g >= 2:
                            pe.wait_ge(aT1_ready, g - 1)
                        for k in range(2):
                            mm = pe.matmul(dst, qkv1[:, k, 2 * D + HD1 * h:2 * D + HD1 * h + PAD1], probT[:, slot, k, :],
                                           start=(k == 0), stop=(k == 1), tile_position=(0, PAD1 * j))
                        return mm

                    def router0(i):
                        if i in (3, 4):
                            project0(i - 3, range(0, 4))
                        if i in (5, 6):
                            for t in range(T):
                                project0(t, range(2 * i - 6, 2 * i - 4))
                        if i == 11:
                            turn_xn(1, bank[6])
                        if i == 14:
                            pe.wait_ge(xT_ready[1], 1)
                            for t in range(T):
                                mm = pe.matmul(bank[6][:, 12 * t:12 * t + 12], xT[:, t * P:(t + 1) * P],
                                               wroute0[:, :], start=True, stop=True)
                            mm.then_inc(logits0_psum, 1)

                    def up0(n):
                        if n == 0:
                            pe.wait_ge(xT_ready[1], 1)
                        if n < 2 and y_on:
                            pe.wait_ge(exp_ready, 2 * (len(heads) - 1 + n))
                        if 2 <= n < 4 and y_on:
                            pe.wait_ge(probT_ready, len(heads) - 3 + n)
                        if n >= 4:
                            pe.wait_ge(hid0_ready, 2 * (n - 3))
                        for c in range(2):
                            w = slice((2 * n + c) * P, (2 * n + c + 1) * P)
                            mm = three(bank[n % 4][:, c * S:(c + 1) * S], w1_0h[:, w], w1_0l[:, w],
                                       xT_h[:, 0, :], xT_l[:, 0, :])
                        mm.then_inc(hid0_psum, 1)

                    if y_on and not x_on:
                        for n in range(4):
                            fill_1(n)
                    for i in range(len(heads) + 6 if heads else 0):
                        if i < len(heads):
                            layer, h = heads[i]
                            if i >= 3:
                                pe.wait_ge(exp_ready, 2 * (i - 2))
                            (scores0, scores1)[layer](h, s_bank(i)).then_inc(scores_psum, 1)
                        if 4 <= i < len(heads) + 4:
                            n = i - 4
                            pe.wait_ge(prob_ready, 2 * (n + 1))
                            if n >= 2:
                                pe.wait_ge(probT_ready, n - 1)
                            for t in range(T):
                                for k in range(2):
                                    c = k * S + t * P
                                    tr = pe.transpose(bank[2 + n % 2][:, c:c + P],
                                                      prob[:, n % 4, t, k * P:(k + 1) * P], ident[:, :])
                            tr.then_inc(probT_psum, 1)
                        if i >= 6:
                            layer, h = heads[i - 6]
                            pe.wait_ge(probT_ready, i - 5)
                            (outputs0, outputs1)[layer](h, (i - 6) % 3).then_inc(heads_done, 1)
                        if x_on and i in FILLS0:
                            fill_q0(FILLS0.index(i))
                        if x_on and y_on and i in FILLS1:
                            fill_1(FILLS1.index(i))
                        if x_on and y_on and i >= NQ:
                            router0(i - NQ)
                        if x_on and y_on and i > len(heads) + 2:
                            for n in [0, 1] if i == len(heads) + 3 else [i - len(heads) - 2]:
                                up0(n)
                    if x_on and not y_on:
                        for i in range(NH1):
                            router0(i)

                    def project1():
                        pe.wait_ge(aT1_ready, G1)
                        if x_on:
                            pe.wait_ge(route_in0, 1)
                        for t in range(T):
                            for g in range(G1):
                                mm = pe.matmul(bank[6][:, t * D:(t + 1) * D], aT[:, G1 + g, t * P:(t + 1) * P],
                                               wo1[:, g, :], start=(g == 0), stop=(g == G1 - 1))
                        mm.then_inc(attn1_psum, 1)

                    def router1(e):
                        if e == 2:
                            turn_xn(3, bank[6])
                        if e == 3:
                            pe.wait_ge(xT_ready[3], 1)
                            for t in range(T):
                                mm = pe.matmul(bank[7][:, E1 * t:E1 * (t + 1)], xT[:, t * P:(t + 1) * P],
                                               wgate1[:, :], start=True, stop=True)
                            mm.then_inc(logits1_psum, 1)

                    def down0(e):
                        pe.wait_ge(hid0_ready, 4 * (e + 1))
                        if e >= 2:
                            pe.wait_ge(exp_added, T * (e - 1))
                        for t in range(T):
                            for c in range(4):
                                mm = pe.matmul(bank[4 + e % 2][:, t * D:(t + 1) * D],
                                               hT[:, (e % 2) * 4 + c, t * P:(t + 1) * P], w2_0[:, 4 * e + c, :],
                                               start=(c == 0), stop=(c == 3))
                        mm.then_inc(exp_out, 1)

                    def turn_cw(cw, ready, psum):
                        pe.wait_ge(ready, 1)
                        for t in range(T):
                            tr = pe.transpose(bank[7][:, t * P:(t + 1) * P], cw[:, t, :], ident[:, :])
                        tr.then_inc(psum, 1)

                    if x_on:
                        for e in range(E0):
                            for f in range(2):
                                if 2 * e + f >= 4 or not y_on:
                                    up0(2 * e + f)
                            if e == 0 and y_on:
                                project1()
                            if e >= 1:
                                down0(e - 1)
                            if y_on:
                                router1(e)
                            if e == 4 and q_on:
                                turn_xn(0, bank[6])
                            if e == 5:
                                if y_on:
                                    pe.wait_ge(route_in1, 1)
                                turn_cw(cw0, cw0_ready, cwT0_psum)
                        down0(E0 - 1)
                        if q_on:
                            pe.wait_ge(xT_ready[0], 1)
                        pe.wait_ge(cwT0_ready, 1)
                        for t in range(T):
                            mm = pe.matmul(bank[6][:, t * D:(t + 1) * D], cwT[:, t * P:(t + 1) * P].bitcast(F32),
                                           b2_0[:, :], start=True, stop=True)
                        mm.then_inc(biases0_psum, 1)
                    else:
                        if y_on:
                            project1()
                            router1(2)
                            router1(3)
                        if q_on:
                            turn_xn(0, bank[6])

                    def chunks(n):
                        return [C1 - 1] if n == 0 else [2 * n - 2, 2 * n - 1]

                    def up1(n):
                        if n >= 2:
                            pe.wait_ge(gated_ready, 2 * (n - 2) + 1)
                        for which in range(2):
                            for j, c in enumerate(chunks(n)):
                                w = slice(c * P, (c + 1) * P)
                                mm = three(bank[2 * which + n % 2][:, j * S:(j + 1) * S], w13_h[:, which, w],
                                           w13_l[:, which, w], xT_h[:, 1, :], xT_l[:, 1, :])
                        mm.then_inc(up1_psum, 1)

                    def spread1(n):
                        if n >= 2:
                            pe.wait_ge(hid1_ready, n)
                        for j, c in enumerate(chunks(n)):
                            mm = pe.matmul(bank[4][:, j * S:(j + 1) * S], spread[:, c * P:(c + 1) * P], cwT[:, :],
                                           start=True, stop=True)
                        mm.then_inc(spread_psum, 1)

                    def down1(n):
                        pe.wait_ge(hid1_ready, n + 1)
                        for j, c in enumerate(chunks(n)):
                            for t in range(T):
                                mm = pe.matmul(bank[6][:, t * D:(t + 1) * D],
                                               hT[:, 2 * (n % 4) + j, t * P:(t + 1) * P], w2_1[:, c, :],
                                               start=(n == 0 and t == 0), stop=False, skip_group_check=True)
                        mm.then_inc(down1_done, 1)

                    def beside1(n):
                        if q_on and n < 6:
                            if n == 0:
                                pe.wait_ge(xT_ready[0], 1)
                                if x_on:
                                    pe.wait_ge(exp_added, T * E0)
                            else:
                                pe.wait_ge(rotating, 2 * n)
                                pe.wait_ge(v0_ready, min(n, T))
                            t, j = QKV_ORDER[n]
                            tok, c = slice(t * P, (t + 1) * P), slice(512 * j, 512 * (j + 1))
                            three(bank[5][:, :], xT_h[:, 2, tok], xT_l[:, 2, tok], wqkv0_h[:, c], wqkv0_l[:, c])\
                                .then_inc(qkv0_psum, 1)
                        if x_on and n == 3:
                            turn_xn(2, bank[7])
                        if x_on and n in (4, 5):
                            t = n - 4
                            if t == 0:
                                pe.wait_ge(xT_ready[2], 1)
                            else:
                                pe.wait_ge(qkv1_ready, 1)
                            tok = slice(t * P, (t + 1) * P)
                            three(bank[7][:, 0:3 * D], xT_h[:, 0, tok], xT_l[:, 0, tok], wqkv1_h[:, :],
                                  wqkv1_l[:, :]).then_inc(qkv1_psum, 1)

                    def fill_next(m):
                        if m == 0:
                            pe.wait_ge(stacked0, 2)
                            if x_on:
                                pe.wait_ge(qkv1_ready, 2)
                        else:
                            pe.wait_ge(head_turned_out, m)
                        if m == NKV:
                            pe.wait_ge(stacked0, 4)
                        blocks = [k_stk[:, t, m, part, :] for part in range(2) for t in range(T)] if m < NKV\
                            else [q_stk[:, t, j, :] for j in range(2) for t in range(T)]
                        for j, block_in in enumerate(blocks):
                            tr = pe.transpose(bank[7][:, j * P:(j + 1) * P], block_in, ident[:, :])
                        tr.then_inc(head_turned, 1)

                    if y_on:
                        up1(0)
                        up1(1)
                        beside1(0)
                        turn_cw(cw1, cw1_ready, cwT1_psum)
                        down1(0)
                        pe.wait_ge(cwT1_ready, 1)
                        pe.wait_ge(spread_loaded, y_of * 16 + 16)
                        spread1(1)
                        beside1(1)
                        for n in range(2, 9):
                            up1(n)
                            if q_on and n >= 6:
                                fill_next(2 * n - 12)
                            down1(n - 1)
                            spread1(n)
                            beside1(n)
                            if q_on and n in (6, 7):
                                fill_next(2 * n - 11)
                        down1(8)
                        for t in range(T):
                            mm = pe.matmul(bank[6][:, t * D:(t + 1) * D], cwT[:, t * P:(t + 1) * P].bitcast(F32),
                                           b2_1[:, :], start=False, stop=(t == T - 1), skip_group_check=True)
                        mm.then_inc(down1_done, 1)
                    else:
                        for n in range(9):
                            beside1(n)
                        if q_on:
                            for m in range(NKV + 1):
                                fill_next(m)

                @block.scalar
                def _(act):
                    def exps(h):
                        act.wait_ge(max_ready, h + 1)
                        if h >= 4:
                            act.wait_ge(probT_psum, h - 3)
                        if h >= 4:
                            act.wait_ge(rsum_ready, h - 3)
                        for t in range(T):
                            act.activation(prob[:, h % 4, t, :], s_bank(h)[:, t * S:(t + 1) * S], ACT.Exp,
                                           bias=nmax[:, h % 4, t:t + 1],
                                           accum_out=psums[:, h % 4, t:t + 1]).then_inc(exp_ready, 1)

                    def copy_probT(h):
                        act.wait_ge(probT_psum, h + 1)
                        if h >= 3:
                            act.wait_ge(heads_done, h - 2)
                        act.activation(probT[:, h % 3, :, :].rearrange("p k s -> p (k s)"), bank[2 + h % 2][:, :],
                                       ACT.Copy).then_inc(probT_ready, 1)

                    def copy_turned(n, dst):
                        act.wait_ge(turned, n + 1)
                        act.activation(dst.rearrange("p a s -> p (a s)"), bank[6][:, :], ACT.Copy)\
                            .then_inc(turned_out, 1)

                    def route_exp0(n):
                        act.wait_ge(route_in0, n + 1)
                        z = gate_z[:, :, 0:(NLANG, E0)[n]]
                        act.activation(z, z, ACT.Exp).then_inc(route_exp, 1)

                    for i in range(len(heads) + 7 if heads else 0):
                        if x_on and i - 1 in FILLS0:
                            n = FILLS0.index(i - 1)
                            copy_turned(n, qT[:, 2 * n + 2:2 * n + 4, :])
                        if i < len(heads):
                            exps(i)
                        if 4 <= i < len(heads) + 4:
                            copy_probT(i - 4)
                        if x_on and 7 <= i < NQ + 7 and i % 2 == 1:
                            j = (i - 7) // 2
                            act.wait_ge(heads_done, 2 * j + 2)
                            act.activation(aT[:, j, :], bank[4 + j % 2][:, 0:S], ACT.Copy).then_inc(aT0_ready, 1)
                        i1 = i - first1
                        if y_on and i1 >= 10 and i1 % 4 == 2:
                            g = i1 // 4 - 2
                            act.wait_ge(heads_done, first1 + 4 * g + 4)
                            if x_on and g == 0:
                                act.wait_ge(attn0_psum, 1)
                            act.activation(aT[:, G1 + g, :], bank[4 + g % 2][:, 0:S], ACT.Copy,
                                           scale=float(1 / np.sqrt(D))).then_inc(aT1_ready, 1)
                        if x_on and y_on and i1 in (16, 19):
                            route_exp0((i1 - 16) // 3)
                    if x_on and not y_on:
                        route_exp0(0)
                        route_exp0(1)

                    if x_on:
                        for c in range(C0):
                            act.wait_ge(hid0_psum, c // 2 + 1)
                            if c == 4 and y_on:
                                act.wait_ge(attn1_psum, 1)
                            if c >= 8:
                                act.wait_ge(exp_out, c // 4 - 1)
                            act.activation(hT[:, c % 8, :], bank[c // 2 % 4][:, (c % 2) * S:(c % 2 + 1) * S],
                                           ACT.Gelu, bias=b1_0[:, c:c + 1]).then_inc(hid0_ready, 1)
                            if c == 17 and y_on:
                                act.wait_ge(route_in1, 1)
                                act.activation(gate_z[:, :, :], gate_z[:, :, :], ACT.Exp).then_inc(route_exp1, 1)
                    elif y_on:
                        act.wait_ge(route_in1, 1)
                        act.activation(gate_z[:, :, :], gate_z[:, :, :], ACT.Exp).then_inc(route_exp1, 1)

                    def silus(n):
                        for k in ([0] if n == 0 else [2 * n - 1, 2 * n]):
                            j = 0 if k == 0 else (k + 1) % 2
                            c = C1 - 1 if k == 0 else k - 1
                            act.wait_ge(up1_psum, n + 1)
                            if k >= 2:
                                act.wait_ge(gated_ready, k - 1)
                            act.activation(silu[:, k % 2, :], bank[n % 2][:, j * S:(j + 1) * S], ACT.Silu,
                                           bias=b13[:, 0, c:c + 1]).then_inc(silu_ready, 1)

                    def high_parts(m):
                        t, j = QKV_ORDER[m]
                        if j == 2:
                            act.wait_ge(rotating, 2 * (m + 1))
                            act.activation(v0[:, t, :, :].rearrange("p h d -> p (h d)"), bank[5][:, 256:512],
                                           ACT.Copy).then_inc(v0_ready, 1)
                        act.wait_ge(rotated, m + 1)
                        if j == 2:
                            for half in range(2):
                                hi = act.activation(k_stk[:, t, :, 0, half * HD:(half + 1) * HD].bitcast(F32R),
                                                    ro[m % 2][:, 0:NKV * HD].rearrange("p (h d) -> p h d", d=HD), ACT.Copy)
                        else:
                            hi = act.activation(q_stk[:, t, 8 * j:8 * j + 8, 0:HD].bitcast(F32R),
                                                ro[m % 2][:, :].rearrange("p (h d) -> p h d", d=HD), ACT.Copy)
                        hi.then_inc(high_ready, 1)

                    def copy_first_turned(m):
                        act.wait_ge(head_turned, m + 1)
                        dst = kT[:, m, :, :] if m < NKV else qT[:, 0:2, :]
                        act.activation(dst.rearrange("p a s -> p (a s)"), bank[7][:, :], ACT.Copy)\
                            .then_inc(head_turned_out, 1)

                    for n in range(9):
                        if q_on and n in (7, 8):
                            copy_first_turned(2 * n - 13)
                        if y_on:
                            silus(n)
                        if q_on and n >= 6:
                            copy_first_turned(2 * n - 12)
                        if q_on and 1 <= n < 7:
                            high_parts(n - 1)

                @block.gpsimd
                def _(pool):
                    link = Chain(pool, pool_own).link

                    def refine(s):
                        pool.wait_ge(guessed[s], 1)
                        for n in range(3):
                            link(pool.tensor_tensor(newton[:, :], rstd[:, :], rstd[:, :], ALU.mult))
                            link(pool.tensor_tensor(newton[:, :], newton[:, :], var[:, :], ALU.mult))
                            link(pool.tensor_scalar(newton[:, :], newton[:, :], -0.5, 1.5, ALU.mult, ALU.add))
                            ins = pool.tensor_tensor(rstd[:, :], rstd[:, :], newton[:, :], ALU.mult)
                            if n < 2:
                                link(ins)
                        ins.then_inc(refined[s], 1)

                    if y_on:
                        pool.wait_ge(y_free, 1)
                        pool.tensor_tensor(xres_y[:, :, :], xres_x[:, :, :],
                                           bias[:, B_OUT1:B_OUT1 + D].unsqueeze(1).to_broadcast([P, T, D]),
                                           ALU.add).then_inc(handed, 1)
                    if x_on:
                        refine(1)
                    if y_on:
                        pool.wait_ge(attn1_psum, 1)
                        pool.dma_start(spread, a["spread"]).then_inc(spread_loaded, 16)
                        refine(3)
                    if q_on:
                        refine(0)
                    def rotate(m):
                        n = (8 if QKV_ORDER[m][1] < 2 else NKV) * HD
                        xc = ra[:, 0:n].rearrange("p (h a d) -> p h a d", a=2, d=HALF)
                        xs = rb[:, 0:n].rearrange("p (h a d) -> p h a d", a=2, d=HALF)
                        o = ro[m % 2][:, 0:n].rearrange("p (h a d) -> p h a d", a=2, d=HALF)
                        pool.wait_ge(rotating, 2 * (m + 1))
                        if m >= 2:
                            pool.wait_ge(stacked0, m - 1)
                        pool.tensor_tensor(o[:, :, 0, :], xc[:, :, 0, :], xs[:, :, 1, :], ALU.subtract)\
                            .then_inc(rotated_half, 1)
                        pool.tensor_tensor(o[:, :, 1, :], xs[:, :, 0, :], xc[:, :, 1, :], ALU.add)\
                            .then_inc(rotated, 1)

                    def rests(m):
                        t, j = QKV_ORDER[m]
                        n = (8 if j < 2 else NKV) * HD
                        pool.wait_ge(rotated_half, m + 1)
                        pool.wait_ge(rotated, m + 1)
                        pool.wait_ge(high_ready, m + 1)
                        o = ro[m % 2][:, 0:n].rearrange("p (h d) -> p h d", d=HD)
                        if j < 2:
                            stk = q_stk[:, t, 8 * j:8 * j + 8, :]
                            lo = pool.tensor_tensor(stk[:, :, HD:2 * HD].bitcast(F32R), o, stk[:, :, 0:HD],
                                                    ALU.subtract)
                        else:
                            for half in range(2):
                                lo = pool.tensor_tensor(k_stk[:, t, :, 1, half * HD:(half + 1) * HD].bitcast(F32R),
                                                        o, k_stk[:, t, :, 0, 0:HD], ALU.subtract)
                        lo.then_inc(stacked0, 1)

                    if q_on:
                        rotate(0)
                        if x_on:
                            refine(2)
                        for m in range(len(QKV_ORDER)):
                            if m + 1 < len(QKV_ORDER):
                                rotate(m + 1)
                            rests(m)

                @block.vector
                def _(dve):
                    own = Chain(dve, dve_own)
                    link, step = own.link, own.step

                    def advance(side):
                        next(side, None)

                    def finish(*sides):
                        while sides:
                            sides = [side for side in sides if next(side, "over") != "over"]

                    def norm_stats(s, src):
                        step(dve.bn_stats(stats[:, 0, :], src[:, 0, :]))
                        step(dve.bn_stats(stats[:, 1, :], src[:, 1, :]))
                        done = own.n
                        yield
                        own.settle(done)
                        step(dve.bn_aggr(mv[:, 0, :], stats[:, 0, :]))
                        step(dve.bn_aggr(mv[:, 1, :], stats[:, 1, :]))
                        done = own.n
                        yield
                        own.settle(done)
                        step(dve.tensor_scalar(var[:, :], mv[:, :, 1], LN_EPS, None, ALU.add))
                        done = own.n
                        yield
                        own.settle(done)
                        bits = rstd[:, :].bitcast(I32)
                        step(dve.tensor_scalar(bits, var[:, :].bitcast(I32), 1, None, ALU.logical_shift_right))
                        done = own.n
                        yield
                        own.settle(done)
                        dve.tensor_scalar(bits, bits, -1.0, float(0x5F3759DF), ALU.mult, ALU.add).then_inc(guessed[s], 1)

                    def norm_apply(s, src):
                        dve.wait_ge(refined[s], 1)
                        for t in range(T):
                            dve.tensor_scalar(xn[:, t, :], src[:, t, :], mv[:, t, 0:1], rstd[:, t:t + 1],
                                              ALU.subtract, ALU.mult).then_inc(normed[s], 1)

                    def split_xT(s, src, slot, whole):
                        dve.wait_ge(xT_psum[s], 1)
                        if whole:
                            step(dve.tensor_copy(xT[:, :], src[:, 0:S]))
                            done = own.n
                            yield
                            own.settle(done)
                            src = xT
                        step(dve.tensor_copy(xT_h[:, slot, :], src[:, 0:S]))
                        done = own.n
                        yield
                        own.settle(done)
                        dve.tensor_tensor(xT_l[:, slot, :], src[:, 0:S], xT_h[:, slot, :].bitcast(F32), ALU.subtract)\
                            .then_inc(xT_ready[s], 1)

                    def softmax_steps(i, side):
                        if i >= 2:
                            h = i - 2
                            dve.wait_ge(exp_ready, 2 * (h + 1))
                            dve.reciprocal(rsums[:, h % 4, :], psums[:, h % 4, :]).then_inc(rsum_ready, 1)
                        if i < len(heads):
                            dve.wait_ge(scores_psum, i + 1)
                            if i >= 4:
                                dve.wait_ge(exp_ready, 2 * (i - 3))
                            dve.tensor_reduce(nmax[:, i % 4, :], s_bank(i)[:, :].rearrange("p (t s) -> p t s", t=T),
                                              AX_X, ALU.max, negate=True).then_inc(max_ready, 1)
                            advance(side)
                        if i >= 2:
                            h = i - 2
                            dve.wait_ge(rsum_ready, h + 1)
                            for t in range(T):
                                dve.tensor_scalar(prob[:, h % 4, t, :], prob[:, h % 4, t, :],
                                                  rsums[:, h % 4, t:t + 1], None, ALU.mult)\
                                    .then_inc(prob_ready, 1)
                                advance(side)
                        finish(side)

                    def stack1(i):
                        if i >= 8:
                            return
                        part = [slice(HD1 * n, HD1 * (n + 1)) for n in range(4)]
                        t, n = i // 4, i % 4
                        q = qkv1[:, t, 0:D].rearrange("p (h e) -> p h e", e=HD1)
                        k = qkv1[:, t, D:2 * D].rearrange("p (h e) -> p h e", e=HD1)
                        qs, ks = q_stk1[:, t, :, :], k_stk1[:, t, :, :]
                        if n == 0:
                            for p in (0, 2):
                                step(dve.tensor_copy(qs[:, :, part[p]].bitcast(F32R), q))
                            done = own.n
                            yield
                            own.settle(done)
                        if n == 1:
                            for p in (1, 3):
                                step(dve.tensor_tensor(qs[:, :, part[p]].bitcast(F32R), q, qs[:, :, part[0]],
                                                       ALU.subtract))
                            done = own.n
                            yield
                            own.settle(done)
                        if n == 2:
                            for p in (0, 1):
                                step(dve.tensor_copy(ks[:, :, part[p]].bitcast(F32R), k))
                            done = own.n
                            yield
                            own.settle(done)
                        if n == 3:
                            for p in (2, 3):
                                step(dve.tensor_tensor(ks[:, :, part[p]].bitcast(F32R), k, ks[:, :, part[0]],
                                                       ALU.subtract))
                            done = own.n
                            yield
                            own.settle(done)
                            dve.sem_inc(stacked1, 1)

                    def g(k, n):
                        return gate_t[:, k, :, 0:n]

                    def sc(k):
                        return gate_s[:, k, :]

                    def wide(v, n):
                        return v.unsqueeze(2).to_broadcast([P, T, n])

                    def softmax_in(z, n):
                        step(dve.tensor_reduce(sc(0), z, AX_X, ALU.max))
                        done = own.n
                        yield
                        own.settle(done)
                        step(dve.tensor_tensor(gate_z[:, :, 0:n], z, wide(sc(0), n), ALU.subtract))
                        done = own.n
                        yield
                        own.settle(done)

                    def softmax_out(n, dst):
                        step(dve.tensor_reduce(sc(1), gate_z[:, :, 0:n], AX_X, ALU.add))
                        done = own.n
                        yield
                        own.settle(done)
                        step(dve.reciprocal(sc(2), sc(1)))
                        done = own.n
                        yield
                        own.settle(done)
                        step(dve.tensor_tensor(dst, gate_z[:, :, 0:n], wide(sc(2), n), ALU.mult))
                        done = own.n
                        yield
                        own.settle(done)

                    def top(slot, vals, n):
                        step(dve.max(out=top8[:, slot, 0, :], in_=vals[:, 0, :]))
                        step(dve.max(out=top8[:, slot, 1, :], in_=vals[:, 1, :]))
                        done = own.n
                        yield
                        own.settle(done)
                        step(dve.max_index(topi[:, slot, 0, :], top8[:, slot, 0, :], vals[:, 0, :]))
                        step(dve.max_index(topi[:, slot, 1, :], top8[:, slot, 1, :], vals[:, 1, :]))
                        done = own.n
                        yield
                        own.settle(done)
                        step(dve.tensor_copy(topf[:, slot, :, :], topi[:, slot, :, :]))
                        done = own.n
                        yield
                        own.settle(done)

                    def hit(dst, slot, k, n):
                        return dve.tensor_tensor(dst, iota[:, 0:n].unsqueeze(1).to_broadcast([P, T, n]),
                                                 wide(topf[:, slot, :, k], n), ALU.is_equal)

                    def route0(i):
                        if i == 7:
                            dve.wait_ge(attn0_psum, 1)
                            if y_on:
                                dve.wait_ge(handed, 1)
                            step(dve.tensor_tensor(xres_x[:, :, :], bank[6][:, 0:S].rearrange("p (t d) -> p t d", t=T),
                                                   x_in[:, :, :], ALU.add))
                            done = own.n
                            yield
                            own.settle(done)
                            dve.sem_inc(x_taken, 1)
                            yield from norm_stats(1, xres_x)
                        if i == 10:
                            norm_apply(1, xres_x)
                        if i == 12:
                            yield from split_xT(1, bank[6], 0, True)
                        if i == 15:
                            dve.wait_ge(logits0_psum, 1)
                            nr = NLANG + E0
                            b_route = bias[:, B_ROUTE0:B_ROUTE0 + nr].unsqueeze(1).to_broadcast([P, T, nr])
                            step(dve.tensor_tensor(g(0, nr), bank[6][:, 0:T * nr].rearrange("p (t n) -> p t n", t=T),
                                                   b_route, ALU.add))
                            done = own.n
                            yield
                            own.settle(done)
                            yield from softmax_in(g(0, NLANG), NLANG)
                            dve.sem_inc(route_in0, 1)
                        if i == 18:
                            dve.wait_ge(route_exp, 1)
                            yield from softmax_out(NLANG, g(1, NLANG))
                            step(dve.tensor_tensor(g(2, NLANG - 1), g(1, NLANG - 1), gate_t[:, 1, :, 1:NLANG], ALU.add))
                            done = own.n
                            yield
                            own.settle(done)
                            step(dve.tensor_copy(gate_t[:, 2, :, NLANG - 1:NLANG], gate_t[:, 1, :, NLANG - 1:NLANG]))
                            done = own.n
                            yield
                            own.settle(done)
                            for r in range(E0 // NLANG):
                                step(dve.scalar_tensor_tensor(out=gate_t[:, 3, :, r * NLANG:(r + 1) * NLANG],
                                                              in0=g(2, NLANG), scalar=0.1,
                                                              in1=gate_t[:, 0, :, (r + 1) * NLANG:(r + 2) * NLANG],
                                                              op0=ALU.mult, op1=ALU.add))
                            done = own.n
                            yield
                            own.settle(done)
                            yield from softmax_in(g(3, E0), E0)
                            dve.sem_inc(route_in0, 1)
                        if i == 19:
                            dve.wait_ge(route_exp, 2)
                            yield from softmax_out(E0, g(4, E0))
                            yield from top(0, g(4, E0), E0)
                            step(dve.tensor_tensor(sc(3), top8[:, 0, :, 0], top8[:, 0, :, 1], ALU.add))
                            done = own.n
                            yield
                            own.settle(done)
                            step(dve.reciprocal(sc(4), sc(3)))
                            step(hit(g(5, E0), 0, 0, E0))
                            step(hit(g(6, E0), 0, 1, E0))
                            done = own.n
                            yield
                            own.settle(done)
                            step(dve.tensor_tensor(sc(5), top8[:, 0, :, 0], sc(4), ALU.mult))
                            step(dve.tensor_tensor(sc(6), top8[:, 0, :, 1], sc(4), ALU.mult))
                            done = own.n
                            yield
                            own.settle(done)
                            step(dve.tensor_tensor(g(7, E0), g(5, E0), wide(sc(5), E0), ALU.mult))
                            step(dve.tensor_tensor(g(8, E0), g(6, E0), wide(sc(6), E0), ALU.mult))
                            done = own.n
                            yield
                            own.settle(done)
                            step(dve.tensor_tensor(cw0[:, :, 0:E0], g(7, E0), g(8, E0), ALU.add))
                            done = own.n
                            yield
                            own.settle(done)
                            dve.sem_inc(cw0_ready, 1)

                    def norm_next(e):
                        if e == 2:
                            if x_on:
                                dve.wait_ge(x_loaded, 16)
                            yield from norm_stats(0, x_in)
                        if e == 3:
                            norm_apply(0, x_in)
                        if e == 6:
                            yield from split_xT(0, bank[6], 2, False)

                    def copy_turned1(n):
                        dve.wait_ge(turned1, n + 1)
                        if x_on:
                            dve.wait_ge(scores_psum, NQ // 2)
                        dst = qT[:, n - 1:n + 1, :] if n % 2 else kT[:, n // 2, :, :]
                        dve.tensor_copy(dst.rearrange("p a s -> p (a s)"), bank[6][:, :]).then_inc(turned1_out, 1)

                    def beside_heads(i):
                        if x_on and y_on and i - 1 in FILLS1:
                            copy_turned1(FILLS1.index(i - 1))
                            yield
                        if x_on and y_on:
                            yield from stack1(i) if i < NQ else route0(i - NQ)

                    if y_on and not x_on:
                        for i in range(8):
                            finish(stack1(i))
                        for n in range(4):
                            copy_turned1(n)
                    for i in range(len(heads) + 2 if heads else 0):
                        softmax_steps(i, beside_heads(i))
                    if x_on and y_on:
                        finish(beside_heads(NQ + 18))
                        finish(beside_heads(NQ + 19))
                    if x_on and not y_on:
                        for i in range(20):
                            finish(route0(i))

                    def gate1(e):
                        if e == 0:
                            dve.wait_ge(attn1_psum, 1)
                            dve.wait_ge(handed, 1)
                            step(dve.tensor_tensor(xres_y[:, :, :], bank[6][:, 0:S].rearrange("p (t d) -> p t d", t=T),
                                                   xres_y[:, :, :], ALU.add))
                            done = own.n
                            yield
                            own.settle(done)
                            yield from norm_stats(3, xres_y)
                        if e == 1:
                            norm_apply(3, xres_y)
                        if e == 2:
                            yield from split_xT(3, bank[6], 1, True)
                        if e == 3:
                            dve.wait_ge(logits1_psum, 1)
                            step(dve.tensor_tensor(g(0, E1), bank[7][:, 0:T * E1].rearrange("p (t n) -> p t n", t=T),
                                                   bias[:, B_GATE1:B_GATE1 + E1].unsqueeze(1).to_broadcast([P, T, E1]),
                                                   ALU.add))
                            done = own.n
                            yield
                            own.settle(done)
                            yield from softmax_in(g(0, E1), E1)
                            dve.sem_inc(route_in1, 1)
                        if e == 4:
                            dve.wait_ge(route_exp1, 1)
                            yield from softmax_out(E1, g(1, E1))
                            pairs = gate_t[:, 1, :, :].rearrange("p t (g b) -> p t g b", b=2)
                            hi, lo = g(2, 2 * GROUPS), g(3, 2 * GROUPS)
                            step(dve.tensor_tensor(hi, pairs[:, :, :, 0], pairs[:, :, :, 1], ALU.max))
                            step(dve.tensor_tensor(lo, pairs[:, :, :, 0], pairs[:, :, :, 1], ALU.min))
                            done = own.n
                            yield
                            own.settle(done)
                            hi2, lo2 = (v.rearrange("p t (g a) -> p t g a", a=2) for v in (hi, lo))
                            step(dve.tensor_tensor(g(4, GROUPS), hi2[:, :, :, 0], hi2[:, :, :, 1], ALU.max))
                            step(dve.tensor_tensor(g(5, GROUPS), hi2[:, :, :, 0], hi2[:, :, :, 1], ALU.min))
                            step(dve.tensor_tensor(g(6, GROUPS), lo2[:, :, :, 0], lo2[:, :, :, 1], ALU.max))
                            done = own.n
                            yield
                            own.settle(done)
                            step(dve.tensor_tensor(g(7, GROUPS), g(5, GROUPS), g(6, GROUPS), ALU.max))
                            done = own.n
                            yield
                            own.settle(done)
                            step(dve.tensor_tensor(g(8, GROUPS), g(4, GROUPS), g(7, GROUPS), ALU.add))
                            done = own.n
                            yield
                            own.settle(done)
                        if e == 5:
                            yield from top(0, g(8, GROUPS), GROUPS)
                            step(hit(g(2, GROUPS), 0, 0, GROUPS))
                            step(hit(g(3, GROUPS), 0, 1, GROUPS))
                            step(hit(g(4, GROUPS), 0, 2, GROUPS))
                            step(hit(g(5, GROUPS), 0, 3, GROUPS))
                            done = own.n
                            yield
                            own.settle(done)
                            step(dve.tensor_tensor(g(6, GROUPS), g(2, GROUPS), g(3, GROUPS), ALU.add))
                            step(dve.tensor_tensor(g(7, GROUPS), g(4, GROUPS), g(5, GROUPS), ALU.add))
                            done = own.n
                            yield
                            own.settle(done)
                            step(dve.tensor_tensor(g(9, GROUPS), g(6, GROUPS), g(7, GROUPS), ALU.add))
                            done = own.n
                            yield
                            own.settle(done)
                            step(dve.tensor_scalar(g(10, GROUPS), g(9, GROUPS), -1.0, None, ALU.add))
                            done = own.n
                            yield
                            own.settle(done)
                        if e == 5:
                            by_group = gate_t[:, 1, :, :].rearrange("p t (g e) -> p t g e", g=GROUPS)
                            kept = gate_t[:, 11, :, :].rearrange("p t (g e) -> p t g e", g=GROUPS)
                            for src, op in ((9, ALU.mult), (10, ALU.add)):
                                for t in range(T):
                                    ins = dve.tensor_tensor(
                                        kept[:, t], (by_group if op == ALU.mult else kept)[:, t],
                                        gate_t[:, src, t, 0:GROUPS].unsqueeze(2).to_broadcast([P, GROUPS, 4]), op)
                                    step(ins)
                                done = own.n
                                yield
                                own.settle(done)
                            yield from top(1, g(11, E1), E1)
                        if e == 6:
                            for k in range(TOPK1 - 1):
                                step(hit(g(2 + k, E1), 1, k, E1))
                            step(hit(g(1 + TOPK1, E1), 1, TOPK1 - 1, E1))
                            done = own.n
                            yield
                            own.settle(done)
                            for k in range(TOPK1):
                                ins = dve.tensor_tensor(g(6 + k, E1), g(2 + k, E1), wide(top8[:, 1, :, k], E1), ALU.mult)
                                step(ins)
                            done = own.n
                            yield
                            own.settle(done)
                            step(dve.tensor_tensor(g(10, E1), g(6, E1), g(7, E1), ALU.add))
                            step(dve.tensor_tensor(g(11, E1), g(8, E1), g(9, E1), ALU.add))
                            done = own.n
                            yield
                            own.settle(done)
                            whole = g(2, E1)
                            step(dve.tensor_tensor(whole, g(10, E1), g(11, E1), ALU.add))
                            done = own.n
                            yield
                            own.settle(done)
                            step(dve.tensor_copy(cw1[:, :, 0:E1].bitcast(F32R), whole))
                            done = own.n
                            yield
                            own.settle(done)
                            step(dve.tensor_tensor(cw1[:, :, E1:2 * E1].bitcast(F32R), whole, cw1[:, :, 0:E1],
                                                   ALU.subtract))
                            done = own.n
                            yield
                            own.settle(done)
                            dve.sem_inc(cw1_ready, 1)

                    def add_expert(e):
                        dve.wait_ge(exp_out, e + 1)
                        for t in range(T):
                            dve.scalar_tensor_tensor(
                                out=xres_x[:, t, :], in0=bank[4 + e % 2][:, t * D:(t + 1) * D],
                                scalar=cw0[:, t, e:e + 1], in1=xres_x[:, t, :], op0=ALU.mult, op1=ALU.add)\
                                .then_inc(exp_added, 1)
                        dve.wait_ge(exp_added, T * (e + 1))

                    for e in range(E0):
                        finish(*([gate1(e)] if y_on else []), *([norm_next(e)] if q_on else []))
                        if x_on:
                            if e == 5:
                                dve.wait_ge(cwT0_psum, 1)
                                dve.tensor_copy(cwT[:, :], bank[7][:, 0:S]).then_inc(cwT0_ready, 1)
                            add_expert(e)
                    if x_on:
                        dve.wait_ge(biases0_psum, 1)
                        link(dve.tensor_tensor(xres_x[:, :, :], bank[6][:, 0:S].rearrange("p (t d) -> p t d", t=T),
                                               xres_x[:, :, :], ALU.add))

                    def gate_chunk(k):
                        n, j = (0, 0) if k == 0 else ((k + 1) // 2, (k + 1) % 2)
                        c = C1 - 1 if k == 0 else k - 1
                        dve.wait_ge(silu_ready, k + 1)
                        dst = hT[:, 0, :] if k == 0 else gated[:, n % 2, j, :]
                        dve.scalar_tensor_tensor(out=dst, in0=bank[2 + n % 2][:, j * S:(j + 1) * S],
                                                 scalar=b13[:, 1, c:c + 1], in1=silu[:, k % 2, :],
                                                 op0=ALU.add, op1=ALU.mult).then_inc(gated_ready, 1)
                        if k == 0:
                            dve.wait_ge(gated_ready, 1)
                            dve.sem_inc(hid1_ready, 1)

                    def weigh(n):
                        dve.wait_ge(spread_psum, n)
                        dve.wait_ge(gated_ready, 2 * n + 1)
                        if n >= 4:
                            dve.wait_ge(down1_done, n - 3)
                        dve.tensor_tensor(hT[:, 2 * (n % 4):2 * (n % 4) + 2, :], gated[:, n % 2, :, :],
                                          bank[4][:, :].rearrange("p (c s) -> p c s", c=2), ALU.mult)\
                            .then_inc(hid1_ready, 1)

                    def beside1(n):
                        if x_on and n == 2:
                            norm_apply(2, xres_x)
                        if q_on and n < 6:
                            m = n
                            t, j = QKV_ORDER[m]
                            many = 8 if j < 2 else NKV
                            w = many * HD
                            dve.wait_ge(qkv0_psum, m + 1)
                            if m >= 1:
                                dve.wait_ge(rotated, m)
                                dve.wait_ge(rotated_half, m)
                            for k, dst in ((0, ra), (1, rb)):
                                table = rope[:, t, k + (0 if j < 2 else 2), :].unsqueeze(1)\
                                    .to_broadcast([P, 2 * many, HALF])
                                ins = dve.tensor_tensor(dst[:, 0:w].rearrange("p (h d) -> p h d", d=HALF),
                                                        bank[5][:, 0:w].rearrange("p (h d) -> p h d", d=HALF),
                                                        table, ALU.mult)
                                ins.then_inc(rotating, 1)
                        if x_on and n == 3:
                            yield from split_xT(2, bank[7], 0, False)
                        if x_on and n in (4, 5):
                            t = n - 4
                            dve.wait_ge(qkv1_psum, t + 1)
                            dve.tensor_tensor(qkv1[:, t, 0:3 * D], bank[7][:, 0:3 * D], bias[:, B_QKV1:B_QKV1 + 3 * D],
                                              ALU.add).then_inc(qkv1_ready, 1)

                    if y_on:
                        gate_chunk(0)
                    finish(beside1(0))
                    if y_on:
                        dve.wait_ge(cwT1_psum, 1)
                        dve.tensor_copy(cwT[:, :], bank[7][:, 0:S]).then_inc(cwT1_ready, 1)
                    for n in range(1, 9):
                        side = norm_stats(2, xres_x) if x_on and n == 1 else iter(())
                        if y_on:
                            gate_chunk(2 * n - 1)
                            advance(side)
                            gate_chunk(2 * n)
                            advance(side)
                            weigh(n)
                        finish(side)
                        finish(beside1(n))
                    if y_on:
                        dve.wait_ge(down1_done, 10)
                        dve.tensor_tensor(xres_y[:, :, :], bank[6][:, 0:S].rearrange("p (t d) -> p t d", t=T),
                                          xres_y[:, :, :], ALU.add).then_inc(y_ready, 1)

            nc.all_engine_barrier(sems_to_clear=range(sems[0].num, sems[-1].num + 1))

        one_turn(x_on=False, y_on=False, q_on=True)
        one_turn(x_on=True, y_on=False, q_on=True, x_next=1)
        with nc.Fori(1, NB) as b:
            one_turn(x_on=True, y_on=True, q_on=True, x_next=(b + 1) % NB, y_of=b - 1)
        one_turn(x_on=False, y_on=True, q_on=False, y_of=NB - 1)
        nc.sync.wait_ge(y_stored, 16 * (NB + 1))


def laid_out(i):
    f = np.float32

    def halves(w):
        h = w.shape[0] // HD
        return w.reshape(h, HALF, 2, -1).transpose(0, 2, 1, 3).reshape(w.shape)

    def cat(*xs):
        return np.ascontiguousarray(np.concatenate(xs, axis=-1))

    inv_freq = (f(1.0) / f(THETA) ** (np.arange(0, HD, 2, dtype=f) / f(HD))).astype(f)
    ang = np.arange(S, dtype=f)[:, None] * inv_freq[None, :]
    cos, sin = np.cos(ang).astype(f), np.sin(ang).astype(f)
    scale = f(1 / np.sqrt(HD))
    rope = np.stack([cos * scale, sin * scale, cos, sin], axis=1).reshape(T, P, 4, HALF)
    spread = np.zeros((P, C1 - 1, 2, H1), f)
    for e in range(E1):
        spread[e, e // 2, e % 2] = 1
        spread[E1 + e, e // 2, e % 2] = 1
    wo1 = np.zeros((G1, 4, PAD1, D), f)
    wo1[:, :, 0:HD1] = i["L1_attn_W_out"].reshape(G1, 4, HD1, D)

    def columns(w, sw):
        return cat(w.transpose(1, 0, 2).reshape(D, E1 * H1), sw)

    def chunked(w, sw):
        return np.concatenate([w.reshape(-1, D), sw]).reshape(-1, P, D).transpose(1, 0, 2)

    def per_chunk(b, sb):
        return np.concatenate([b.reshape(-1), sb]).reshape(-1, P).T

    return {
        "x": i["L0_attn_x"].reshape(NB, T, P, D).transpose(0, 2, 1, 3),
        "wqkv0": cat(halves(i["L0_attn_Wq"]).T, halves(i["L0_attn_Wk"]).T, i["L0_attn_Wv"].T),
        "lora_a": cat(i["L0_attn_qA"], i["L0_attn_kA"], i["L0_attn_vA"], i["L0_attn_oA"]),
        "lora_b": cat(halves(i["L0_attn_qB"]).T, halves(i["L0_attn_kB"]).T, i["L0_attn_vB"].T,
                      i["L0_attn_oB"].T),
        "wo0": i["L0_attn_Wo"].T.reshape(NQ // 2, P, D).transpose(1, 0, 2),
        "wroute0": cat(i["L0_ffn_lang_w"].T, i["L0_ffn_router_w"].T),
        "w1_0": i["L0_ffn_w1"].transpose(1, 0, 2).reshape(D, E0 * H0),
        "b1_0": i["L0_ffn_b1"].reshape(C0, P).T,
        "w2_0": i["L0_ffn_w2"].reshape(C0, P, D).transpose(1, 0, 2),
        "b2_0": i["L0_ffn_b2"],
        "wqkv1": i["L1_attn_W_qkv"],
        "wo1": wo1.reshape(G1, P, D).transpose(1, 0, 2),
        "wgate1": i["L1_ffn_gw"],
        "w13": np.stack([columns(i["L1_ffn_w1"], i["L1_ffn_sw1"]), columns(i["L1_ffn_w3"], i["L1_ffn_sw3"])]),
        "b13": np.stack([per_chunk(i["L1_ffn_b1"], i["L1_ffn_sb1"]),
                         per_chunk(i["L1_ffn_b3"], i["L1_ffn_sb3"])], axis=1),
        "w2_1": chunked(i["L1_ffn_w2"], i["L1_ffn_sw2"]),
        "b2_1": np.concatenate([i["L1_ffn_b2"], i["L1_ffn_b2"], i["L1_ffn_sb2"][None]]),
        "bias": cat(i["L0_ffn_lang_b"], i["L0_ffn_router_b"], i["L1_ffn_gb"], i["L1_attn_b_qkv"],
                    i["L1_attn_b_out"]),
        "rope": rope.transpose(1, 0, 2, 3),
        "ident": np.eye(P, dtype=f),
        "iota": np.tile(np.arange(E1, dtype=f), (P, 1)),
        "spread": spread.reshape(P, -1),
    }


def kernel(**inputs):
    import concourse.bacc as bacc
    from concourse.bass_utils import run_bass_kernel_spmd

    nc = bacc.Bacc("TRN2", target_bir_lowering=False, num_devices=1)
    arrays, aps = {}, {}
    for name, v in laid_out({k: np.asarray(v) for k, v in inputs.items()}).items():
        arrays[f"in_{name}"] = np.ascontiguousarray(v)
        aps[name] = nc.dram_tensor(f"in_{name}", v.shape, F32, kind="ExternalInput").ap()
    out = nc.dram_tensor("out", (NB, P, T, D), F32, kind="ExternalOutput").ap()
    transformer_layers(nc, aps, out)
    r = run_bass_kernel_spmd(nc, [arrays], core_ids=[0])
    return r.results[0]["out"].transpose(0, 2, 1, 3).reshape(NB, S, D)
```
